# Optimizing a Trainium2 kernel written in Bass

```python
import numpy as np
import jax
import jax.numpy as jnp

def _softmax(x, axis=-1):
    return jax.nn.softmax(x, axis=axis)

def _gelu(x):
    return jax.nn.gelu(x, approximate=True)

def _silu(x):
    return jax.nn.silu(x)

def _sigmoid(x):
    return jax.nn.sigmoid(x)

def _layernorm(x, axis=-1, eps=1e-05):
    m = jnp.mean(x, axis=axis, keepdims=True)
    v = jnp.var(x, axis=axis, keepdims=True)
    return (x - m) / jnp.sqrt(v + eps)

def _scatter_add(tgt, idx, src, axis=0):
    return tgt.at[idx].add(src)

def _segment_sum(src, seg, n):
    return jax.ops.segment_sum(src, seg, n)
kernel_name = 'mk_perceiver_d2_seqx_r8_67aae6'

def setup_inputs(seed: int=0):
    np.random.seed(seed)
    _w = jnp.asarray

    def _rec_inputs():
        import jax
        import jax.numpy as jnp
        _rk = jax.random.key(seed)
        x = -0.0002928 + 1 * jax.random.normal(jax.random.fold_in(_rk, 1), (1, 64, 128), jnp.float32)
        _lenS = 64 - jax.random.randint(jax.random.fold_in(_rk, 7), (1,), 0, max(1, 64 // 4) + 1, jnp.int32)
        _lenS2 = 6272 - jax.random.randint(jax.random.fold_in(_rk, 8), (1,), 0, max(1, 6272 // 4) + 1, jnp.int32)
        _ctx_1024P = jax.random.normal(jax.random.fold_in(_rk, 11), (1, 16, 128), jnp.float32)
        _ctx_1024c = jax.random.dirichlet(jax.random.fold_in(_rk, 511), 0.3 * jnp.ones((16,), jnp.float32), (1, 6272))
        _ctx_1024t = jnp.einsum('bsk,bkd->bsd', _ctx_1024c, _ctx_1024P)
        _ctx_1024t = _ctx_1024t * jax.lax.rsqrt(jnp.mean(jnp.square(_ctx_1024t)) + 1e-12) * 0.953939
        ctx_1024 = -1.39393e-06 + 0.999914 * (_ctx_1024t + 0.3 * jax.random.normal(jax.random.fold_in(_rk, 611), (1, 6272, 128), jnp.float32))
        _validS = jnp.arange(64)[None, :] < _lenS[:, None]
        _validS2 = jnp.arange(6272)[None, :] < _lenS2[:, None]
        _causal = jnp.tril(jnp.ones((64, 64), dtype=bool))
        mask_SxS2_ik0 = jnp.where(jnp.broadcast_to(_validS2[0:1, :], (64, 6272)), 0, 1).astype(jnp.int32)
        return (x, ctx_1024, mask_SxS2_ik0)
    x, ctx_1024, mask_SxS2_ik0 = _rec_inputs()

    def _L0_xattn_setup():
        import jax, jax.numpy as jnp
        import numpy as np
        D_M = 128
        H = 16
        D_K = 64
        D_V = 64
        key = jax.random.key(seed)
        ks = jax.random.split(key, 6)
        b, m, n = (2, 256, 256)
        query = jax.random.normal(ks[0], (b, m, D_M), dtype=jnp.float32)
        key_value = jax.random.normal(ks[1], (b, n, D_M), dtype=jnp.float32)
        mask = jnp.tril(jnp.ones((m, n), dtype=jnp.int32))
        s = 1.0 / np.sqrt(D_M)
        W_q = jax.random.normal(ks[2], (D_M, H * D_K), dtype=jnp.float32) * s
        W_k = jax.random.normal(ks[3], (D_M, H * D_K), dtype=jnp.float32) * s
        W_v = jax.random.normal(ks[4], (D_M, H * D_V), dtype=jnp.float32) * s
        W_o = jax.random.normal(ks[5], (H * D_V, D_M), dtype=jnp.float32) * s
        return {'query': query, 'key_value': key_value, 'mask': mask, 'W_q': W_q, 'W_k': W_k, 'W_v': W_v, 'W_o': W_o}
    _L0_xattn_all = _L0_xattn_setup()
    _L0_xattn_in = {k: v for k, v in _L0_xattn_all.items() if k in ('W_q', 'W_k', 'W_v', 'W_o')}
    del _L0_xattn_all

    def _L0_attn_setup():
        import jax, jax.numpy as jnp
        import numpy as np
        import math
        D_MODEL = 128
        N_HEADS = 16
        DH = D_MODEL // N_HEADS
        THETA = 10000.0

        def _rope_tables(S):
            inv_freq = 1.0 / THETA ** (jnp.arange(0, DH, 2, dtype=jnp.float32) / DH)
            ang = jnp.arange(S, dtype=jnp.float32)[:, None] * inv_freq[None, :]
            cos = jnp.concatenate([jnp.cos(ang), jnp.cos(ang)], axis=-1)
            sin = jnp.concatenate([jnp.sin(ang), jnp.sin(ang)], axis=-1)
            return (cos, sin)

        def _apply_rope(x, cos, sin):
            x1, x2 = jnp.split(x, 2, axis=-1)
            rot = jnp.concatenate([-x2, x1], axis=-1)
            c = cos[None, :, None, :]
            s = sin[None, :, None, :]
            return x * c + rot * s
        key = jax.random.key(seed)
        k1, k2, k3 = jax.random.split(key, 3)
        x = jax.random.normal(k1, (4, 256, D_MODEL), dtype=jnp.float32)
        qkv = 0.01 * jax.random.normal(k2, (3 * D_MODEL, D_MODEL), dtype=jnp.float32)
        wo = 0.01 * jax.random.normal(k3, (D_MODEL, D_MODEL), dtype=jnp.float32)
        return {'x': x, 'qkv': qkv, 'wo': wo}
    _L0_attn_all = _L0_attn_setup()
    _L0_attn_in = {k: v for k, v in _L0_attn_all.items() if k in ('qkv', 'wo')}
    del _L0_attn_all

    def _L0_ffn_setup():
        import jax, jax.numpy as jnp
        import numpy as np
        TOP_K = 2
        key = jax.random.key(seed)
        ks = jax.random.split(key, 5)
        B, S, H, I, E = (4, 256, 128, 512, 8)
        scale_hi = (2.0 / (H + I)) ** 0.5
        scale_he = (2.0 / (H + E)) ** 0.5
        return {'x': jax.random.normal(ks[0], (B, S, H), dtype=jnp.float32), 'router_w': jax.random.normal(ks[1], (E, H), dtype=jnp.float32) * scale_he, 'gate_w': jax.random.normal(ks[2], (E, I, H), dtype=jnp.float32) * scale_hi, 'up_w': jax.random.normal(ks[3], (E, I, H), dtype=jnp.float32) * scale_hi, 'down_w': jax.random.normal(ks[4], (E, H, I), dtype=jnp.float32) * scale_hi}
    _L0_ffn_all = _L0_ffn_setup()
    _L0_ffn_in = {k: v for k, v in _L0_ffn_all.items() if k in ('router_w', 'gate_w', 'up_w', 'down_w')}
    del _L0_ffn_all

    def _L1_xattn_setup():
        import jax, jax.numpy as jnp
        import numpy as np
        DIM = 128
        HEADS = 16
        DIM_HEAD = 64
        INNER = HEADS * DIM_HEAD
        SCALE = DIM_HEAD ** (-0.5)
        B, N = (4, 256)

        def _split_heads(t):
            b, n, _ = t.shape
            return t.reshape(b, n, HEADS, DIM_HEAD).transpose(0, 2, 1, 3)

        def _attn_block(q_src, k_src, v_src, Wq, Wk, Wv, Wo, bo):
            q = _split_heads(q_src @ Wq)
            k = _split_heads(k_src @ Wk)
            v = _split_heads(v_src @ Wv)
            dots = jnp.einsum('bhid,bhjd->bhij', q, k) * SCALE
            attn = jax.nn.softmax(dots, axis=-1)
            out = jnp.einsum('bhij,bhjd->bhid', attn, v)
            out = out.transpose(0, 2, 1, 3).reshape(q_src.shape[0], q_src.shape[1], INNER)
            return out @ Wo + bo
        key = jax.random.key(seed)
        ks = jax.random.split(key, 7)
        s = DIM ** (-0.5)
        return {'x1': jax.random.normal(ks[0], (B, N, DIM), jnp.float32), 'x2': jax.random.normal(ks[1], (B, N, DIM), jnp.float32), 'Wq': jax.random.normal(ks[2], (DIM, INNER), jnp.float32) * s, 'Wk': jax.random.normal(ks[3], (DIM, INNER), jnp.float32) * s, 'Wv': jax.random.normal(ks[4], (DIM, INNER), jnp.float32) * s, 'Wo': jax.random.normal(ks[5], (INNER, DIM), jnp.float32) * INNER ** (-0.5), 'bo': jnp.zeros((DIM,), jnp.float32)}
    _L1_xattn_all = _L1_xattn_setup()
    _L1_xattn_in = {k: v for k, v in _L1_xattn_all.items() if k in ('Wq', 'Wk', 'Wv', 'Wo', 'bo')}
    del _L1_xattn_all

    def _L1_attn_setup():
        import jax, jax.numpy as jnp
        import numpy as np
        B, L, D, H = (2, 512, 128, 4)
        DK = D // H
        DV = D // H
        CONV_K = 4
        FIR_S, FIR_L = (5, 64)
        GATE_HID = D * 2 // 2
        CHUNK = 32
        FLOOR_EPS = 0.08
        GATE_BIAS = np.array([-0.5, -0.5, 1.0, 3.0], np.float32)
        GATE_LOGIT_INIT = float(np.log(np.expm1(0.7)))
        CONV_RES_INIT = float(np.log(0.1 / 0.9))

        def _l2norm(x):
            return x / jnp.sqrt(jnp.sum(x * x, -1, keepdims=True) + 1e-12)

        def _causal_dwconv(x, w):
            k = w.shape[-1]
            xp = jnp.pad(x, ((0, 0), (k - 1, 0), (0, 0))).transpose(0, 2, 1)
            y = jax.lax.conv_general_dilated(xp, w[:, None, :], (1,), 'VALID', feature_group_count=w.shape[0], dimension_numbers=('NCH', 'OIH', 'NCH'))
            return y.transpose(0, 2, 1)

        def _delta_chunkwise(q, k, v, beta):
            b, h, Lq, dk = q.shape
            dv = v.shape[-1]
            c = CHUNK
            n = Lq // c
            q = _l2norm(q)
            k = _l2norm(k)
            v = v * beta[..., None]
            kb = k * beta[..., None]
            rs = lambda t: t.reshape(b, h, n, c, t.shape[-1])
            q, k, v, kb = map(rs, (q, k, v, kb))
            tri_lo_strict = jnp.tril(jnp.ones((c, c), bool), -1)
            tri_lo = jnp.tril(jnp.ones((c, c), bool), 0)
            A = jnp.where(tri_lo_strict, kb @ jnp.swapaxes(k, -1, -2), 0.0)
            eye = jnp.eye(c, dtype=q.dtype)
            inv = jax.scipy.linalg.solve_triangular(eye + A, jnp.broadcast_to(eye, A.shape), lower=True, unit_diagonal=True)
            u = inv @ v
            w = inv @ kb

            def step(S, xs):
                qi, ki, ui, wi = xs
                attn = jnp.where(tri_lo, qi @ jnp.swapaxes(ki, -1, -2), 0.0)
                u_i = ui - wi @ S
                o = qi @ S + attn @ u_i
                return (S + jnp.swapaxes(ki, -1, -2) @ u_i, o)
            mv = lambda t: jnp.moveaxis(t, 2, 0)
            S0 = jnp.zeros((b, h, dk, dv), q.dtype)
            _, out = jax.lax.scan(step, S0, (mv(q), mv(k), mv(u), mv(w)))
            return jnp.moveaxis(out, 0, 2).reshape(b, h, Lq, dv)

        def _stats(x):
            mean = jnp.mean(x, -1, keepdims=True)
            var = jnp.var(x, -1, keepdims=True)
            am = jnp.mean(jnp.abs(x), -1, keepdims=True)
            l2 = jnp.linalg.norm(x, axis=-1, keepdims=True)
            return jnp.concatenate([mean, var, am, l2], -1)
        key = jax.random.key(seed)
        ks = jax.random.split(key, 20)
        rn = lambda i, shape, sc: jax.random.normal(ks[i], shape, jnp.float32) * sc
        fir_s = jnp.zeros((H, DV, FIR_S), jnp.float32).at[..., 0].set(1.0) + rn(8, (H, DV, FIR_S), 0.02)
        fir_l = jnp.zeros((H, DV, FIR_L), jnp.float32).at[..., 0].set(1.0) + rn(9, (H, DV, FIR_L), 0.02)
        return {'hidden_states': rn(0, (B, L, D), 1.0), 'Wq': rn(1, (D, D), 0.02), 'Wk': rn(2, (D, D), 0.02), 'Wv': rn(3, (D, D), 0.02), 'Wb': rn(4, (D, H), 0.02), 'conv_w_q': rn(5, (D, CONV_K), 0.3), 'conv_w_k': rn(6, (D, CONV_K), 0.3), 'conv_w_v': rn(7, (D, CONV_K), 0.3), 'fir_short_w': fir_s, 'fir_long_w': fir_l, 'mlp_w1': rn(10, (D + 16, GATE_HID), 0.02), 'mlp_b1': jnp.zeros((GATE_HID,), jnp.float32), 'mlp_w2': rn(11, (GATE_HID, 4), 0.02), 'mlp_b2': jnp.asarray(GATE_BIAS), 'logit_temp': jnp.full((1,), GATE_LOGIT_INIT, jnp.float32), 'conv_res_logit': jnp.full((H,), CONV_RES_INIT, jnp.float32), 'rms_w': jnp.ones((DV,), jnp.float32), 'Wo': rn(12, (D, D), 0.02)}
    _L1_attn_all = _L1_attn_setup()
    _L1_attn_in = {k: v for k, v in _L1_attn_all.items() if k in ('Wq', 'Wk', 'Wv', 'Wb', 'conv_w_q', 'conv_w_k', 'conv_w_v', 'fir_short_w', 'fir_long_w', 'mlp_w1', 'mlp_b1', 'mlp_w2', 'mlp_b2', 'logit_temp', 'conv_res_logit', 'rms_w', 'Wo')}
    del _L1_attn_all

    def _L1_ffn_setup():
        import jax, jax.numpy as jnp
        import numpy as np

        def _ste(w, w_q):
            return w + jax.lax.stop_gradient(w_q - w)

        def quantize_w8_per(w, axis):
            amax = jnp.clip(jnp.max(jnp.abs(w), axis=axis, keepdims=True), 1e-08, None)
            scale = 127.0 / amax
            w_q = jnp.clip(jnp.round(w * scale), -128.0, 127.0) / scale
            return _ste(w, w_q)

        def quantize_a16(x):
            amax = jnp.clip(jnp.max(jnp.abs(x)), 1e-08, None)
            scale = 32767.0 / amax
            x_q = jnp.clip(jnp.round(x * scale), -32768.0, 32767.0) / scale
            return _ste(x, x_q)
        key = jax.random.key(seed)
        k1, k2, k3 = jax.random.split(key, 3)
        d_model, d_ff = (128, 512)
        x = jax.random.normal(k1, (4, 256, d_model), dtype=jnp.float32)
        W_in = jax.random.normal(k2, (d_model, d_ff), dtype=jnp.float32) / np.sqrt(d_model)
        b_in = jnp.zeros((d_ff,), dtype=jnp.float32)
        W_out = jax.random.normal(k3, (d_ff, d_model), dtype=jnp.float32) / np.sqrt(d_ff)
        b_out = jnp.zeros((d_model,), dtype=jnp.float32)
        return {'x': x, 'W_in': W_in, 'b_in': b_in, 'W_out': W_out, 'b_out': b_out}
    _L1_ffn_all = _L1_ffn_setup()
    _L1_ffn_in = {k: v for k, v in _L1_ffn_all.items() if k in ('W_in', 'b_in', 'W_out', 'b_out')}
    del _L1_ffn_all
    return {'x': x, 'ctx_1024': ctx_1024, 'mask_SxS2_ik0': mask_SxS2_ik0, 'L0_xattn_W_q': _L0_xattn_in['W_q'], 'L0_xattn_W_k': _L0_xattn_in['W_k'], 'L0_xattn_W_v': _L0_xattn_in['W_v'], 'L0_xattn_W_o': _L0_xattn_in['W_o'], 'L0_attn_qkv': _L0_attn_in['qkv'], 'L0_attn_wo': _L0_attn_in['wo'], 'L0_ffn_router_w': _L0_ffn_in['router_w'], 'L0_ffn_gate_w': _L0_ffn_in['gate_w'], 'L0_ffn_up_w': _L0_ffn_in['up_w'], 'L0_ffn_down_w': _L0_ffn_in['down_w'], 'L1_xattn_Wq': _L1_xattn_in['Wq'], 'L1_xattn_Wk': _L1_xattn_in['Wk'], 'L1_xattn_Wv': _L1_xattn_in['Wv'], 'L1_xattn_Wo': _L1_xattn_in['Wo'], 'L1_xattn_bo': _L1_xattn_in['bo'], 'L1_attn_Wq': _L1_attn_in['Wq'], 'L1_attn_Wk': _L1_attn_in['Wk'], 'L1_attn_Wv': _L1_attn_in['Wv'], 'L1_attn_Wb': _L1_attn_in['Wb'], 'L1_attn_conv_w_q': _L1_attn_in['conv_w_q'], 'L1_attn_conv_w_k': _L1_attn_in['conv_w_k'], 'L1_attn_conv_w_v': _L1_attn_in['conv_w_v'], 'L1_attn_fir_short_w': _L1_attn_in['fir_short_w'], 'L1_attn_fir_long_w': _L1_attn_in['fir_long_w'], 'L1_attn_mlp_w1': _L1_attn_in['mlp_w1'], 'L1_attn_mlp_b1': _L1_attn_in['mlp_b1'], 'L1_attn_mlp_w2': _L1_attn_in['mlp_w2'], 'L1_attn_mlp_b2': _L1_attn_in['mlp_b2'], 'L1_attn_logit_temp': _L1_attn_in['logit_temp'], 'L1_attn_conv_res_logit': _L1_attn_in['conv_res_logit'], 'L1_attn_rms_w': _L1_attn_in['rms_w'], 'L1_attn_Wo': _L1_attn_in['Wo'], 'L1_ffn_W_in': _L1_ffn_in['W_in'], 'L1_ffn_b_in': _L1_ffn_in['b_in'], 'L1_ffn_W_out': _L1_ffn_in['W_out'], 'L1_ffn_b_out': _L1_ffn_in['b_out']}

def reference(x, ctx_1024, mask_SxS2_ik0, L0_xattn_W_q, L0_xattn_W_k, L0_xattn_W_v, L0_xattn_W_o, L0_attn_qkv, L0_attn_wo, L0_ffn_router_w, L0_ffn_gate_w, L0_ffn_up_w, L0_ffn_down_w, L1_xattn_Wq, L1_xattn_Wk, L1_xattn_Wv, L1_xattn_Wo, L1_xattn_bo, L1_attn_Wq, L1_attn_Wk, L1_attn_Wv, L1_attn_Wb, L1_attn_conv_w_q, L1_attn_conv_w_k, L1_attn_conv_w_v, L1_attn_fir_short_w, L1_attn_fir_long_w, L1_attn_mlp_w1, L1_attn_mlp_b1, L1_attn_mlp_w2, L1_attn_mlp_b2, L1_attn_logit_temp, L1_attn_conv_res_logit, L1_attn_rms_w, L1_attn_Wo, L1_ffn_W_in, L1_ffn_b_in, L1_ffn_W_out, L1_ffn_b_out):
    import jax
    import jax.numpy as jnp

    def _L0_xattn_ref(query, key_value, mask, W_q, W_k, W_v, W_o):
        import jax, jax.numpy as jnp
        import numpy as np
        D_M = 128
        H = 16
        D_K = 64
        D_V = 64
        b, m, _ = query.shape
        n = key_value.shape[1]
        Q = (query @ W_q).reshape(b, m, H, D_K).transpose(0, 2, 1, 3)
        K = (key_value @ W_k).reshape(b, n, H, D_K).transpose(0, 2, 1, 3)
        V = (key_value @ W_v).reshape(b, n, H, D_V).transpose(0, 2, 1, 3)
        scores = jnp.einsum('bhmk,bhnk->bhmn', Q, K)
        scores = jnp.where(mask == 0, jnp.float32(-1e+20), scores)
        attn = jax.nn.softmax(scores / np.sqrt(D_K).astype(np.float32), axis=-1)
        ctx = jnp.einsum('bhmn,bhnv->bhmv', attn, V)
        ctx = ctx.transpose(0, 2, 1, 3).reshape(b, m, H * D_V)
        return ctx @ W_o

    def _L0_attn_ref(x, qkv, wo):
        import jax, jax.numpy as jnp
        import numpy as np
        import math
        D_MODEL = 128
        N_HEADS = 16
        DH = D_MODEL // N_HEADS
        THETA = 10000.0

        def _rope_tables(S):
            inv_freq = 1.0 / THETA ** (jnp.arange(0, DH, 2, dtype=jnp.float32) / DH)
            ang = jnp.arange(S, dtype=jnp.float32)[:, None] * inv_freq[None, :]
            cos = jnp.concatenate([jnp.cos(ang), jnp.cos(ang)], axis=-1)
            sin = jnp.concatenate([jnp.sin(ang), jnp.sin(ang)], axis=-1)
            return (cos, sin)

        def _apply_rope(x, cos, sin):
            x1, x2 = jnp.split(x, 2, axis=-1)
            rot = jnp.concatenate([-x2, x1], axis=-1)
            c = cos[None, :, None, :]
            s = sin[None, :, None, :]
            return x * c + rot * s
        B, S, D = x.shape
        QKV = x @ qkv.T
        Q, K, V = jnp.split(QKV, 3, axis=-1)
        q = Q.reshape(B, S, N_HEADS, DH)
        k = K.reshape(B, S, N_HEADS, DH)
        v = V.reshape(B, S, N_HEADS, DH)
        cos, sin = _rope_tables(S)
        q = _apply_rope(q, cos, sin)
        k = _apply_rope(k, cos, sin)
        q = q.transpose(0, 2, 1, 3)
        k = k.transpose(0, 2, 1, 3)
        v = v.transpose(0, 2, 1, 3)
        scores = jnp.einsum('bhsd,bhtd->bhst', q, k) / math.sqrt(float(DH))
        mask = jnp.tril(jnp.ones((S, S), dtype=scores.dtype))
        scores = scores * mask
        scores = jnp.where(scores == 0.0, -jnp.inf, scores)
        attn = jax.nn.softmax(scores, axis=-1)
        out = jnp.einsum('bhst,bhtd->bhsd', attn, v)
        out = out.transpose(0, 2, 1, 3).reshape(B, S, D)
        return out @ wo.T

    def _L0_ffn_ref(x, router_w, gate_w, up_w, down_w):
        import jax, jax.numpy as jnp
        import numpy as np
        TOP_K = 2
        B, S, H = x.shape
        E = router_w.shape[0]
        xf = x.reshape(-1, H)
        logits = xf @ router_w.T
        probs = jax.nn.softmax(logits, axis=-1)
        topk_p, topk_i = jax.lax.top_k(probs, TOP_K)
        topk_p = topk_p / topk_p.sum(axis=-1, keepdims=True)

        def body(out, inputs):
            e, gw, uw, dw = inputs
            sel = topk_i == e
            mask = sel.any(axis=-1)
            w_tok = (topk_p * sel).sum(axis=-1)
            cnt = mask.sum().astype(xf.dtype)
            mean_w = jnp.where(cnt > 0, w_tok.sum() / jnp.maximum(cnt, 1.0), 0.0)
            h = jax.nn.silu(xf @ gw.T) * (xf @ uw.T)
            eo = h @ dw.T
            out = out + mask[:, None].astype(xf.dtype) * eo * mean_w
            return (out, None)
        out0 = jnp.zeros_like(xf)
        out, _ = jax.lax.scan(body, out0, (jnp.arange(E), gate_w, up_w, down_w))
        return out.reshape(B, S, H)

    def _L1_xattn_ref(x1, x2, Wq, Wk, Wv, Wo, bo):
        import jax, jax.numpy as jnp
        import numpy as np
        DIM = 128
        HEADS = 16
        DIM_HEAD = 64
        INNER = HEADS * DIM_HEAD
        SCALE = DIM_HEAD ** (-0.5)
        B, N = (4, 256)

        def _split_heads(t):
            b, n, _ = t.shape
            return t.reshape(b, n, HEADS, DIM_HEAD).transpose(0, 2, 1, 3)

        def _attn_block(q_src, k_src, v_src, Wq, Wk, Wv, Wo, bo):
            q = _split_heads(q_src @ Wq)
            k = _split_heads(k_src @ Wk)
            v = _split_heads(v_src @ Wv)
            dots = jnp.einsum('bhid,bhjd->bhij', q, k) * SCALE
            attn = jax.nn.softmax(dots, axis=-1)
            out = jnp.einsum('bhij,bhjd->bhid', attn, v)
            out = out.transpose(0, 2, 1, 3).reshape(q_src.shape[0], q_src.shape[1], INNER)
            return out @ Wo + bo
        out = x1 + _attn_block(x1, x2, x2, Wq, Wk, Wv, Wo, bo)
        return _attn_block(out, out, x1, Wq, Wk, Wv, Wo, bo)

    def _L1_attn_ref(hidden_states, Wq, Wk, Wv, Wb, conv_w_q, conv_w_k, conv_w_v, fir_short_w, fir_long_w, mlp_w1, mlp_b1, mlp_w2, mlp_b2, logit_temp, conv_res_logit, rms_w, Wo):
        import jax, jax.numpy as jnp
        import numpy as np
        B, L, D, H = (2, 512, 128, 4)
        DK = D // H
        DV = D // H
        CONV_K = 4
        FIR_S, FIR_L = (5, 64)
        GATE_HID = D * 2 // 2
        CHUNK = 32
        FLOOR_EPS = 0.08
        GATE_BIAS = np.array([-0.5, -0.5, 1.0, 3.0], np.float32)
        GATE_LOGIT_INIT = float(np.log(np.expm1(0.7)))
        CONV_RES_INIT = float(np.log(0.1 / 0.9))

        def _l2norm(x):
            return x / jnp.sqrt(jnp.sum(x * x, -1, keepdims=True) + 1e-12)

        def _causal_dwconv(x, w):
            k = w.shape[-1]
            xp = jnp.pad(x, ((0, 0), (k - 1, 0), (0, 0))).transpose(0, 2, 1)
            y = jax.lax.conv_general_dilated(xp, w[:, None, :], (1,), 'VALID', feature_group_count=w.shape[0], dimension_numbers=('NCH', 'OIH', 'NCH'))
            return y.transpose(0, 2, 1)

        def _delta_chunkwise(q, k, v, beta):
            b, h, Lq, dk = q.shape
            dv = v.shape[-1]
            c = CHUNK
            n = Lq // c
            q = _l2norm(q)
            k = _l2norm(k)
            v = v * beta[..., None]
            kb = k * beta[..., None]
            rs = lambda t: t.reshape(b, h, n, c, t.shape[-1])
            q, k, v, kb = map(rs, (q, k, v, kb))
            tri_lo_strict = jnp.tril(jnp.ones((c, c), bool), -1)
            tri_lo = jnp.tril(jnp.ones((c, c), bool), 0)
            A = jnp.where(tri_lo_strict, kb @ jnp.swapaxes(k, -1, -2), 0.0)
            eye = jnp.eye(c, dtype=q.dtype)
            inv = jax.scipy.linalg.solve_triangular(eye + A, jnp.broadcast_to(eye, A.shape), lower=True, unit_diagonal=True)
            u = inv @ v
            w = inv @ kb

            def step(S, xs):
                qi, ki, ui, wi = xs
                attn = jnp.where(tri_lo, qi @ jnp.swapaxes(ki, -1, -2), 0.0)
                u_i = ui - wi @ S
                o = qi @ S + attn @ u_i
                return (S + jnp.swapaxes(ki, -1, -2) @ u_i, o)
            mv = lambda t: jnp.moveaxis(t, 2, 0)
            S0 = jnp.zeros((b, h, dk, dv), q.dtype)
            _, out = jax.lax.scan(step, S0, (mv(q), mv(k), mv(u), mv(w)))
            return jnp.moveaxis(out, 0, 2).reshape(b, h, Lq, dv)

        def _stats(x):
            mean = jnp.mean(x, -1, keepdims=True)
            var = jnp.var(x, -1, keepdims=True)
            am = jnp.mean(jnp.abs(x), -1, keepdims=True)
            l2 = jnp.linalg.norm(x, axis=-1, keepdims=True)
            return jnp.concatenate([mean, var, am, l2], -1)
        hs = hidden_states
        b, l, _ = hs.shape
        silu = jax.nn.silu
        q = silu(_causal_dwconv(hs @ Wq, conv_w_q))
        k = silu(_causal_dwconv(hs @ Wk, conv_w_k))
        v = silu(_causal_dwconv(hs @ Wv, conv_w_v))
        qh = q.reshape(b, l, H, DK)
        kh = k.reshape(b, l, H, DK)
        vh = v.reshape(b, l, H, DV)
        beta = jax.nn.sigmoid(hs @ Wb)
        tr = lambda t: jnp.transpose(t, (0, 2, 1, 3))
        delta_out = tr(_delta_chunkwise(tr(qh), tr(kh), tr(vh), jnp.transpose(beta, (0, 2, 1))))
        fir = lambda x, w: _causal_dwconv(x.reshape(b, l, H * DV), w.reshape(H * DV, -1)).reshape(b, l, H, DV)
        local_short = fir(vh, fir_short_w)
        local_long = fir(vh, fir_long_w)
        stats = jnp.concatenate([_stats(local_short), _stats(local_long), _stats(delta_out), _stats(vh)], -1)
        hs_exp = jnp.broadcast_to(hs[:, :, None, :], (b, l, H, hs.shape[-1]))
        gate_in = jnp.concatenate([hs_exp, stats], -1)
        hgate = jax.nn.gelu(gate_in @ mlp_w1 + mlp_b1, approximate=False)
        logits = hgate @ mlp_w2 + mlp_b2
        temp = jax.nn.softplus(logit_temp) + 1e-06
        probs = jax.nn.softmax(logits / temp, -1)
        floor = jnp.array([FLOOR_EPS, FLOOR_EPS, 0.0, 0.0], probs.dtype)
        probs = probs * (1.0 - 2.0 * FLOOR_EPS) + floor
        o = probs[..., 0:1] * local_short + probs[..., 1:2] * local_long + probs[..., 2:3] * delta_out + probs[..., 3:4] * vh
        o = o + jax.nn.sigmoid(conv_res_logit)[None, None, :, None] * local_short
        o = o * jax.lax.rsqrt(jnp.mean(o * o, -1, keepdims=True) + 1e-05) * rms_w
        return o.reshape(b, l, H * DV) @ Wo

    def _L1_ffn_ref(x, W_in, b_in, W_out, b_out):
        import jax, jax.numpy as jnp
        import numpy as np

        def _ste(w, w_q):
            return w + jax.lax.stop_gradient(w_q - w)

        def quantize_w8_per(w, axis):
            amax = jnp.clip(jnp.max(jnp.abs(w), axis=axis, keepdims=True), 1e-08, None)
            scale = 127.0 / amax
            w_q = jnp.clip(jnp.round(w * scale), -128.0, 127.0) / scale
            return _ste(w, w_q)

        def quantize_a16(x):
            amax = jnp.clip(jnp.max(jnp.abs(x)), 1e-08, None)
            scale = 32767.0 / amax
            x_q = jnp.clip(jnp.round(x * scale), -32768.0, 32767.0) / scale
            return _ste(x, x_q)
        W_in_sim = quantize_w8_per(W_in, axis=0)
        W_out_sim = quantize_w8_per(W_out, axis=1)
        x_sim = quantize_a16(x)
        hidden = jax.nn.gelu(x_sim @ W_in_sim + b_in, approximate=False)
        hidden_sim = quantize_a16(hidden)
        out = hidden_sim @ W_out_sim + b_out
        return out
    x = x + _L0_xattn_ref(_layernorm(x, axis=-1), ctx_1024, mask_SxS2_ik0, L0_xattn_W_q, L0_xattn_W_k, L0_xattn_W_v, L0_xattn_W_o)
    x = x + _L0_attn_ref(_layernorm(x, axis=-1), L0_attn_qkv, L0_attn_wo)
    x = x + _L0_ffn_ref(_layernorm(x, axis=-1), L0_ffn_router_w, L0_ffn_gate_w, L0_ffn_up_w, L0_ffn_down_w)
    x = x + _L1_xattn_ref(_layernorm(x, axis=-1), ctx_1024, L1_xattn_Wq, L1_xattn_Wk, L1_xattn_Wv, L1_xattn_Wo, L1_xattn_bo)
    x = x + _L1_attn_ref(_layernorm(x, axis=-1), L1_attn_Wq, L1_attn_Wk, L1_attn_Wv, L1_attn_Wb, L1_attn_conv_w_q, L1_attn_conv_w_k, L1_attn_conv_w_v, L1_attn_fir_short_w, L1_attn_fir_long_w, L1_attn_mlp_w1, L1_attn_mlp_b1, L1_attn_mlp_w2, L1_attn_mlp_b2, L1_attn_logit_temp, L1_attn_conv_res_logit, L1_attn_rms_w, L1_attn_Wo)
    x = x + _L1_ffn_ref(_layernorm(x, axis=-1), L1_ffn_W_in, L1_ffn_b_in, L1_ffn_W_out, L1_ffn_b_out)
    return x

_drawn_inputs = setup_inputs


def setup_inputs(seed=0):
    import zlib

    import numpy as np

    out = dict(_drawn_inputs(seed))
    spreads = {'L1_xattn_bo': (0.0, 0.1),
     'L1_attn_mlp_b1': (0.0, 2.0),
     'L1_attn_conv_res_logit': (-2.1972246170043945, 0.6),
     'L1_attn_rms_w': (1.0, 0.6),
     'L1_ffn_b_in': (0.0, 0.268),
     'L1_ffn_b_out': (0.0, 0.1)}
    factors = {'L0_attn_qkv': 8.0,
     'L0_attn_wo': 8.0,
     'L1_attn_Wq': 64.0,
     'L1_attn_Wk': 64.0,
     'L1_attn_Wb': 64.0,
     'L1_attn_conv_w_q': 64.0,
     'L1_attn_conv_w_k': 64.0,
     'L1_attn_fir_short_w': 4.109,
     'L1_attn_fir_long_w': 25.105,
     'L1_attn_mlp_w1': 200.0,
     'L1_attn_mlp_w2': 25.029,
     'L1_attn_mlp_b2': 54.448}
    for name, (base, spread) in spreads.items():
        noise = np.random.default_rng([zlib.crc32(name.encode()), seed]).standard_normal(out[name].shape)
        drawn = base * np.exp(spread * noise) if base else spread * noise
        out[name] = jnp.asarray(drawn.astype(out[name].dtype))
    for name, factor in factors.items():
        out[name] = (out[name] * factor).astype(out[name].dtype)
    return out
```

```python
from contextlib import ExitStack

import numpy as np

import concourse.bass as bass
from concourse import mybir

P = 128
S = 64
D = 128
H = 16
DK = 64
PAIRS = H // 2
NK = 6272
KT = NK // P
CH = 7
TC = KT // CH
CK = TC * P
HALF = CK // 2
RT = H * S // P
EXPERTS = 8
FF = 512
FT = FF // P
AH, AD = 16, 8
DH, DD = 4, 32
FIR_S, FIR_L, TAPS = 5, 64, 4
FLOOR = 0.08
MASKED = -1e20
NEVER = -1e30
LN_EPS = 1e-5
ROUND = 12582912.0

ALU = mybir.AluOpType
ACT = mybir.ActivationFunctionType
AX = mybir.AxisListType.X
F32 = mybir.dt.float32
BF16 = mybir.dt.bfloat16
I32 = mybir.dt.int32
U32 = mybir.dt.uint32

CONST = {}
_at = 0
for _name, _width in [("ident", P), ("ones", P), ("block32", P), ("later", S), ("upto", S), ("head8", AH),
                      ("half", 2), ("cos", AD), ("sin", AD), ("head32", DH), ("iota8", EXPERTS),
                      ("power", 1)]:
    CONST[_name] = (_at, _at + _width)
    _at += _width
CONST_W = _at

PARAM = {}
_at = 0
for _name, _width in [("conv_q", TAPS), ("conv_k", TAPS), ("conv_v", TAPS), ("fir_s", FIR_S), ("fir_l", FIR_L),
                      ("b1", 1), ("b_in", FT), ("rms_w", D), ("bo", D), ("b_out", D), ("b2", 4), ("temp", 1),
                      ("res", DH), ("wb", D), ("w2", 4), ("router", EXPERTS)]:
    PARAM[_name] = (_at, _at + _width)
    _at += _width
PARAM_W = _at


def constants():
    t = np.zeros((P, CONST_W), np.float32)

    def put(name, value):
        a, b = CONST[name]
        t[:, a:b] = value

    p = np.arange(P)[:, None]
    tok = p % S
    put("ident", np.eye(P))
    put("ones", 1.0)
    put("block32", p // DD == np.arange(P)[None] // DD)
    put("later", np.arange(S)[None] > tok)
    put("upto", tok <= np.arange(S)[None])
    put("head8", p // AD == np.arange(AH)[None])
    put("half", p // S == np.arange(2)[None])
    inv = (1.0 / 10000.0 ** (np.arange(0, AD, 2, dtype=np.float32) / AD)).astype(np.float32)
    ang = tok.astype(np.float32) * inv[None]
    put("cos", np.concatenate([np.cos(ang), np.cos(ang)], 1))
    put("sin", np.concatenate([-np.sin(ang), np.sin(ang)], 1))
    put("head32", p // DD == np.arange(DH)[None])
    put("iota8", np.arange(EXPERTS)[None])
    put("power", -0.5)
    return t


def build(nc, dram):
    with ExitStack() as ctx:
        def sb(name, shape, dt=F32):
            return ctx.enter_context(nc.sbuf_tensor(name, shape, dt))

        sems = {}

        def sem(name):
            if name not in sems:
                sems[name] = ctx.enter_context(nc.semaphore(name))
            return sems[name]

        ps = ctx.enter_context(nc.psum_tensor("ps", [P, 8, 512], F32))

        cst = sb("cst", [P, CONST_W])
        par = sb("par", [P, PARAM_W])
        x = sb("x", [P, D])
        ctxT = sb("ctxT", [P, NK])
        ctxN = sb("ctxN", [P, KT * D])
        early = sb("early", [P, NK])
        mask_raw = early[0:S, :].bitcast(I32)
        maskb = sb("maskb", [S, NK], BF16)
        wq = sb("wq", [P, H * DK])
        wkT = sb("wkT", [P, PAIRS, D])
        wv = sb("wv", [P, H * DK])
        wo = sb("wo", [P, PAIRS, D])
        a_w = sb("a_w", [P, 4 * D])
        gateT = sb("gateT", [P, EXPERTS * FF])
        upT = sb("upT", [P, EXPERTS * FF])
        down_flat = sb("downT", [P, EXPERTS * FT * D])
        downT = down_flat[:].rearrange("p (f d) -> p f d", d=D)
        d_w = sb("d_w", [P, 5 * D])
        w1s = sb("w1s", [16, D])
        win = sb("win", [P, FT, D])
        wout = sb("wout", [P, FT, D])

        def C(name, rows=slice(0, P)):
            return cst[rows, CONST[name][0]:CONST[name][1]]

        def W(name, rows=slice(0, P)):
            return par[rows, PARAM[name][0]:PARAM[name][1]]

        ident = C("ident")

        regions = [[upT, 0, EXPERTS * FF], [early, S * S, NK], [down_flat, 0, EXPERTS * FF]]

        def late(rows, *shape):
            n = int(np.prod(shape))
            region = next(g for g in regions if g[2] - g[1] >= n)
            v = region[0][0:rows, region[1]:region[1] + n]
            region[1] += n
            return v.rearrange("p (a b) -> p a b", a=shape[0]) if len(shape) > 1 else v

        stats6 = sb("stats6", [P, 6])
        mv = sb("mv", [P, 2])
        veps = sb("veps", [P, 1])
        rstd = sb("rstd", [P, 1])
        xn = sb("xn", [P, D])
        xnT = sb("xnT", [P, P])
        GT = sb("GT", [P, RT, P])
        sel = sb("sel", [S, 2, S], BF16)
        probs = sb("probs", [P, 2, CK])
        probsT = sb("probsT", [P, 2, CK])
        rowmax = sb("rowmax", [P, 2])
        negmax = sb("negmax", [P, (CH + 1) * RT])
        alpha = sb("alpha", [P, CH * RT])
        chunksum = sb("chunksum", [P, CH * RT])
        den = sb("den", [P, RT])
        rden = sb("rden", [P, RT])
        U = sb("U", [P, RT, D])
        UT = sb("UT", [P, RT, P])
        OT = sb("OT", [P, PAIRS, 2, S])
        QT = OT[:, 0:4, :, :].rearrange("p j a s -> p (j a) s")
        qk = sb("qk", [P, 2 * D])
        vblk = sb("vblk", [P, PAIRS, 2, AD])
        aqT = sb("aqT", [P, P])
        kexp = UT[:].rearrange("p r (a t) -> p (r a) t", a=2)
        sm = sb("sm", [P, 8, S])
        sm2 = sb("sm2", [P, 8, S])
        smx = sb("smx", [P, 8])
        ssum = sb("ssum", [P, 8])
        PT = sb("PT", [P, 4, P])
        rot1 = PT[:, 0:2, :].rearrange("p a b -> p (a b)")
        rot2 = PT[:, 2:4, :].rearrange("p a b -> p (a b)")
        o_s = sb("o_s", [S, D])
        oT = sb("oT", [P, 2, S])
        nlog = sb("nlog", [P, 1])
        eprob = sb("eprob", [P, EXPERTS])
        top8 = sb("top8", [P, 8])
        topi = sb("topi", [P, 8], U32)
        topf = sb("topf", [P, 8])
        chosen = sb("chosen", [P, 2, EXPERTS])
        rt16 = sb("rt16", [P, 2 * EXPERTS])
        pairsum = sb("pairsum", [P, 2])
        meanw = sb("meanw", [P, EXPERTS])
        coef = sb("coef", [P, EXPERTS])
        sg = probs[:, :, 0:FT * S]
        hT = probsT[:, :, 0:FT * P].rearrange("p b (f a s) -> p b f a s", f=FT, a=2)
        o1 = late(P, D)
        o1T = late(P, P)
        qkv_pad = [sb(f"pad{i}", [P, TAPS - 1 + S]) for i in range(3)]
        cv = late(P, 3, S)
        vpad = sb("vpad", [P, FIR_L - 1 + S])
        qkc = late(P, 2, S)
        sq = late(P, 2 * S)
        nrm = late(P, 2 * S)
        rn = late(P, 2, S)
        qkh = late(P, 2, S)
        eb = late(P, S)
        beta = late(P, S)
        kbneg = late(P, S)
        R = late(P, S)
        Z = early[:, 0:S * S].rearrange("p (g c) -> p g c", g=8)
        firp = gateT[:, 0:S * FIR_L].rearrange("p (t k) -> p t k", t=S)
        loc = late(P, 2, S)
        qexp = late(P, DH, S)
        Bm = late(S, DH, S)
        u_s = late(S, D)
        br = late(S, 4, D)
        cen = late(S, 4, D)
        st = sb("st", [S, DH, 4, 4])
        mom = sb("mom", [S, 3, 16])
        statsT = late(16, DH, S)
        hg = late(P, DH, S)
        gsm = sb("gsm", [S, DH, 4])
        gmx = sb("gmx", [S, 2, DH])
        tmpp = sb("tmpp", [P, 4])
        rtemp = sb("rtemp", [P, 1])
        sres = sb("sres", [P, 3, DH])
        prod = late(S, 4, D)
        om = late(S, D)
        osq = late(S, D)
        oms = sb("oms", [S, DH])
        orn = sb("orn", [S, DH])
        pows = sb("pows", [S, DH])
        wamx = sb("wamx", [P, 2 * FT])
        wsc = sb("wsc", [P, 2, 2 * FT])
        wqi = late(P, FT, D)
        wqo = late(P, FT, D)
        winq = late(P, FT, P)
        amx = sb("amx", [P, 1])
        amxr = sb("amxr", [1, 1])
        qs = sb("qs", [P, 3])
        xq = late(P, P)
        hid = late(P, FT, S)
        out_s = late(S, D)

        LOADS = ["x", "cst", "wq0", "wkT0", "par", "wv0", "wo0", "a_w", "gateT", "upT", "downT",
                 "wq1", "wkT1", "wv1", "wo1", "d_w", "w1s", "win", "wout"]

        block = ctx.enter_context(nc.Block())

        def loaded(eng, *names):
            for name in names:
                eng.wait_ge(sem("ld_" + name), 16)

        @block.sync
        def _(sp):
            def load(name, dst, src):
                sp.dma_start(dst, src).then_inc(sem("ld_" + name), 16)

            def chunk(kind, dst, src, c, w):
                sp.dma_start(dst[:, c * w:(c + 1) * w], src[:, c * w:(c + 1) * w]).then_inc(
                    sem(f"ld_{kind}{c}"), 16)

            load("x", x[:], dram["x"])
            load("cst", cst[:], dram["cst"])
            load("wq0", wq[:], dram["wq0"])
            load("wkT0", wkT[:], dram["wkT0"])
            for c in range(CH):
                chunk("mask", mask_raw, dram["mask"], c, CK)
                chunk("ctx", ctxT, dram["ctxT"], c, CK)
                chunk("ctx", ctxN, dram["ctxN"], c, TC * D)
            load("wv0", wv[:], dram["wv0"])
            load("wo0", wo[:], dram["wo0"])
            load("par", par[:], dram["par"])
            load("win", win[:], dram["win"])
            load("wout", wout[:], dram["wout"])
            load("a_w", a_w[:], dram["a_w"])
            load("gateT", gateT[:], dram["gateT"])
            load("upT", upT[:], dram["upT"])
            load("downT", downT, dram["downT"])
            load("d_w", d_w[:], dram["d_w"])
            load("w1s", w1s[:], dram["w1s"])
            for c in range(CH):
                sp.wait_ge(sem(f"ld_ctx{c}"), 2 * 16)
                sp.sem_inc(sem("chunks_landed"), 1)
            sp.wait_ge(sem("g_ready"), 1)
            load("wq1", wq[:], dram["wq1"])
            load("wkT1", wkT[:], dram["wkT1"])
            sp.wait_ge(sem("y_ready"), 1)
            load("wv1", wv[:], dram["wv1"])
            load("wo1", wo[:], dram["wo1"])
            sp.wait_ge(sem("result"), 1)
            sp.dma_start(dram["out"], out_s).then_inc(sem("stored"), 16)
            sp.wait_ge(sem("stored"), 16)

        def flash_pe(pe, L):
            base = L * CH * RT
            scores_ready, exp_done = sem("scores_ready"), sem("exp_done")
            turned = [sem("turned_lo"), sem("turned_hi")]
            copied = [sem("copied_lo"), sem("copied_hi")]
            pv_done, u_added = sem("pv_done"), sem("u_added")

            def scores(c, r):
                n, b, first = c * RT + r, r % 2, isinstance(c, int) and c == 0
                if not (first and r < 2):
                    pe.wait_ge(exp_done, base + n - 1)
                if r == 0 and L == 0:
                    pe.wait_ge(sem("chunks_landed"), c + 1)
                    pe.wait_ge(sem("mask_ready"), c + 1)
                for h in range(2):
                    out = ps[:, 2 * b + h, 0:HALF]
                    keys = bass.ds(c * CK + h * HALF, HALF)
                    ins = pe.matmul(out, GT[:, r, :], ctxT[:, keys], start=True, stop=(L == 1))
                    if L == 0:
                        ins = pe.matmul(out, sel[:].rearrange("p j s -> p (j s)"), maskb[:, keys], start=False,
                                        stop=True)
                ins.then_inc(scores_ready, 1)

            def turn(c, r):
                n, b, first = c * RT + r, r % 2, isinstance(c, int) and c == 0
                pe.wait_ge(exp_done, base + n + 1)
                for part, tiles in enumerate((range(0, 4), range(4, TC))):
                    if not (first and r == 0):
                        pe.wait_ge(copied[part], base + n)
                    for k in tiles:
                        ins = pe.transpose(ps[:, 4 + part, (k % 4) * P:(k % 4 + 1) * P],
                                           probs[:, b, k * P:(k + 1) * P], ident)
                    ins.then_inc(turned[part], 1)

            def pv(c, r):
                n, b, first = c * RT + r, r % 2, isinstance(c, int) and c == 0
                pe.wait_ge(copied[0], base + n + 1)
                pe.wait_ge(copied[1], base + n + 1)
                if not (first and r < 2):
                    pe.wait_ge(u_added, base + n - 1)
                for k in range(TC):
                    ins = pe.matmul(ps[:, 6 + b, 0:D], probsT[:, b, k * P:(k + 1) * P],
                                    ctxN[:, bass.ds((c * TC + k) * D, D)], start=(k == 0), stop=(k == TC - 1))
                ins.then_inc(pv_done, 1)

            def chunk(c, first=False, last=False):
                for r in range(RT):
                    if r < RT - 1:
                        scores(c, r + 1)
                    elif not last:
                        scores(c + 1, 0)
                    if r > 0:
                        pv(c, r - 1)
                    elif not first:
                        pv(c - 1, RT - 1)
                    turn(c, r)

            scores(0, 0)
            chunk(0, first=True)
            with pe.Fori(1, CH - 1) as c:
                chunk(c)
            chunk(CH - 1, last=True)
            pv(CH - 1, RT - 1)

        def flash_act(act, L):
            base = L * CH * RT
            nm_ready, exp_done = sem("negmax_ready"), sem("exp_done")
            turned, copied, pv_done = sem("turned_lo"), sem("copied_lo"), sem("pv_done")

            def exps(c, r):
                n, b, first = c * RT + r, r % 2, isinstance(c, int) and c == 0
                act.wait_ge(nm_ready, base + n + 1)
                new = negmax[:, bass.ds(n + RT, 1)]
                act.activation(alpha[:, bass.ds(n, 1)], negmax[:, bass.ds(n, 1)], ACT.Exp, bias=new, scale=-1.0)
                if not (first and r < 2):
                    act.wait_ge(sem("turned_hi"), base + n - 1)
                act.activation(probs[:, b, :].rearrange("p (h k) -> p h k", h=2), ps[:, 2 * b:2 * b + 2, 0:HALF],
                               ACT.Exp, bias=new, scale=DK ** -0.5,
                               accum_out=chunksum[:, bass.ds(n, 1)]).then_inc(exp_done, 1)

            def copy_lo(c, r):
                n, b, first = c * RT + r, r % 2, isinstance(c, int) and c == 0
                act.wait_ge(turned, base + n + 1)
                if not (first and r < 2):
                    act.wait_ge(pv_done, base + n - 1)
                act.copy(probsT[:, b, 0:4 * P], ps[:, 4, :]).then_inc(copied, 1)

            def chunk(c, last=False):
                for r in range(RT):
                    if r < RT - 1:
                        exps(c, r + 1)
                    elif not last:
                        exps(c + 1, 0)
                    copy_lo(c, r)

            exps(0, 0)
            chunk(0)
            with act.Fori(1, CH - 1) as c:
                chunk(c)
            chunk(CH - 1, last=True)

        def flash_dve(dve, L):
            base = L * CH * RT
            scores_ready, nm_ready, rowmax_ready = sem("scores_ready"), sem("negmax_ready"), sem("rowmax")
            turned, copied = sem("turned_hi"), sem("copied_hi")
            pv_done, u_added, den_added = sem("pv_done"), sem("u_added"), sem("den_added")

            def maximum(c, r):
                n, b = c * RT + r, r % 2
                dve.wait_ge(scores_ready, base + n + 1)
                dve.tensor_reduce(rowmax[:, b:b + 1], ps[:, 2 * b:2 * b + 2, 0:HALF], mybir.AxisListType.XY,
                                  ALU.max).then_inc(rowmax_ready, 1)
                dve.wait_ge(rowmax_ready, base + n + 1)
                dve.tensor_scalar(negmax[:, bass.ds(n + RT, 1)], rowmax[:, b:b + 1], -(DK ** -0.5),
                                  negmax[:, bass.ds(n, 1)], ALU.mult, ALU.min).then_inc(nm_ready, 1)

            def add(c, r):
                n, b, first = c * RT + r, r % 2, isinstance(c, int) and c == 0
                dve.wait_ge(sem("exp_done"), base + n + 1)
                if not first:
                    dve.wait_ge(den_added, base + n - RT + 1)
                dve.scalar_tensor_tensor(den[:, r:r + 1], den[:, r:r + 1], alpha[:, bass.ds(n, 1)],
                                         chunksum[:, bass.ds(n, 1)], ALU.mult, ALU.add).then_inc(den_added, 1)
                dve.wait_ge(pv_done, base + n + 1)
                if not first:
                    dve.wait_ge(u_added, base + n - RT + 1)
                dve.scalar_tensor_tensor(U[:, r, :], U[:, r, :], alpha[:, bass.ds(n, 1)],
                                         ps[:, 6 + b, 0:D], ALU.mult, ALU.add).then_inc(u_added, 1)

            def copy_hi(c, r):
                n, b, first = c * RT + r, r % 2, isinstance(c, int) and c == 0
                dve.wait_ge(turned, base + n + 1)
                if not (first and r < 2):
                    dve.wait_ge(pv_done, base + n - 1)
                dve.tensor_copy(probsT[:, b, 4 * P:CK], ps[:, 5, 0:(TC - 4) * P]).then_inc(copied, 1)

            def chunk(c, first=False, last=False):
                for r in range(RT):
                    if r < RT - 1:
                        maximum(c, r + 1)
                    elif not last:
                        maximum(c + 1, 0)
                    if r > 0:
                        add(c, r - 1)
                    elif not first:
                        add(c - 1, RT - 1)
                    copy_hi(c, r)

            maximum(0, 0)
            chunk(0, first=True)
            with dve.Fori(1, CH - 1) as c:
                chunk(c)
            chunk(CH - 1, last=True)
            add(CH - 1, RT - 1)
            dve.wait_ge(den_added, base + CH * RT)
            dve.wait_ge(u_added, base + CH * RT)

        def norm_dve(dve, seq, i):
            seq(dve.bn_stats(stats6[:], x[:]))
            seq(dve.bn_aggr(mv[:], stats6[:]))
            dve.tensor_scalar(veps[:], mv[:, 1:2], LN_EPS, None, ALU.add).then_inc(sem("ln_var"), 1)
            dve.wait_ge(sem("ln_rstd"), i + 1)
            dve.tensor_scalar(xn[:], x[:], mv[:, 0:1], rstd[:], ALU.subtract, ALU.mult).then_inc(sem("ln_xn"), 1)
            dve.wait_ge(sem("ln_turned"), i + 1)
            dve.tensor_copy(xnT[:], ps[:, 7, 0:P]).then_inc(sem("ln_xnT"), 1)
            dve.wait_ge(sem("ln_xnT"), i + 1)

        def norm_pool(pool, i):
            pool.wait_ge(sem("ln_var"), i + 1)
            pool.tensor_tensor(rstd[:], veps[:], C("power"), ALU.pow).then_inc(sem("ln_rstd"), 1)

        def norm_pe(pe, i):
            pe.wait_ge(sem("ln_xn"), i + 1)
            pe.transpose(ps[:, 7, 0:P], xn[:], ident).then_inc(sem("ln_turned"), 1)

        def fold_q_pe(pe, L, i, src):
            for j in range(PAIRS):
                ins = pe.matmul(ps[:, 0, j * S:(j + 1) * S], wq[:, j * P:(j + 1) * P], src[:, 0:S],
                                start=True, stop=True)
            ins.then_inc(sem("q_ready"), 1)
            pe.wait_ge(sem("q_copied"), i + 1)
            for j in range(PAIRS):
                for par_ in range(2):
                    rows = slice(par_ * DK, (par_ + 1) * DK)
                    ins = pe.matmul(ps[:, 1 + par_, j * S:(j + 1) * S], wkT[rows, j, :], QT[rows, j, :],
                                    start=True, stop=True)
            ins.then_inc(sem("g_ready"), 1)

        def fold_q_dve(dve, i):
            dve.wait_ge(sem("q_ready"), i + 1)
            dve.tensor_copy(QT.rearrange("p j s -> p (j s)"), ps[:, 0, :]).then_inc(sem("q_copied"), 1)
            dve.wait_ge(sem("g_ready"), i + 1)
            dve.tensor_copy(GT[:, 0:4, :].rearrange("p r c -> p (r c)"), ps[:, 1, :]).then_inc(sem("g_copied"), 1)

        def fold_q_act(act, i):
            act.wait_ge(sem("g_ready"), i + 1)
            act.copy(GT[:, 4:8, :].rearrange("p r c -> p (r c)"), ps[:, 2, :]).then_inc(sem("g_copied"), 1)

        def project_pe(pe, L, i):
            pe.wait_ge(sem("ut_copied"), 2 * i + 2)
            for j in range(PAIRS):
                for par_ in range(2):
                    h, g = 2 * j + par_, par_ * PAIRS + j
                    ins = pe.matmul(ps[par_ * DK:(par_ + 1) * DK, 2, j * S:(j + 1) * S],
                                    wv[:, h * DK:(h + 1) * DK], UT[:, g // 2, (g % 2) * S:(g % 2 + 1) * S],
                                    start=True, stop=True)
            ins.then_inc(sem("o_ready"), 1)
            pe.wait_ge(sem("o_copied"), i + 1)
            for j in range(PAIRS):
                ins = pe.matmul(ps[:, 3, 0:D], OT[:, j, :, :].rearrange("p a s -> p (a s)"), wo[:, j, :],
                                start=(j == 0), stop=(j == PAIRS - 1))
            ins.then_inc(sem("y_ready"), 1)

        def project_dve(dve, i):
            dve.wait_ge(sem("o_ready"), i + 1)
            dve.tensor_copy(OT[:], ps[:, 2, :].rearrange("p (j s) -> p j s", j=PAIRS).unsqueeze(2).broadcast_to(
                [P, PAIRS, 2, S])).then_inc(sem("o_copied"), 1)
            dve.wait_ge(sem("y_ready"), i + 1)

        def turn_u_pe(pe, L):
            pe.wait_ge(sem("u_scaled"), L + 1)
            for r in range(RT):
                ins = pe.transpose(ps[:, r // 4, (r % 4) * P:(r % 4 + 1) * P], U[:, r, :], ident)
                if r % 4 == 3:
                    ins.then_inc(sem("u_turned"), 1)

        def turn_u_dve(dve, seq, L):
            seq(dve.reciprocal(rden[:], den[:]))
            dve.tensor_tensor(U[:], U[:], rden[:].unsqueeze(2).broadcast_to([P, RT, D]),
                              ALU.mult).then_inc(sem("u_scaled"), 1)
            dve.wait_ge(sem("u_turned"), 2 * L + 1)
            dve.tensor_copy(UT[:, 0:4, :].rearrange("p r c -> p (r c)"), ps[:, 0, :]).then_inc(sem("ut_copied"), 1)

        def turn_u_act(act, L):
            act.wait_ge(sem("u_turned"), 2 * L + 2)
            act.copy(UT[:, 4:8, :].rearrange("p r c -> p (r c)"), ps[:, 1, :]).then_inc(sem("ut_copied"), 1)

        @block.tensor
        def _(pe):
            loaded(pe, "cst", "wq0", "wkT0")
            norm_pe(pe, 0)
            pe.wait_ge(sem("ln_xnT"), 1)
            fold_q_pe(pe, 0, 0, xnT)
            pe.wait_ge(sem("g_copied"), 2)
            pe.wait_ge(sem("sel_ready"), 1)
            flash_pe(pe, 0)
            turn_u_pe(pe, 0)
            loaded(pe, "wv0", "wo0")
            project_pe(pe, 0, 0)

            norm_pe(pe, 1)
            pe.wait_ge(sem("ln_xnT"), 2)
            loaded(pe, "a_w")
            pe.matmul(ps[:, 0, 0:2 * D], xnT[:], a_w[:, 0:2 * D], start=True, stop=True)
            pe.matmul(ps[:, 1, 0:D], xnT[:], a_w[:, 2 * D:3 * D], start=True, stop=True).then_inc(sem("a_qkv"), 1)
            pe.wait_ge(sem("a_rotated"), 1)
            pe.transpose(ps[:, 2, 0:P], qk[:, 0:D], ident)
            pe.transpose(ps[:, 2, P:2 * P], qk[:, D:2 * D], ident).then_inc(sem("a_turned"), 1)
            pe.wait_ge(sem("a_kexp"), 1)
            for hh in range(2):
                ins = pe.matmul(ps[hh * S:(hh + 1) * S, 3, :], aqT[:, hh * S:(hh + 1) * S],
                                kexp[:, 8 * hh:8 * hh + 8, :], start=True, stop=True)
            ins.then_inc(sem("a_scores"), 1)
            pe.wait_ge(sem("a_probs"), 1)
            for j in range(4):
                ins = pe.transpose(ps[:, 4, j * P:(j + 1) * P], sm[:, 2 * j:2 * j + 2, :].rearrange("p a t -> p (a t)"),
                                   ident)
            ins.then_inc(sem("a_pturned"), 1)
            pe.wait_ge(sem("a_pcopied"), 1)
            for hh in range(2):
                for j in range(4):
                    pr = 4 * hh + j
                    ins = pe.matmul(ps[0:S, 5, pr * 16:(pr + 1) * 16], PT[:, j, hh * S:(hh + 1) * S],
                                    vblk[:, pr, :, :].rearrange("p a d -> p (a d)"), start=True, stop=True)
            ins.then_inc(sem("a_out"), 1)
            pe.wait_ge(sem("a_ocopied"), 1)
            pe.transpose(ps[:, 6, 0:S], o_s[:], C("ident", slice(0, S))[:, 0:S]).then_inc(sem("a_oturned"), 1)
            pe.wait_ge(sem("a_oT"), 1)
            pe.matmul(ps[:, 5, 128:256], oT[:].rearrange("p a s -> p (a s)"), a_w[:, 3 * D:4 * D],
                      start=True, stop=True).then_inc(sem("a_y"), 1)

            norm_pe(pe, 2)
            pe.wait_ge(sem("ln_xnT"), 3)
            loaded(pe, "par", "gateT", "upT", "downT")
            pe.matmul(ps[:, 0, 0:EXPERTS], xnT[:], W("router"), start=True, stop=True).then_inc(sem("m_logits"), 1)

            def gate_up(e):
                b = e % 2
                if e >= 2:
                    pe.wait_ge(sem("m_h"), e - 1)
                for w, bank in ((gateT, 2 + b), (upT, 4 + b)):
                    for f in range(FT):
                        ins = pe.matmul(ps[:, bank, f * S:(f + 1) * S], w[:, (e * FT + f) * P:(e * FT + f + 1) * P],
                                        xnT[:, 0:S], start=True, stop=True)
                    ins.then_inc(sem("m_gate" if bank < 4 else "m_up"), 1)

            def down(e):
                pe.wait_ge(sem("m_h"), e + 1)
                for f in range(FT):
                    ins = pe.matmul(ps[:, 6 + e // 4, (e % 4) * D:(e % 4 + 1) * D],
                                    hT[:, e % 2, f, :, :].rearrange("p a s -> p (a s)"), downT[:, e * FT + f, :],
                                    start=(f == 0), stop=(f == FT - 1))
                ins.then_inc(sem("m_down"), 1)

            gate_up(0)
            gate_up(1)
            pe.wait_ge(sem("m_chosen"), 1)
            pe.matmul(ps[:, 1, 0:2 * EXPERTS], C("ones", slice(0, S)), rt16[0:S, :], start=True,
                      stop=True).then_inc(sem("m_counts"), 1)
            for e in range(2, EXPERTS):
                down(e - 2)
                gate_up(e)
            down(EXPERTS - 2)
            down(EXPERTS - 1)

            norm_pe(pe, 3)
            pe.wait_ge(sem("ln_xnT"), 4)
            loaded(pe, "wq1", "wkT1")
            fold_q_pe(pe, 1, 1, xnT)
            pe.wait_ge(sem("g_copied"), 4)
            flash_pe(pe, 1)
            turn_u_pe(pe, 1)
            loaded(pe, "wv1", "wo1")
            project_pe(pe, 1, 1)
            pe.wait_ge(sem("o1_ready"), 1)
            pe.transpose(ps[:, 7, 0:P], o1, ident).then_inc(sem("o1_turned"), 1)
            pe.wait_ge(sem("o1T_ready"), 1)
            fold_q_pe(pe, 1, 2, o1T)
            pe.wait_ge(sem("g_copied"), 6)
            for r in range(RT):
                ins = pe.matmul(ps[:, 3, r * S:(r + 1) * S], GT[:, r, :], o1T[:, 0:S], start=True, stop=True)
            ins.then_inc(sem("b_scores"), 1)
            pe.wait_ge(sem("b_probs"), 1)
            for j in range(4):
                ins = pe.transpose(ps[:, 4, j * P:(j + 1) * P], sm[:, 2 * j:2 * j + 2, :].rearrange("p a t -> p (a t)"),
                                   ident)
            ins.then_inc(sem("b_pturned"), 1)
            pe.wait_ge(sem("b_pcopied"), 1)
            for jj in range(2):
                rows = slice(jj * S, (jj + 1) * S)
                pe.matmul(ps[:, jj, :], xn[rows, :], PT[rows, :, :].rearrange("p j c -> p (j c)"), start=True,
                          stop=True).then_inc(sem("b_u"), 1)
            project_pe(pe, 1, 2)

            norm_pe(pe, 4)
            pe.wait_ge(sem("ln_xnT"), 5)
            loaded(pe, "d_w", "w1s")
            for i in range(3):
                ins = pe.matmul(ps[:, 0, i * S:(i + 1) * S], d_w[:, i * D:(i + 1) * D], xnT[:, 0:S],
                                start=True, stop=True)
            ins.then_inc(sem("d_qkv"), 1)
            pe.matmul(ps[:, 1, 0:S], W("wb"), xnT[:, 0:S], start=True, stop=True).then_inc(sem("d_beta"), 1)
            pe.wait_ge(sem("d_sq"), 1)
            pe.matmul(ps[:, 2, 0:2 * S], C("block32"), sq, start=True, stop=True).then_inc(sem("d_norm"), 1)
            for g in range(8):
                pe.wait_ge(sem("d_z"), g + 1)
                w = S - 8 * g
                pe.matmul(ps[:, g, 0:8 * w], C("block32"), Z[:, g, 0:8 * w], start=True,
                          stop=True).then_inc(sem("d_a"), 1)
            pe.wait_ge(sem("d_subst"), S - 1)
            pe.matmul(ps[0:S, 0, 0:DH * S], qkh[:, 1, :], qexp.rearrange("p h t -> p (h t)"), start=True,
                      stop=True).then_inc(sem("d_b"), 1)
            pe.transpose(ps[0:S, 1, 0:D], R, ident).then_inc(sem("d_uturned"), 1)
            pe.wait_ge(sem("d_fir"), 1)
            for i, src in ((0, loc[:, 0, :]), (1, loc[:, 1, :]), (3, vpad[:, FIR_L - 1:])):
                ins = pe.transpose(ps[0:S, 2, i * D:(i + 1) * D], src, ident)
            pe.wait_ge(sem("d_bcopied"), 1)
            pe.wait_ge(sem("d_ucopied"), 1)
            for h in range(DH):
                ins = pe.matmul(ps[0:S, 2, 2 * D + h * DD:2 * D + (h + 1) * DD], Bm[:, h, :],
                                u_s[:, h * DD:(h + 1) * DD], start=True, stop=True)
            ins.then_inc(sem("d_branches"), 1)
            pe.wait_ge(sem("d_stats"), 1)
            for h in range(DH):
                ins = pe.transpose(ps[0:16, 3, h * S:(h + 1) * S], st[:, h, :, :].rearrange("p a b -> p (a b)"),
                                   C("ident", slice(0, S))[:, 0:S])
            ins.then_inc(sem("d_sturned"), 1)
            pe.matmul(ps[:, 4, 0:DH * S], d_w[:, 4 * D:5 * D], xnT[:, 0:S].unsqueeze(1).broadcast_to([P, DH, S]),
                      start=True, stop=False)
            pe.wait_ge(sem("d_scopied"), 1)
            pe.matmul(ps[:, 4, 0:DH * S], w1s[:], statsT.rearrange("p h t -> p (h t)"), start=False,
                      stop=True).then_inc(sem("d_hidden"), 1)
            pe.wait_ge(sem("d_gelu"), 1)
            for h in range(DH):
                ins = pe.matmul(ps[0:S, 5, 4 * h:4 * h + 4], hg[:, h, :], W("w2"), start=True, stop=True)
            ins.then_inc(sem("d_gate"), 1)
            pe.wait_ge(sem("d_mixed"), 1)
            pe.transpose(ps[:, 6, 0:S], om, C("ident", slice(0, S))[:, 0:S]).then_inc(sem("d_mturned"), 1)
            pe.wait_ge(sem("d_mcopied"), 1)
            pe.matmul(ps[:, 5, 128:256], oT[:].rearrange("p a s -> p (a s)"), d_w[:, 3 * D:4 * D],
                      start=True, stop=True).then_inc(sem("d_y"), 1)

            pe.wait_ge(sem("f_wq"), 1)
            for f in range(FT):
                ins = pe.transpose(ps[:, 0, f * P:(f + 1) * P], wqi[:, f, :], ident)
            ins.then_inc(sem("f_wturned"), 1)
            norm_pe(pe, 5)
            for i in range(2):
                pe.wait_ge(sem("f_amx"), i + 1)
                pe.transpose(ps[0:1, 1, 0:P], amx[:], ident).then_inc(sem("f_amxT"), 1)
                pe.wait_ge(sem("f_amxr"), i + 1)
                pe.matmul(ps[:, 2, 0:1], C("ones", slice(0, 1)), amxr[:], start=True,
                          stop=True).then_inc(sem("f_amxb"), 1)
                if i == 0:
                    pe.wait_ge(sem("f_xq"), 1)
                    for f in range(FT):
                        ins = pe.matmul(ps[:, 3, f * S:(f + 1) * S], winq[:, f, :], xq[:, 0:S], start=True, stop=True)
                    ins.then_inc(sem("f_hidden"), 1)
            pe.wait_ge(sem("f_hq"), 1)
            for f in range(FT):
                ins = pe.matmul(ps[0:S, 4, 0:D], hid[:, f, :], wqo[:, f, :], start=(f == 0), stop=(f == FT - 1))
            ins.then_inc(sem("f_y"), 1)

        @block.gpsimd
        def _(pool):
            pool.memset(den[:], 0.0).then_inc(sem("cleared"), 1)
            pool.memset(U[:], 0.0).then_inc(sem("cleared"), 1)
            pool.memset(negmax[:, 0:RT], 3e38).then_inc(sem("cleared"), 1)
            for i in range(3):
                pool.memset(qkv_pad[i][:, 0:TAPS - 1], 0.0)
            pool.memset(vpad[:, 0:FIR_L - 1], 0.0).then_inc(sem("pads"), 1)
            loaded(pool, "cst")
            norm_pool(pool, 0)
            for c in range(CH):
                keys = slice(c * CK, (c + 1) * CK)
                pool.wait_ge(sem(f"ld_mask{c}"), 16)
                pool.tensor_scalar(maskb[:, keys], mask_raw[:, keys], 0.0, MASKED, ALU.is_equal,
                                   ALU.mult).then_inc(sem("mask_ready"), 1)
            for i in range(1, 5):
                if i == 3:
                    pool.wait_ge(sem("u_turned"), 2)
                    pool.memset(den[:], 0.0).then_inc(sem("cleared"), 1)
                    pool.memset(U[:], 0.0).then_inc(sem("cleared"), 1)
                norm_pool(pool, i)
            pool.wait_ge(sem("d_khat"), 1)
            for g in range(8):
                w = S - 8 * g
                pool.tensor_tensor(Z[:, g, 0:8 * w].rearrange("p (t u) -> p t u", t=8),
                                   qkh[:, 1, 8 * g:8 * g + 8].unsqueeze(2).broadcast_to([P, 8, w]),
                                   kbneg[:, 8 * g:].unsqueeze(1).broadcast_to([P, 8, w]),
                                   ALU.mult).then_inc(sem("d_z"), 1)
            pool.wait_ge(sem("d_msq"), 1)
            pool.tensor_tensor(orn[:], oms[:], pows[:], ALU.pow).then_inc(sem("d_mrn"), 1)
            norm_pool(pool, 5)

        @block.scalar
        def _(act):
            steps = [0]

            def seq(ins):
                steps[0] += 1
                ins.then_inc(sem("act_step"), 1)
                act.wait_ge(sem("act_step"), steps[0])

            fold_q_act(act, 0)
            act.wait_ge(sem("cleared"), 3)
            flash_act(act, 0)
            turn_u_act(act, 0)

            act.wait_ge(sem("a_shifted"), 1)
            act.activation(sm[:], sm2[:], ACT.Exp, scale=float(1.0 / np.sqrt(AD))).then_inc(sem("a_exp"), 1)
            act.wait_ge(sem("a_pturned"), 1)
            act.copy(PT[:].rearrange("p j c -> p (j c)"), ps[:, 4, :]).then_inc(sem("a_pcopied"), 1)

            act.wait_ge(sem("m_nlog"), 1)
            act.activation(eprob[:], ps[:, 0, 0:EXPERTS], ACT.Exp, bias=nlog[:]).then_inc(sem("m_exp"), 1)
            for e in range(EXPERTS):
                act.wait_ge(sem("m_gate"), e + 1)
                if e >= 2:
                    act.wait_ge(sem("m_h"), e - 1)
                act.activation(sg[:, e % 2, :], ps[:, 2 + e % 2, 0:FT * S], ACT.Silu).then_inc(sem("m_silu"), 1)

            fold_q_act(act, 1)
            flash_act(act, 1)
            turn_u_act(act, 1)
            fold_q_act(act, 2)
            act.wait_ge(sem("b_shifted"), 1)
            act.activation(sm[:], sm2[:], ACT.Exp, scale=DK ** -0.5).then_inc(sem("b_exp"), 1)
            act.wait_ge(sem("b_pturned"), 1)
            act.copy(PT[:].rearrange("p j c -> p (j c)"), ps[:, 4, :]).then_inc(sem("b_pcopied"), 1)
            act.wait_ge(sem("b_u"), 2)
            act.copy(UT[:].rearrange("p (j a) c -> p j a c", a=2)[:, :, 1, :],
                     ps[:, 1, :].rearrange("p (j c) -> p j c", j=4)).then_inc(sem("ut_copied"), 1)

            act.wait_ge(sem("d_par0"), 1)
            seq(act.activation(tmpp[:, 1:2], tmpp[:, 0:1], ACT.Exp, scale=-1.0))
            act.activation(sres[:, 1, :], sres[:, 0, :], ACT.Exp, scale=-1.0).then_inc(sem("d_eres"), 1)
            act.wait_ge(sem("d_beta"), 1)
            act.activation(eb, ps[:, 1, 0:S], ACT.Exp, scale=-1.0).then_inc(sem("d_eb"), 1)
            act.activation(tmpp[:, 2:3], tmpp[:, 1:2], ACT.Ln, bias=1.0).then_inc(sem("d_ln"), 1)
            act.wait_ge(sem("d_conv"), 1)
            act.activation(vpad[:, FIR_L - 1:], cv[:, 2, :], ACT.Silu).then_inc(sem("d_v"), 1)
            act.activation(qkc, cv[:, 0:2, :], ACT.Silu).then_inc(sem("d_qk"), 1)
            act.wait_ge(sem("d_nrm"), 1)
            act.activation(rn.rearrange("p a t -> p (a t)"), nrm, ACT.Sqrt).then_inc(sem("d_sqrt"), 1)
            act.wait_ge(sem("d_l2"), 1)
            act.activation(st[:, :, :, 3].rearrange("p h b -> p b h"),
                           mom[:, 2, :].rearrange("p (b h) -> p b h", b=4), ACT.Sqrt).then_inc(sem("d_stats"), 1)
            act.wait_ge(sem("d_hidden"), 1)
            act.activation(hg.rearrange("p h t -> p (h t)"), ps[:, 4, 0:DH * S], ACT.Gelu,
                           bias=W("b1")).then_inc(sem("d_gelu"), 1)
            act.wait_ge(sem("d_gshift"), 1)
            act.activation(gsm[:], gsm[:], ACT.Exp).then_inc(sem("d_gexp"), 1)

            for f in range(FT):
                if f == 0:
                    act.wait_ge(sem("f_hidden"), 1)
                ins = act.activation(hid[:, f, :], ps[:, 3, f * S:(f + 1) * S], ACT.Gelu,
                                     bias=par[:, PARAM["b_in"][0] + f:PARAM["b_in"][0] + f + 1])
            ins.then_inc(sem("f_gelu"), 1)

        @block.vector
        def _(dve):
            steps = [0]

            def seq(ins):
                steps[0] += 1
                ins.then_inc(sem("dve_step"), 1)
                dve.wait_ge(sem("dve_step"), steps[0])

            loaded(dve, "x", "cst")
            norm_dve(dve, seq, 0)
            fold_q_dve(dve, 0)
            dve.tensor_copy(sel[:], C("ident", slice(0, S))[:, 0:S].unsqueeze(1).broadcast_to([S, 2, S])).then_inc(
                sem("sel_ready"), 1)
            dve.wait_ge(sem("cleared"), 3)
            flash_dve(dve, 0)
            turn_u_dve(dve, seq, 0)
            project_dve(dve, 0)
            seq(dve.tensor_tensor(x[:], x[:], ps[:, 3, 0:D], ALU.add))

            norm_dve(dve, seq, 1)
            dve.wait_ge(sem("a_qkv"), 1)
            heads = ps[:, 0, 0:2 * D].rearrange("p (h d) -> p h d", d=AD)
            r1, r2 = rot1.rearrange("p (h d) -> p h d", d=AD), rot2.rearrange("p (h d) -> p h d", d=AD)
            hd = AD // 2
            dve.tensor_tensor(r1, heads, C("cos").unsqueeze(1).broadcast_to([P, 2 * AH, AD]), ALU.mult)
            dve.tensor_tensor(r2[:, :, 0:hd], heads[:, :, hd:AD],
                              C("sin")[:, 0:hd].unsqueeze(1).broadcast_to([P, 2 * AH, hd]), ALU.mult)
            seq(dve.tensor_tensor(r2[:, :, hd:AD], heads[:, :, 0:hd],
                                  C("sin")[:, hd:AD].unsqueeze(1).broadcast_to([P, 2 * AH, hd]), ALU.mult))
            dve.tensor_tensor(qk[:], rot1, rot2, ALU.add).then_inc(sem("a_rotated"), 1)
            seq(dve.tensor_tensor(vblk[:], ps[:, 1, 0:D].rearrange("p (j a d) -> p j a d", j=PAIRS, a=2),
                                  C("half").unsqueeze(1).unsqueeze(3).broadcast_to([P, PAIRS, 2, AD]), ALU.mult))
            dve.wait_ge(sem("a_turned"), 1)
            dve.tensor_copy(aqT[:], ps[:, 2, 0:P])
            dve.tensor_tensor(kexp, ps[:, 2, P:P + S].unsqueeze(1).broadcast_to([P, AH, S]),
                              C("head8").unsqueeze(2).broadcast_to([P, AH, S]), ALU.mult).then_inc(sem("a_kexp"), 1)
            dve.wait_ge(sem("a_scores"), 1)
            sc = ps[:, 3, :].rearrange("p (h t) -> p h t", h=8)
            seq(dve.scalar_tensor_tensor(sm[:], sc, 0.0, C("later").unsqueeze(1).broadcast_to([P, 8, S]),
                                         ALU.is_equal, ALU.max))
            seq(dve.scalar_tensor_tensor(sm2[:], sm[:], NEVER, sc, ALU.mult, ALU.add))

            def shift(name):
                seq(dve.tensor_reduce(smx[:], sm2[:], AX, ALU.max))
                dve.tensor_tensor(sm2[:], sm2[:], smx[:].unsqueeze(2).broadcast_to([P, 8, S]),
                                  ALU.subtract).then_inc(sem(name), 1)

            def normalise(exp_name, name):
                dve.wait_ge(sem(exp_name), 1)
                seq(dve.tensor_reduce(ssum[:], sm[:], AX, ALU.add))
                seq(dve.reciprocal(smx[:], ssum[:]))
                dve.tensor_tensor(sm[:], sm[:], smx[:].unsqueeze(2).broadcast_to([P, 8, S]),
                                  ALU.mult).then_inc(sem(name), 1)

            shift("a_shifted")
            normalise("a_exp", "a_probs")
            dve.wait_ge(sem("a_out"), 1)
            dve.tensor_copy(o_s[:], ps[0:S, 5, 0:D]).then_inc(sem("a_ocopied"), 1)
            dve.wait_ge(sem("a_oturned"), 1)
            dve.tensor_copy(oT[:], ps[:, 6, 0:S].unsqueeze(1).broadcast_to([P, 2, S])).then_inc(sem("a_oT"), 1)
            dve.wait_ge(sem("a_y"), 1)
            seq(dve.tensor_tensor(x[:], x[:], ps[:, 5, 128:256], ALU.add))

            norm_dve(dve, seq, 2)
            dve.wait_ge(sem("m_logits"), 1)
            dve.tensor_reduce(nlog[:], ps[:, 0, 0:EXPERTS], AX, ALU.max, negate=True).then_inc(sem("m_nlog"), 1)
            dve.wait_ge(sem("m_exp"), 1)
            seq(dve.max(top8[:], eprob[:]))
            seq(dve.max_index(topi[:], top8[:], eprob[:]))
            seq(dve.tensor_copy(topf[:], topi[:]))
            for k in range(2):
                dve.tensor_scalar(chosen[:, k, :], C("iota8"), topf[:, k:k + 1], None, ALU.is_equal)
                seq(dve.tensor_scalar(sm2[:, k, 0:EXPERTS], C("iota8"), topf[:, k:k + 1], top8[:, k:k + 1],
                                      ALU.is_equal, ALU.mult))
            dve.tensor_tensor(rt16[:, 0:EXPERTS], chosen[:, 0, :], chosen[:, 1, :], ALU.add)
            seq(dve.tensor_tensor(pairsum[:, 0:1], top8[:, 0:1], top8[:, 1:2], ALU.add))
            dve.tensor_tensor(sm2[:, 2, 0:EXPERTS], sm2[:, 0, 0:EXPERTS], sm2[:, 1, 0:EXPERTS], ALU.add)
            seq(dve.reciprocal(pairsum[:, 1:2], pairsum[:, 0:1]))
            dve.tensor_scalar(rt16[:, EXPERTS:], sm2[:, 2, 0:EXPERTS], pairsum[:, 1:2], None,
                              ALU.mult).then_inc(sem("m_chosen"), 1)

            def hidden(e):
                dve.wait_ge(sem("m_up"), e + 1)
                dve.wait_ge(sem("m_silu"), e + 1)
                if e >= 2:
                    dve.wait_ge(sem("m_down"), e - 1)
                for a in range(2):
                    ins = dve.tensor_tensor(hT[:, e % 2, :, a, :], sg[:, e % 2, :].rearrange("p (f s) -> p f s", f=FT),
                                            ps[:, 4 + e % 2, 0:FT * S].rearrange("p (f s) -> p f s", f=FT), ALU.mult)
                ins.then_inc(sem("m_h"), 1)

            hidden(0)
            hidden(1)
            dve.wait_ge(sem("m_counts"), 1)
            seq(dve.tensor_scalar(meanw[:], ps[:, 1, 0:EXPERTS], 1.0, None, ALU.max))
            seq(dve.reciprocal(coef[:], meanw[:]))
            seq(dve.tensor_tensor(meanw[:], coef[:], ps[:, 1, EXPERTS:2 * EXPERTS], ALU.mult))
            seq(dve.tensor_tensor(coef[:], meanw[:], rt16[:, 0:EXPERTS], ALU.mult))
            for e in range(2, EXPERTS):
                hidden(e)
            for e in range(EXPERTS):
                dve.wait_ge(sem("m_down"), EXPERTS if e >= 4 else 4)
                seq(dve.scalar_tensor_tensor(x[:], ps[:, 6 + e // 4, (e % 4) * D:(e % 4 + 1) * D], coef[:, e:e + 1],
                                             x[:], ALU.mult, ALU.add))

            norm_dve(dve, seq, 3)
            fold_q_dve(dve, 1)
            dve.wait_ge(sem("cleared"), 5)
            flash_dve(dve, 1)
            turn_u_dve(dve, seq, 1)
            project_dve(dve, 1)
            seq(dve.tensor_tensor(o1, xn[:], ps[:, 3, 0:D], ALU.add))
            dve.tensor_tensor(o1, o1, W("bo"), ALU.add).then_inc(sem("o1_ready"), 1)
            dve.wait_ge(sem("o1_turned"), 1)
            dve.tensor_copy(o1T, ps[:, 7, 0:P]).then_inc(sem("o1T_ready"), 1)
            fold_q_dve(dve, 2)
            dve.wait_ge(sem("b_scores"), 1)
            sc = ps[:, 3, :].rearrange("p (h t) -> p h t", h=8)
            seq(dve.tensor_reduce(smx[:], sc, AX, ALU.max))
            dve.tensor_tensor(sm2[:], sc, smx[:].unsqueeze(2).broadcast_to([P, 8, S]),
                              ALU.subtract).then_inc(sem("b_shifted"), 1)
            normalise("b_exp", "b_probs")
            dve.wait_ge(sem("b_u"), 1)
            dve.tensor_copy(UT[:].rearrange("p (j a) c -> p j a c", a=2)[:, :, 0, :],
                            ps[:, 0, :].rearrange("p (j c) -> p j c", j=4)).then_inc(sem("ut_copied"), 1)
            project_dve(dve, 2)
            seq(dve.tensor_tensor(x[:], x[:], ps[:, 3, 0:D], ALU.add))
            seq(dve.tensor_tensor(x[:], x[:], W("bo"), ALU.add))

            norm_dve(dve, seq, 4)
            seq(dve.tensor_scalar(tmpp[:, 0:1], W("temp"), -1.0, None, ALU.mult))
            seq(dve.tensor_tensor(tmpp[:, 0:1], tmpp[:, 0:1], W("temp"), ALU.max))
            dve.tensor_copy(sres[:, 0, :], W("res")).then_inc(sem("d_par0"), 1)
            dve.wait_ge(sem("pads"), 1)
            dve.wait_ge(sem("d_qkv"), 1)
            for i in range(3):
                seq(dve.tensor_copy(qkv_pad[i][:, TAPS - 1:], ps[:, 0, i * S:(i + 1) * S]))
            for k in range(TAPS):
                for i, name in enumerate(("conv_q", "conv_k", "conv_v")):
                    a = PARAM[name][0] + k
                    if k == 0:
                        ins = dve.tensor_scalar(cv[:, i, :], qkv_pad[i][:, k:k + S], par[:, a:a + 1], None, ALU.mult)
                    else:
                        ins = dve.scalar_tensor_tensor(cv[:, i, :], qkv_pad[i][:, k:k + S], par[:, a:a + 1],
                                                       cv[:, i, :], ALU.mult, ALU.add)
                    if k < TAPS - 1:
                        seq(ins)
            ins.then_inc(sem("d_conv"), 1)
            dve.wait_ge(sem("d_eb"), 1)
            seq(dve.tensor_scalar(eb, eb, 1.0, None, ALU.add))
            seq(dve.reciprocal(beta, eb))
            dve.wait_ge(sem("d_eres"), 1)
            seq(dve.tensor_scalar(sres[:, 1, :], sres[:, 1, :], 1.0, None, ALU.add))
            seq(dve.reciprocal(sres[:, 2, :], sres[:, 1, :]))
            dve.wait_ge(sem("d_ln"), 1)
            seq(dve.scalar_tensor_tensor(tmpp[:, 3:4], W("temp"), 0.0, tmpp[:, 2:3], ALU.max, ALU.add))
            seq(dve.tensor_scalar(tmpp[:, 3:4], tmpp[:, 3:4], 1e-6, None, ALU.add))
            seq(dve.reciprocal(rtemp[:], tmpp[:, 3:4]))
            dve.wait_ge(sem("d_qk"), 1)
            dve.tensor_tensor(sq, qkc.rearrange("p a t -> p (a t)"), qkc.rearrange("p a t -> p (a t)"),
                              ALU.mult).then_inc(sem("d_sq"), 1)
            dve.wait_ge(sem("d_norm"), 1)
            dve.tensor_scalar(nrm, ps[:, 2, 0:2 * S], 1e-12, None, ALU.add).then_inc(sem("d_nrm"), 1)
            dve.wait_ge(sem("d_v"), 1)
            seq(dve.tensor_tensor(R, vpad[:, FIR_L - 1:], beta, ALU.mult))
            dve.wait_ge(sem("d_sqrt"), 1)
            seq(dve.reciprocal(rn, rn))
            seq(dve.tensor_tensor(qkh, qkc, rn, ALU.mult))
            dve.scalar_tensor_tensor(kbneg, qkh[:, 1, :], -1.0, beta, ALU.mult,
                                     ALU.mult).then_inc(sem("d_khat"), 1)
            seq(dve.tensor_tensor(qexp, qkh[:, 0, :].unsqueeze(1).broadcast_to([P, DH, S]),
                                  C("head32").unsqueeze(2).broadcast_to([P, DH, S]), ALU.mult))
            for k in range(FIR_S):
                a = PARAM["fir_s"][0] + k
                win_ = vpad[:, FIR_L - FIR_S + k:FIR_L - FIR_S + k + S]
                if k == 0:
                    seq(dve.tensor_scalar(loc[:, 0, :], win_, par[:, a:a + 1], None, ALU.mult))
                else:
                    seq(dve.scalar_tensor_tensor(loc[:, 0, :], win_, par[:, a:a + 1], loc[:, 0, :],
                                                 ALU.mult, ALU.add))
            for t in range(S - 1):
                if t % 8 == 0:
                    dve.wait_ge(sem("d_a"), t // 8 + 1)
                w = S - 8 * (t // 8)
                a = (t % 8) * w + t % 8 + 1
                dve.scalar_tensor_tensor(R[:, t + 1:], ps[:, t // 8, a:a + S - 1 - t], R[:, t:t + 1], R[:, t + 1:],
                                         ALU.mult, ALU.add).then_inc(sem("d_subst"), 1)
                dve.wait_ge(sem("d_subst"), t + 1)
            windows = bass.AP(tensor=vpad[:].tensor, offset=vpad[:].offset, ap=[list(vpad[:].ap[0]), [1, S], [1, FIR_L]])
            seq(dve.tensor_tensor(firp, windows, W("fir_l").unsqueeze(1).broadcast_to([P, S, FIR_L]), ALU.mult))
            dve.tensor_reduce(loc[:, 1, :], firp, AX, ALU.add).then_inc(sem("d_fir"), 1)
            dve.wait_ge(sem("d_b"), 1)
            dve.tensor_tensor(Bm, ps[0:S, 0, 0:DH * S].rearrange("p (h t) -> p h t", h=DH),
                              C("upto", slice(0, S)).unsqueeze(1).broadcast_to([S, DH, S]),
                              ALU.mult).then_inc(sem("d_bcopied"), 1)
            dve.wait_ge(sem("d_uturned"), 1)
            dve.tensor_copy(u_s, ps[0:S, 1, 0:D]).then_inc(sem("d_ucopied"), 1)
            dve.wait_ge(sem("d_branches"), 1)
            seq(dve.tensor_copy(br.rearrange("p b c -> p (b c)"), ps[0:S, 2, :]))
            g16 = br.rearrange("p b (h d) -> p (b h) d", h=DH)
            c16 = cen.rearrange("p b (h d) -> p (b h) d", h=DH)

            def stat(k):
                return st[:, :, :, k].rearrange("p h b -> p b h")

            def m16(k):
                return mom[:, k, :].rearrange("p (b h) -> p b h", b=4)

            seq(dve.tensor_reduce(mom[:, 0, :], g16, AX, ALU.add))
            dve.tensor_reduce(mom[:, 1, :], g16, AX, ALU.add, apply_absolute_value=True)
            seq(dve.tensor_scalar(mom[:, 0, :], mom[:, 0, :], 1.0 / DD, None, ALU.mult))
            dve.tensor_scalar(stat(0), m16(0), 1.0, None, ALU.mult)
            seq(dve.tensor_tensor(c16, g16, mom[:, 0, :].unsqueeze(2).broadcast_to([S, 16, DD]), ALU.subtract))
            dve.tensor_scalar(stat(2), m16(1), 1.0 / DD, None, ALU.mult)
            seq(dve.tensor_tensor(cen, cen, cen, ALU.mult))
            seq(dve.tensor_reduce(mom[:, 1, :], c16, AX, ALU.add))
            dve.tensor_scalar(stat(1), m16(1), 1.0 / DD, None, ALU.mult)
            seq(dve.tensor_tensor(prod, br, br, ALU.mult))
            dve.tensor_reduce(mom[:, 2, :], prod.rearrange("p b (h d) -> p (b h) d", h=DH), AX,
                              ALU.add).then_inc(sem("d_l2"), 1)
            dve.wait_ge(sem("d_sturned"), 1)
            dve.tensor_copy(statsT.rearrange("p h t -> p (h t)"), ps[0:16, 3, 0:DH * S]).then_inc(
                sem("d_scopied"), 1)
            dve.wait_ge(sem("d_gate"), 1)
            seq(dve.tensor_tensor(gsm[:], ps[0:S, 5, 0:16].rearrange("p (h b) -> p h b", h=DH),
                                  W("b2", slice(0, S)).unsqueeze(1).broadcast_to([S, DH, 4]), ALU.add))
            seq(dve.tensor_scalar(gsm[:], gsm[:], rtemp[0:S, :], None, ALU.mult))
            seq(dve.tensor_reduce(gmx[:, 0, :], gsm[:], AX, ALU.max))
            dve.tensor_tensor(gsm[:], gsm[:], gmx[:, 0, :].unsqueeze(2).broadcast_to([S, DH, 4]),
                              ALU.subtract).then_inc(sem("d_gshift"), 1)
            dve.wait_ge(sem("d_gexp"), 1)
            seq(dve.tensor_reduce(gmx[:, 0, :], gsm[:], AX, ALU.add))
            seq(dve.reciprocal(gmx[:, 1, :], gmx[:, 0, :]))
            seq(dve.tensor_tensor(gsm[:], gsm[:], gmx[:, 1, :].unsqueeze(2).broadcast_to([S, DH, 4]), ALU.mult))
            seq(dve.tensor_scalar(gsm[:], gsm[:], 1.0 - 2.0 * FLOOR, None, ALU.mult))
            seq(dve.tensor_scalar(gsm[:, :, 0:2], gsm[:, :, 0:2], FLOOR, None, ALU.add))
            seq(dve.tensor_tensor(gsm[:, :, 0], gsm[:, :, 0], sres[0:S, 2, :], ALU.add))
            for b in range(4):
                ins = dve.tensor_tensor(prod[:, b, :].rearrange("p (h d) -> p h d", h=DH),
                                        br[:, b, :].rearrange("p (h d) -> p h d", h=DH),
                                        gsm[:, :, b:b + 1].broadcast_to([S, DH, DD]), ALU.mult)
            seq(ins)
            seq(dve.tensor_tensor(prod[:, 0:2, :], prod[:, 0:2, :], prod[:, 2:4, :], ALU.add))
            seq(dve.tensor_tensor(om, prod[:, 0, :], prod[:, 1, :], ALU.add))
            dve.memset(pows[:], -0.5)
            seq(dve.tensor_tensor(osq, om, om, ALU.mult))
            seq(dve.tensor_reduce(oms[:], osq.rearrange("p (h d) -> p h d", h=DH), AX, ALU.add))
            dve.tensor_scalar(oms[:], oms[:], 1.0 / DD, 1e-5, ALU.mult, ALU.add).then_inc(sem("d_msq"), 1)
            dve.wait_ge(sem("d_mrn"), 1)
            seq(dve.tensor_tensor(om.rearrange("p (h d) -> p h d", h=DH), om.rearrange("p (h d) -> p h d", h=DH),
                                  orn[:].unsqueeze(2).broadcast_to([S, DH, DD]), ALU.mult))
            dve.tensor_tensor(om, om, W("rms_w", slice(0, S)), ALU.mult).then_inc(sem("d_mixed"), 1)
            loaded(dve, "win", "wout")
            for i, w in enumerate((win, wout)):
                dve.tensor_reduce(wamx[:, i * FT:(i + 1) * FT], w[:], AX, ALU.max, apply_absolute_value=True)
            seq(dve.memset(qs[:, 0:1], 0.0))
            seq(dve.tensor_scalar(wamx[:], wamx[:], 1e-8, None, ALU.max))
            seq(dve.reciprocal(wsc[:, 0, :], wamx[:]))
            seq(dve.tensor_scalar(wsc[:, 0, :], wsc[:, 0, :], 127.0, None, ALU.mult))
            seq(dve.reciprocal(wsc[:, 1, :], wsc[:, 0, :]))
            for i, (w, q) in enumerate(((win, wqi), (wout, wqo))):
                s0 = wsc[:, 0, i * FT:(i + 1) * FT].unsqueeze(2).broadcast_to([P, FT, D])
                s1 = wsc[:, 1, i * FT:(i + 1) * FT].unsqueeze(2).broadcast_to([P, FT, D])
                seq(dve.tensor_tensor(q, w[:], s0, ALU.mult))
                seq(dve.tensor_scalar(q, q, ROUND, ROUND, ALU.add, ALU.subtract))
                seq(dve.tensor_scalar(q, q, -128.0, 127.0, ALU.max, ALU.min))
                ins = dve.tensor_tensor(q, q, s1, ALU.mult)
                if i == 0:
                    ins.then_inc(sem("f_wq"), 1)
                else:
                    seq(ins)

            dve.wait_ge(sem("d_mturned"), 1)
            dve.tensor_copy(oT[:], ps[:, 6, 0:S].unsqueeze(1).broadcast_to([P, 2, S])).then_inc(sem("d_mcopied"), 1)
            dve.wait_ge(sem("d_y"), 1)
            seq(dve.tensor_tensor(x[:], x[:], ps[:, 5, 128:256], ALU.add))

            dve.wait_ge(sem("f_wturned"), 1)
            seq(dve.tensor_copy(winq.rearrange("p f c -> p (f c)"), ps[:, 0, :]))
            norm_dve(dve, seq, 5)

            def quantise(i, src, dst, name):
                dve.tensor_reduce(amx[:], src, mybir.AxisListType.XY if i else AX, ALU.max,
                                  apply_absolute_value=True).then_inc(sem("f_amx"), 1)
                dve.wait_ge(sem("f_amxT"), i + 1)
                dve.tensor_reduce(amxr[:], ps[0:1, 1, 0:P], AX, ALU.max).then_inc(sem("f_amxr"), 1)
                dve.wait_ge(sem("f_amxb"), i + 1)
                seq(dve.tensor_scalar(qs[:, 0:1], ps[:, 2, 0:1], 1e-8, None, ALU.max))
                seq(dve.reciprocal(qs[:, 1:2], qs[:, 0:1]))
                seq(dve.tensor_scalar(qs[:, 1:2], qs[:, 1:2], 32767.0, None, ALU.mult))
                seq(dve.reciprocal(qs[:, 2:3], qs[:, 1:2]))
                seq(dve.tensor_scalar(dst, src, qs[:, 1:2], ROUND, ALU.mult, ALU.add))
                seq(dve.tensor_scalar(dst, dst, ROUND, 32767.0, ALU.subtract, ALU.min))
                dve.tensor_scalar(dst, dst, -32768.0, qs[:, 2:3], ALU.max, ALU.mult).then_inc(sem(name), 1)

            quantise(0, xnT[:], xq, "f_xq")
            dve.wait_ge(sem("f_gelu"), 1)
            quantise(1, hid, hid, "f_hq")
            dve.wait_ge(sem("f_y"), 1)
            seq(dve.tensor_tensor(out_s, x[0:S, :], ps[0:S, 4, 0:D], ALU.add))
            dve.tensor_tensor(out_s, out_s, W("b_out", slice(0, S)), ALU.add).then_inc(sem("result"), 1)


def kernel(**inputs):
    import concourse.bacc as bacc
    from concourse.bass_utils import run_bass_kernel_spmd

    a = {k: np.asarray(v) for k, v in inputs.items()}

    def rows(name, width):
        return np.broadcast_to(a[name].reshape(1, width), (P, width))

    par = {
        "conv_q": a["L1_attn_conv_w_q"], "conv_k": a["L1_attn_conv_w_k"], "conv_v": a["L1_attn_conv_w_v"],
        "fir_s": a["L1_attn_fir_short_w"].reshape(D, FIR_S), "fir_l": a["L1_attn_fir_long_w"].reshape(D, FIR_L),
        "b1": a["L1_attn_mlp_b1"].reshape(D, 1), "b_in": a["L1_ffn_b_in"].reshape(FT, P).T,
        "rms_w": np.tile(rows("L1_attn_rms_w", DD), (1, DH)), "bo": rows("L1_xattn_bo", D),
        "b_out": rows("L1_ffn_b_out", D), "b2": rows("L1_attn_mlp_b2", 4), "temp": rows("L1_attn_logit_temp", 1),
        "res": rows("L1_attn_conv_res_logit", DH), "wb": np.repeat(a["L1_attn_Wb"], DD, axis=1),
        "w2": a["L1_attn_mlp_w2"], "router": a["L0_ffn_router_w"].T,
    }

    def tiles(w):
        return w.reshape(-1, P, w.shape[1]).transpose(1, 0, 2)

    ctx = a["ctx_1024"][0]
    arrays = {
        "x": np.concatenate([a["x"][0], a["x"][0]], 0),
        "cst": constants(),
        "par": np.concatenate([par[k] for k in PARAM], 1),
        "ctxT": ctx.T, "ctxN": tiles(ctx).reshape(P, KT * D), "mask": a["mask_SxS2_ik0"],
        "a_w": np.concatenate([a["L0_attn_qkv"].T, a["L0_attn_wo"].T], 1),
        "gateT": a["L0_ffn_gate_w"].reshape(EXPERTS * FF, D).T, "upT": a["L0_ffn_up_w"].reshape(EXPERTS * FF, D).T,
        "downT": tiles(a["L0_ffn_down_w"].transpose(0, 2, 1).reshape(EXPERTS * FF, D)),
        "d_w": np.concatenate([a["L1_attn_Wq"], a["L1_attn_Wk"], a["L1_attn_Wv"], a["L1_attn_Wo"],
                               a["L1_attn_mlp_w1"][0:D]], 1),
        "w1s": a["L1_attn_mlp_w1"][D:],
        "win": tiles(a["L1_ffn_W_in"].T), "wout": tiles(a["L1_ffn_W_out"]),
    }
    for i, names in enumerate((("L0_xattn_W_q", "L0_xattn_W_k", "L0_xattn_W_v", "L0_xattn_W_o"),
                               ("L1_xattn_Wq", "L1_xattn_Wk", "L1_xattn_Wv", "L1_xattn_Wo"))):
        arrays[f"wq{i}"] = a[names[0]]
        arrays[f"wkT{i}"] = tiles(a[names[1]].T)
        arrays[f"wv{i}"] = a[names[2]]
        arrays[f"wo{i}"] = tiles(a[names[3]])

    nc = bacc.Bacc("TRN2", target_bir_lowering=False, num_devices=1)
    dram, feed = {}, {}
    for name, v in arrays.items():
        v = np.ascontiguousarray(v)
        feed[f"in_{name}"] = v
        dram[name] = nc.dram_tensor(f"in_{name}", v.shape, mybir.dt.from_np(v.dtype), kind="ExternalInput").ap()
    dram["out"] = nc.dram_tensor("out", (S, D), F32, kind="ExternalOutput").ap()
    build(nc, dram)
    r = run_bass_kernel_spmd(nc, [feed], core_ids=[0])
    return r.results[0]["out"].reshape(1, S, D)
```

```python
from contextlib import ExitStack

import numpy as np

import concourse.bass as bass
from concourse import mybir

P = 128
S = 64
D = 128
H = 16
DK = 64
PAIRS = H // 2
NK = 6272
KT = NK // P
CH = 7
TC = KT // CH
CK = TC * P
HALF = CK // 2
RT = H * S // P
EXPERTS = 8
FF = 512
FT = FF // P
AH, AD = 16, 8
DH, DD = 4, 32
FIR_S, FIR_L, TAPS = 5, 64, 4
SCALE_STEP = (CH - 1) * RT + 3
DOWN_AT = [(6 + e // 4, e % 4 * D) for e in range(EXPERTS - 1)] + [(0, D)]
WARM = [0, 6, 6, 14, 6, 6]
FLOOR = 0.08
MASKED = -1e20
MASK_SLOTS = 5
NEVER = -1e30
LN_EPS = 1e-5
HALF_SCALE = 2.0 ** 15
CTX_SCALE = 2.0 ** 14
ROUND = 12582912.0

ALU = mybir.AluOpType
ACT = mybir.ActivationFunctionType
AX = mybir.AxisListType.X
F32 = mybir.dt.float32
BF16 = mybir.dt.bfloat16
F16 = mybir.dt.float16
I32 = mybir.dt.int32
U32 = mybir.dt.uint32
F32R = mybir.dt.float32r

CONST = {}
_at = 0
for _name, _width in [("ident", P), ("ones", P), ("block32", P), ("later", S), ("upto", S), ("head8", AH),
                      ("half", 2), ("cos", AD), ("sin", AD), ("head32", DH), ("iota8", EXPERTS),
                      ("power", 1)]:
    CONST[_name] = (_at, _at + _width)
    _at += _width
CONST_W = _at

PARAM = {}
_at = 0
for _name, _width in [("conv_q", TAPS), ("conv_k", TAPS), ("conv_v", TAPS), ("fir_s", FIR_S), ("fir_l", FIR_L),
                      ("b1", 1), ("b_in", FT), ("rms_w", D), ("bo", D), ("b_out", D), ("b2", 4), ("temp", 1),
                      ("res", DH), ("wb", D), ("w2", 4), ("router", EXPERTS)]:
    PARAM[_name] = (_at, _at + _width)
    _at += _width
PARAM_W = _at


def constants():
    t = np.zeros((P, CONST_W), np.float32)

    def put(name, value):
        a, b = CONST[name]
        t[:, a:b] = value

    p = np.arange(P)[:, None]
    tok = p % S
    put("ident", np.eye(P))
    put("ones", 1.0)
    put("block32", p // DD == np.arange(P)[None] // DD)
    put("later", np.arange(S)[None] > tok)
    put("upto", tok <= np.arange(S)[None])
    put("head8", p // AD == np.arange(AH)[None])
    put("half", p // S == np.arange(2)[None])
    inv = (1.0 / 10000.0 ** (np.arange(0, AD, 2, dtype=np.float32) / AD)).astype(np.float32)
    ang = tok.astype(np.float32) * inv[None]
    put("cos", np.concatenate([np.cos(ang), np.cos(ang)], 1))
    put("sin", np.concatenate([-np.sin(ang), np.sin(ang)], 1))
    put("head32", p // DD == np.arange(DH)[None])
    put("iota8", np.arange(EXPERTS)[None])
    put("power", -0.5)
    return t


def build(nc, dram):
    with ExitStack() as ctx:
        def sb(name, shape, dt=F32):
            return ctx.enter_context(nc.sbuf_tensor(name, shape, dt))

        sems = {}

        def sem(name):
            if name not in sems:
                sems[name] = ctx.enter_context(nc.semaphore(name))
            return sems[name]

        ps = ctx.enter_context(nc.psum_tensor("ps", [P, 8, 512], F32))

        cst = sb("cst", [P, CONST_W])
        par = sb("par", [P, PARAM_W])
        x = sb("x", [P, D])
        ctxN = sb("ctxN", [P, KT * D])
        ctxT_hi = sb("ctxT_hi", [P, NK], F32R)
        ctxT_lo = sb("ctxT_lo", [P, NK], F32R)
        maskb = sb("maskb", [P, NK], BF16)
        ctxN_parts = ctxN[:].bitcast(F16)
        scale_diag = maskb[:, 0:2 * D].bitcast(F32)
        scale_rows = maskb[:, 2 * D:4 * D].bitcast(F32)
        scaled = maskb[:, CK:3 * CK].bitcast(F32)
        ch_amax = sb("ch_amax", [P, CH + 1])
        ch_scale = sb("ch_scale", [P, 1])
        ch_back = sb("ch_back", [P, 1])
        wq = sb("wq", [P, H * DK])
        wkT = sb("wkT", [P, PAIRS, D])
        wv = sb("wv", [P, H * DK])
        wo = sb("wo", [P, PAIRS, D])
        a_w = sb("a_w", [P, 4 * D])
        moe = sb("moe", [P, 3 * EXPERTS * FF])
        gateT, upT = moe[:, 0:EXPERTS * FF], moe[:, EXPERTS * FF:2 * EXPERTS * FF]
        downT = moe[:, 2 * EXPERTS * FF:].rearrange("p (f d) -> p f d", d=D)
        ctxT_raw = moe[:, 0:NK]
        mask_raw = moe[:, NK:NK + MASK_SLOTS * CK].bitcast(I32)
        d_w = sb("d_w", [P, 5 * D])
        w1s = sb("w1s", [16, D])
        win = sb("win", [P, FT, D])
        wout = sb("wout", [P, FT, D])

        def C(name, rows=slice(0, P)):
            return cst[rows, CONST[name][0]:CONST[name][1]]

        def W(name, rows=slice(0, P)):
            return par[rows, PARAM[name][0]:PARAM[name][1]]

        ident = C("ident")

        regions = [[moe, EXPERTS * FF, 3 * EXPERTS * FF]]

        def late(rows, *shape):
            n = int(np.prod(shape))
            region = next(g for g in regions if g[2] - g[1] >= n)
            v = region[0][0:rows, region[1]:region[1] + n]
            region[1] += n
            return v.rearrange("p (a b) -> p a b", a=shape[0]) if len(shape) > 1 else v

        stats6 = sb("stats6", [P, 6])
        mv = sb("mv", [P, 2])
        veps = sb("veps", [P, 1])
        rstd = sb("rstd", [P, 1])
        xn = sb("xn", [P, D])
        xnT = sb("xnT", [P, P])
        GT_hi = sb("GT_hi", [P, RT, P], F32R)
        GT_lo = sb("GT_lo", [P, RT, P], F32R)
        probs = sb("probs", [P, 2, CK])
        probsT = sb("probsT", [P, 2, CK])
        probsT_parts = probsT[:].rearrange("p b k -> p (b k)").bitcast(F16).rearrange("p (b h k) -> p b h k", b=2, h=2)
        rowmax = sb("rowmax", [P, 2])
        negmax = sb("negmax", [P, (CH + 1) * RT])
        alpha = sb("alpha", [P, CH * RT])
        chunksum = sb("chunksum", [P, CH * RT])
        den = sb("den", [P, RT])
        rden = sb("rden", [P, RT])
        U = sb("U", [P, RT, D])
        GT = U
        UT = sb("UT", [P, RT, P])
        OT = sb("OT", [P, PAIRS, 2, S])
        QT = OT[:, 0:4, :, :].rearrange("p j a s -> p (j a) s")
        qk = probsT[:, 1, 0:2 * D]
        vblk = sb("vblk", [P, PAIRS, 2, AD])
        aqT = probsT[:, 1, 2 * D:3 * D]
        kexp = UT[:].rearrange("p r (a t) -> p (r a) t", a=2)
        sm = probs[:, 0, 0:8 * S].rearrange("p (h t) -> p h t", h=8)
        sm2 = probs[:, 1, 0:8 * S].rearrange("p (h t) -> p h t", h=8)
        smx = sb("smx", [P, 8])
        ssum = sb("ssum", [P, 8])
        PT = probsT[:, 0, 0:4 * P].rearrange("p (j c) -> p j c", j=4)
        rot1 = PT[:, 0:2, :].rearrange("p a b -> p (a b)")
        rot2 = PT[:, 2:4, :].rearrange("p a b -> p (a b)")
        o_s = sb("o_s", [S, D])
        oT = sb("oT", [P, 2, S])
        nlog = sb("nlog", [P, 1])
        eprob = sb("eprob", [P, EXPERTS])
        top8 = sb("top8", [P, 8])
        topi = sb("topi", [P, 8], U32)
        topf = sb("topf", [P, 8])
        chosen = sb("chosen", [P, 2, EXPERTS])
        rt16 = sb("rt16", [P, 2 * EXPERTS])
        pairsum = sb("pairsum", [P, 2])
        meanw = sb("meanw", [P, EXPERTS])
        coef = sb("coef", [P, EXPERTS])
        share = sb("share", [P, 3, EXPERTS])
        sg = probs[:, :, 0:FT * S]
        hT = probsT[:, :, 0:FT * P].rearrange("p b (f a s) -> p b f a s", f=FT, a=2)
        o1 = late(P, D)
        o1T = late(P, P)
        qkv_pad = [sb(f"pad{i}", [P, TAPS - 1 + S]) for i in range(3)]
        cv = late(P, 3, S)
        vpad = sb("vpad", [P, FIR_L - 1 + S])
        qkc = late(P, 2, S)
        sq = late(P, 2 * S)
        nrm = late(P, 2 * S)
        rn = late(P, 2, S)
        qkh = late(P, 2, S)
        eb = late(P, S)
        beta = late(P, S)
        kbneg = late(P, S)
        R = late(P, S)
        Z = ctxN[:, 0:S * S].rearrange("p (g c) -> p g c", g=8)
        firp = gateT[:, 0:S * FIR_L].rearrange("p (t k) -> p t k", t=S)
        loc = late(P, 2, S)
        qexp = late(P, DH, S)
        Bm = late(S, DH, S)
        u_s = late(S, D)
        br = late(S, 4, D)
        cen = late(S, 4, D)
        st = sb("st", [S, DH, 4, 4])
        mom = sb("mom", [S, 3, 16])
        statsT = late(16, DH, S)
        hg = late(P, DH, S)
        gsm = sb("gsm", [S, DH, 4])
        gmx = sb("gmx", [S, 2, DH])
        tmpp = sb("tmpp", [P, 4])
        rtemp = sb("rtemp", [P, 1])
        sres = sb("sres", [P, 3, DH])
        prod = late(S, 4, D)
        om = late(S, D)
        osq = late(S, D)
        oms = sb("oms", [S, DH])
        orn = sb("orn", [S, DH])
        pows = sb("pows", [S, DH])
        wamx = sb("wamx", [P, 2 * FT])
        wsc = sb("wsc", [P, 2, 2 * FT])
        wqi = late(P, FT, D)
        wqo = late(P, FT, D)
        winq = late(P, FT, P)
        amx = sb("amx", [P, 1])
        amxr = sb("amxr", [1, 1])
        qs = sb("qs", [P, 3])
        xq = late(P, P)
        hid = late(P, FT, S)
        out_s = late(S, D)

        block = ctx.enter_context(nc.Block())

        DMAS = {"x": 1, "cst": 1, "par": 1, "in0": 2, "out0": 2, "in1": 2, "out1": 2, "small_attn": 1, "experts": 3,
                "delta": 2, "ffn": 2}

        def loaded(eng, *names):
            for name in names:
                eng.wait_ge(sem("ld_" + name), 16 * DMAS[name])

        @block.sync
        def _(sp):
            def load(name, dst, src):
                sp.dma_start(dst, dram[src]).then_inc(sem("ld_" + name), 16)

            load("x", x[:], "x")
            load("cst", cst[:], "cst")
            for c in range(CH):
                keys, slot = slice(c * CK, (c + 1) * CK), c % MASK_SLOTS
                landed = sem(f"ld_chunk{c}")
                sp.dma_start(ctxT_raw[:, keys], dram["ctxT"][:, keys]).then_inc(landed, 16)
                if c >= MASK_SLOTS:
                    sp.wait_ge(sem("mask_ready"), c - MASK_SLOTS + 1)
                for a in range(2):
                    sp.dma_start(mask_raw[a * S:(a + 1) * S, slot * CK:(slot + 1) * CK],
                                 dram["mask"][:, keys]).then_inc(landed, 16)
                sp.dma_start(ctxN[:, keys], dram["ctxN"][:, keys]).then_inc(landed, 16)
                if c == 0:
                    load("par", par[:], "par")
            for name, t, src in (("out0", wv, "wv0"), ("out0", wo, "wo0"), ("ffn", win, "win"), ("ffn", wout, "wout"),
                                 ("small_attn", a_w, "a_w"), ("delta", d_w, "d_w"), ("delta", w1s, "w1s")):
                load(name, t[:], src)
            sp.wait_ge(sem("ctxT_ready"), CH)
            sp.wait_ge(sem("mask_ready"), CH)
            load("experts", gateT, "gateT")
            load("experts", upT, "upT")
            load("experts", downT, "downT")
            sp.wait_ge(sem("g_ready"), 1)
            load("in1", wq[:], "wq1")
            load("in1", wkT[:], "wkT1")
            sp.wait_ge(sem("y_ready"), 1)
            load("out1", wv[:], "wv1")
            load("out1", wo[:], "wo1")
            sp.wait_ge(sem("result"), 1)
            sp.dma_start(dram["out"], out_s).then_inc(sem("stored"), 16)
            sp.wait_ge(sem("stored"), 16)

        def flash_pe(pe, L):
            base = L * CH * RT
            scores_ready, exp_done = sem("scores_ready"), sem("exp_done")
            turned = [sem("turned_lo"), sem("turned_hi")]
            copied = [sem("copied_lo"), sem("copied_hi")]
            pv_done, u_added = sem("pv_done"), sem("u_added")

            def scores(c, r):
                n, b, first = c * RT + r, r % 2, isinstance(c, int) and c == 0
                if not (first and r < 2):
                    pe.wait_ge(exp_done if L else sem("masked"), base + n - 1)
                if first and r == RT // 2:
                    pe.wait_ge(sem("g_copied"), 3 * L + 3)
                if r == 0 and L == 0:
                    pe.wait_ge(sem("ctxT_ready"), c + 1)
                for h in range(2):
                    out = ps[:, 2 * b + h, 0:HALF]
                    keys = bass.ds(c * CK + h * HALF, HALF)
                    pe.matmul(out, GT_hi[:, r, :], ctxT_hi[:, keys], start=True, stop=False)
                    pe.matmul(out, GT_hi[:, r, :], ctxT_lo[:, keys], start=False, stop=False)
                    ins = pe.matmul(out, GT_lo[:, r, :], ctxT_hi[:, keys], start=False, stop=True)
                ins.then_inc(scores_ready, 1)

            def turn(c, r):
                n, b, first = c * RT + r, r % 2, isinstance(c, int) and c == 0
                pe.wait_ge(exp_done, base + n + 1)
                for part, tiles in enumerate((range(0, 4), range(4, TC))):
                    if not (first and r == 0):
                        pe.wait_ge(copied[part], base + n)
                    for k in tiles:
                        ins = pe.transpose(ps[:, 4 + part, (k % 4) * P:(k % 4 + 1) * P],
                                           probs[:, b, k * P:(k + 1) * P], ident)
                    ins.then_inc(turned[part], 1)

            def pv(c, r):
                n, b, first = c * RT + r, r % 2, isinstance(c, int) and c == 0
                if L == 1:
                    pe.wait_ge(sem("uppers"), 2 * n + 2)
                    if first and r == 0:
                        pe.wait_ge(sem("ctx_parts"), CH)
                    if not (first and r < 2):
                        pe.wait_ge(u_added, base + n - 1)
                    parts = ctxN_parts[:, bass.ds(2 * c * CK, 2 * CK)]
                    for p_part, c_part in ((0, 0), (0, 1), (1, 0)):
                        if p_part == 1:
                            pe.wait_ge(copied[0], base + n + 1)
                            pe.wait_ge(copied[1], base + n + 1)
                        for k in range(TC):
                            ins = pe.matmul(ps[:, 6 + b, 0:D], probsT_parts[:, b, p_part, k * P:(k + 1) * P],
                                            parts[:, c_part * CK + k * D:c_part * CK + (k + 1) * D],
                                            start=(c_part == 0 and p_part == 0 and k == 0),
                                            stop=(p_part == 1 and k == TC - 1))
                    ins.then_inc(pv_done, 1)
                    return
                pe.wait_ge(copied[0], base + n + 1)
                pe.wait_ge(copied[1], base + n + 1)
                if not (first and r < 2):
                    pe.wait_ge(u_added, base + n - 1)
                if L == 0 and isinstance(n, int) and n == SCALE_STEP:
                    pe.wait_ge(sem("scale_diag"), 1)
                    pe.matmul(ps[:, 6 + b, D:2 * D], C("ones"), scale_diag, start=True, stop=True)
                for k in range(TC):
                    ins = pe.matmul(ps[:, 6 + b, 0:D], probsT[:, b, k * P:(k + 1) * P],
                                    ctxN[:, bass.ds((c * TC + k) * D, D)], start=(k == 0), stop=(k == TC - 1))
                ins.then_inc(pv_done, 1)

            def chunk(c, last=False):
                for r in range(RT):
                    if r < RT - 2:
                        scores(c, r + 2)
                    elif not last:
                        scores(c + 1, r + 2 - RT)
                    pv(c, r)
                    if r < RT - 1:
                        turn(c, r + 1)
                    elif not last:
                        turn(c + 1, 0)

            scores(0, 0)
            scores(0, 1)
            turn(0, 0)
            chunk(0)
            with pe.Fori(1, CH - 1) as c:
                chunk(c)
            chunk(CH - 1, last=True)

        def flash_act(act, L):
            base = L * CH * RT
            nm_ready, exp_done = sem("negmax_ready"), sem("exp_done")
            turned, copied, pv_done = sem("turned_lo"), sem("copied_lo"), sem("pv_done")

            def exps(c, r):
                n, b, first = c * RT + r, r % 2, isinstance(c, int) and c == 0
                act.wait_ge(nm_ready, base + n + 1)
                new = negmax[:, bass.ds(n + RT, 1)]
                act.activation(alpha[:, bass.ds(n, 1)], negmax[:, bass.ds(n, 1)], ACT.Exp, bias=new, scale=-1.0)
                pr = probs[:, b, :].rearrange("p (h k) -> p h k", h=2)
                if L and not (first and r < 2):
                    act.wait_ge(sem("turned_hi"), base + n - 1)
                act.activation(pr, ps[:, 2 * b:2 * b + 2, 0:HALF] if L else pr, ACT.Exp, bias=new, scale=DK ** -0.5,
                               accum_out=chunksum[:, bass.ds(n, 1)]).then_inc(exp_done, 1)

            def copy_lo(c, r):
                n, b, first = c * RT + r, r % 2, isinstance(c, int) and c == 0
                act.wait_ge(turned, base + n + 1)
                if not (first and r < 2):
                    act.wait_ge(pv_done, base + n - 1)
                if L == 1:
                    act.activation(probsT_parts[:, b, 0, 0:4 * P], ps[:, 4, :], ACT.Copy,
                                   scale=HALF_SCALE).then_inc(sem("uppers"), 1)
                    act.wait_ge(sem("turned_hi"), base + n + 1)
                    act.activation(probsT_parts[:, b, 0, 4 * P:CK], ps[:, 5, 0:(TC - 4) * P], ACT.Copy,
                                   scale=HALF_SCALE).then_inc(sem("uppers"), 1)
                    return
                act.copy(probsT[:, b, 0:4 * P], ps[:, 4, :]).then_inc(copied, 1)
                if L == 0:
                    act.wait_ge(sem("turned_hi"), base + n + 1)
                    act.copy(probsT[:, b, 4 * P:CK], ps[:, 5, 0:(TC - 4) * P]).then_inc(sem("copied_hi"), 1)

            def chunk(c, last=False):
                for r in range(RT):
                    copy_lo(c, r)
                    if r < RT - 1:
                        exps(c, r + 1)
                    elif not last:
                        exps(c + 1, 0)

            exps(0, 0)
            chunk(0)
            with act.Fori(1, CH - 1) as c:
                chunk(c)
            chunk(CH - 1, last=True)

        def flash_dve(dve, L):
            base = L * CH * RT
            scores_ready, nm_ready, rowmax_ready = sem("scores_ready"), sem("negmax_ready"), sem("rowmax")
            copied = [sem("copied_lo"), sem("copied_hi")]
            pv_done, u_added, den_added = sem("pv_done"), sem("u_added"), sem("den_added")

            def maximum(c, r):
                n, b, first = c * RT + r, r % 2, isinstance(c, int) and c == 0
                dve.wait_ge(scores_ready, base + n + 1)
                src = ps[:, 2 * b:2 * b + 2, 0:HALF]
                if L == 0:
                    if r == 0:
                        dve.wait_ge(sem("mask_ready"), c + 1)
                    if not (first and r < 2):
                        dve.wait_ge(sem("turned_hi"), base + n - 1)
                    masked = probs[:, b, :].rearrange("p (h k) -> p h k", h=2)
                    dve.tensor_tensor(masked, src, maskb[:, bass.ds(c * CK, CK)].rearrange("p (h k) -> p h k", h=2),
                                      ALU.add).then_inc(sem("masked"), 1)
                    dve.wait_ge(sem("masked"), base + n + 1)
                    src = masked
                dve.tensor_reduce(rowmax[:, b:b + 1], src, mybir.AxisListType.XY,
                                  ALU.max).then_inc(rowmax_ready, 1)
                dve.wait_ge(rowmax_ready, base + n + 1)
                dve.tensor_scalar(negmax[:, bass.ds(n + RT, 1)], rowmax[:, b:b + 1], -(DK ** -0.5),
                                  negmax[:, bass.ds(n, 1)], ALU.mult, ALU.min).then_inc(nm_ready, 1)

            def add(c, r):
                n, b, first = c * RT + r, r % 2, isinstance(c, int) and c == 0
                dve.wait_ge(sem("exp_done"), base + n + 1)
                if not first:
                    dve.wait_ge(den_added, base + n - RT + 1)
                dve.scalar_tensor_tensor(den[:, r:r + 1], den[:, r:r + 1], alpha[:, bass.ds(n, 1)],
                                         chunksum[:, bass.ds(n, 1)], ALU.mult, ALU.add).then_inc(den_added, 1)
                dve.wait_ge(pv_done, base + n + 1)
                if L == 0 and isinstance(n, int) and n == SCALE_STEP:
                    dve.tensor_copy(scale_rows, ps[:, 6 + b, D:2 * D]).then_inc(sem("scale_rows"), 1)
                if not first:
                    dve.wait_ge(u_added, base + n - RT + 1)
                dve.scalar_tensor_tensor(U[:, r, :], U[:, r, :], alpha[:, bass.ds(n, 1)],
                                         ps[:, 6 + b, 0:D], ALU.mult, ALU.add).then_inc(u_added, 1)

            def scale(r):
                dve.wait_ge(den_added, base + (CH - 1) * RT + r + 1)
                dve.reciprocal(rden[:, r:r + 1], den[:, r:r + 1]).then_inc(sem("den_inverted"), 1)
                dve.wait_ge(u_added, base + (CH - 1) * RT + r + 1)
                dve.wait_ge(sem("den_inverted"), L * RT + r + 1)
                dve.tensor_scalar(U[:, r, :], U[:, r, :], rden[:, r:r + 1], None, ALU.mult).then_inc(
                    sem("u_scaled"), 1)

            def lowers(c, r):
                n, b = c * RT + r, r % 2
                for part, (a, w) in enumerate(((0, 4 * P), (4 * P, CK - 4 * P))):
                    dve.wait_ge(sem("uppers"), 2 * n + part + 1)
                    dve.scalar_tensor_tensor(probsT_parts[:, b, 1, a:a + w], ps[:, 4 + part, 0:w], HALF_SCALE,
                                             probsT_parts[:, b, 0, a:a + w], ALU.mult,
                                             ALU.subtract).then_inc(copied[part], 1)

            def chunk(c, first=False, last=False):
                for r in range(RT):
                    if r < RT - 1:
                        maximum(c, r + 1)
                    elif not last:
                        maximum(c + 1, 0)
                    if r > 0:
                        add(c, r - 1)
                    elif not first:
                        add(c - 1, RT - 1)
                    if L == 1:
                        lowers(c, r)
                    elif r == 1 and not last:
                        channel_max(c + 1)
                    elif r == 4 and first:
                        channel_max(0)
                    elif r == 0 and last:
                        channel_scales()
                    if last and r > 0:
                        scale(r - 1)

            def channel_max(c):
                dve.wait_ge(sem("ctxT_ready"), c + 1)
                dve.tensor_reduce(ch_amax[:, bass.ds(c, 1)], ctxT_hi[:, bass.ds(c * CK, CK)].bitcast(F32), AX,
                                  ALU.max, apply_absolute_value=True).then_inc(sem("ch_max"), 1)

            def channel_scales():
                whole = ch_amax[:, CH:CH + 1]
                steps = iter(range(CH + 1, CH + 6))
                dve.wait_ge(sem("ch_max"), CH)
                dve.tensor_reduce(whole, ch_amax[:, 0:CH], AX, ALU.max).then_inc(sem("ch_max"), 1)
                dve.wait_ge(sem("ch_max"), next(steps))
                dve.tensor_scalar(whole, whole, 1e-20, None, ALU.max).then_inc(sem("ch_max"), 1)
                dve.wait_ge(sem("ch_max"), next(steps))
                dve.tensor_scalar(whole.bitcast(I32), whole.bitcast(I32), 0x7F800000, None,
                                  ALU.bitwise_and).then_inc(sem("ch_max"), 1)
                dve.wait_ge(sem("ch_max"), next(steps))
                dve.reciprocal(ch_scale[:], whole).then_inc(sem("ch_max"), 1)
                dve.tensor_scalar(ch_back[:], whole, 1.0 / (CTX_SCALE * HALF_SCALE), None,
                                  ALU.mult).then_inc(sem("ch_back"), 1)
                dve.wait_ge(sem("ch_max"), next(steps))
                dve.tensor_scalar(ch_scale[:], ch_scale[:], CTX_SCALE, None, ALU.mult).then_inc(sem("ch_scale"), 1)

            maximum(0, 0)
            chunk(0, first=True)
            with dve.Fori(1, CH - 1) as c:
                chunk(c)
            chunk(CH - 1, last=True)
            add(CH - 1, RT - 1)
            scale(RT - 1)

        def norm_dve(dve, seq, i):
            seq(dve.bn_stats(stats6[:], x[:]))
            seq(dve.bn_aggr(mv[:], stats6[:]))
            dve.tensor_scalar(veps[:], mv[:, 1:2], LN_EPS, None, ALU.add).then_inc(sem("ln_var"), 1)
            dve.wait_ge(sem("ln_rstd"), i + 1)
            dve.tensor_scalar(xn[:], x[:], mv[:, 0:1], rstd[:], ALU.subtract, ALU.mult).then_inc(sem("ln_xn"), 1)
            dve.wait_ge(sem("ln_turned"), i + 1)
            dve.tensor_copy(xnT[:], ps[:, 7, 0:P]).then_inc(sem("ln_xnT"), 1)
            dve.wait_ge(sem("ln_xnT"), i + 1)

        def norm_pool(pool, i):
            pool.wait_ge(sem("ln_var"), i + 1)
            pool.tensor_tensor(rstd[:], veps[:], C("power"), ALU.pow).then_inc(sem("ln_rstd"), 1)

        def stay_warm(pe, bank, k):
            for _ in range(k):
                pe.matmul(ps[:, bank, 0:P], ident, ident, start=True, stop=True)

        def norm_pe(pe, i):
            if i:
                stay_warm(pe, 2, WARM[i])
            pe.wait_ge(sem("ln_xn"), i + 1)
            pe.transpose(ps[:, 7, 0:P], xn[:], ident).then_inc(sem("ln_turned"), 1)
            stay_warm(pe, 2, 2)

        def fold_q_pe(pe, L, i, src):
            for j in range(PAIRS):
                ins = pe.matmul(ps[:, 0, j * S:(j + 1) * S], wq[:, j * P:(j + 1) * P], src[:, 0:S],
                                start=True, stop=True)
            ins.then_inc(sem("q_ready"), 1)
            stay_warm(pe, 6, 5)
            pe.wait_ge(sem("q_copied"), i + 1)
            for j in range(PAIRS):
                for par_ in range(2):
                    rows = slice(par_ * DK, (par_ + 1) * DK)
                    ins = pe.matmul(ps[:, 4 + par_, j * S:(j + 1) * S], wkT[rows, j, :], QT[rows, j, :],
                                    start=True, stop=True)
            ins.then_inc(sem("g_ready"), 1)

        def fold_q_dve(dve, seq, i):
            dve.wait_ge(sem("q_ready"), i + 1)
            dve.tensor_copy(QT.rearrange("p j s -> p (j s)"), ps[:, 0, :]).then_inc(sem("q_copied"), 1)
            if i == 0:
                dve.wait_ge(sem("ld_chunk0"), 4 * 16)
                dve.tensor_copy(ctxT_hi[:, 0:CK], ctxT_raw[:, 0:CK]).then_inc(sem("ctxT_upper"), 1)
                dve.tensor_scalar(maskb[:, 0:CK], mask_raw[:, 0:CK], 0.0, MASKED, ALU.is_equal,
                                  ALU.mult).then_inc(sem("mask_ready"), 1)
                dve.wait_ge(sem("ctxT_upper"), 1)
                dve.tensor_tensor(ctxT_lo[:, 0:CK], ctxT_raw[:, 0:CK], ctxT_hi[:, 0:CK].bitcast(F32),
                                  ALU.subtract).then_inc(sem("ctxT_ready"), 1)
            dve.wait_ge(sem("g_ready"), i + 1)
            if i == 2:
                dve.tensor_copy(GT[:, 0:4, :].rearrange("p r c -> p (r c)"), ps[:, 4, :]).then_inc(
                    sem("g_copied"), 1)
                return
            seq(dve.tensor_copy(GT_hi[:, 0:4, :].rearrange("p r c -> p (r c)"), ps[:, 4, :]))
            for half in range(2):
                if half == 1:
                    dve.wait_ge(sem("g_copied"), 3 * i + 2)
                hi = GT_hi[:, 4 * half:4 * half + 4, :].rearrange("p r c -> p (r c)").bitcast(F32)
                dve.tensor_tensor(GT_lo[:, 4 * half:4 * half + 4, :].rearrange("p r c -> p (r c)"),
                                  ps[:, 4 + half, :], hi, ALU.subtract).then_inc(sem("g_copied"), 1)

        def fold_q_act(act, i):
            act.wait_ge(sem("g_ready"), i + 1)
            act.copy((GT if i == 2 else GT_hi)[:, 4:8, :].rearrange("p r c -> p (r c)"), ps[:, 5, :]).then_inc(
                sem("g_copied"), 1)

        def project_pe(pe, L, i):
            stay_warm(pe, 6, 4)
            pe.wait_ge(sem("ut_copied"), 2 * i + 2)
            for j in range(PAIRS):
                for par_ in range(2):
                    h, g = 2 * j + par_, par_ * PAIRS + j
                    ins = pe.matmul(ps[par_ * DK:(par_ + 1) * DK, 2, j * S:(j + 1) * S],
                                    wv[:, h * DK:(h + 1) * DK], UT[:, g // 2, (g % 2) * S:(g % 2 + 1) * S],
                                    start=True, stop=True)
            ins.then_inc(sem("o_ready"), 1)
            stay_warm(pe, 6, 4)
            for j in range(PAIRS):
                if j % (PAIRS // 2) == 0:
                    pe.wait_ge(sem("o_copied"), 2 * i + 1 + j // (PAIRS // 2))
                ins = pe.matmul(ps[:, 3, 0:D], OT[:, j, :, :].rearrange("p a s -> p (a s)"), wo[:, j, :],
                                start=(j == 0), stop=(j == PAIRS - 1))
            ins.then_inc(sem("y_ready"), 1)

        def project_dve(dve, i):
            dve.wait_ge(sem("o_ready"), i + 1)
            for part in range(2):
                js = slice(part * PAIRS // 2, (part + 1) * PAIRS // 2)
                dve.tensor_copy(OT[:, js, :, :], ps[:, 2, :].rearrange("p (j s) -> p j s", j=PAIRS)[:, js, :]
                                .unsqueeze(2).broadcast_to([P, PAIRS // 2, 2, S])).then_inc(sem("o_copied"), 1)
            dve.wait_ge(sem("y_ready"), i + 1)

        def turn_u_pe(pe, L):
            for r in range(RT):
                pe.wait_ge(sem("u_scaled"), L * RT + r + 1)
                ins = pe.transpose(ps[:, r // 4, (r % 4) * P:(r % 4 + 1) * P], U[:, r, :], ident)
                if r % 4 == 3:
                    ins.then_inc(sem("u_turned"), 1)

        def turn_u_dve(dve, seq, L):
            dve.wait_ge(sem("u_turned"), 2 * L + 1)
            ut, src = UT[:, 0:4, :].rearrange("p r c -> p (r c)"), ps[:, 0, :]
            if L == 1:
                dve.tensor_scalar(ut, src, ch_back[:], None, ALU.mult).then_inc(sem("ut_copied"), 1)
            else:
                dve.tensor_copy(ut, src).then_inc(sem("ut_copied"), 1)

        def turn_u_act(act, L):
            act.wait_ge(sem("u_turned"), 2 * L + 2)
            ut, src = UT[:, 4:8, :].rearrange("p r c -> p (r c)"), ps[:, 1, :]
            if L == 1:
                act.activation(ut, src, ACT.Copy, scale=ch_back[:]).then_inc(sem("ut_copied"), 1)
            else:
                act.copy(ut, src).then_inc(sem("ut_copied"), 1)

        @block.tensor
        def _(pe):
            pe.wait_ge(sem("cleared"), 2)
            for _ in range(12):
                pe.matmul(ps[:, 6, 0:P], U[:, 0, :], U[:, 0, :], start=True, stop=True)
            loaded(pe, "cst", "in0")
            norm_pe(pe, 0)
            pe.wait_ge(sem("ln_xnT"), 1)
            fold_q_pe(pe, 0, 0, xnT)
            stay_warm(pe, 6, 8)
            pe.wait_ge(sem("g_copied"), 2)
            flash_pe(pe, 0)
            turn_u_pe(pe, 0)
            loaded(pe, "out0")
            project_pe(pe, 0, 0)

            norm_pe(pe, 1)
            pe.wait_ge(sem("ln_xnT"), 2)
            loaded(pe, "small_attn")
            pe.matmul(ps[:, 0, 0:2 * D], xnT[:], a_w[:, 0:2 * D], start=True, stop=True)
            pe.matmul(ps[:, 1, 0:D], xnT[:], a_w[:, 2 * D:3 * D], start=True, stop=True).then_inc(sem("a_qkv"), 1)
            stay_warm(pe, 6, 6)
            pe.wait_ge(sem("a_rotated"), 1)
            pe.transpose(ps[:, 2, 0:P], qk[:, 0:D], ident)
            pe.transpose(ps[:, 2, P:2 * P], qk[:, D:2 * D], ident).then_inc(sem("a_turned"), 1)
            stay_warm(pe, 6, 6)
            pe.wait_ge(sem("a_kexp"), 1)
            for hh in range(2):
                ins = pe.matmul(ps[hh * S:(hh + 1) * S, 3, :], aqT[:, hh * S:(hh + 1) * S],
                                kexp[:, 8 * hh:8 * hh + 8, :], start=True, stop=True)
            ins.then_inc(sem("a_scores"), 1)
            stay_warm(pe, 6, 18)
            pe.wait_ge(sem("a_probs"), 1)
            for j in range(4):
                ins = pe.transpose(ps[:, 4, j * P:(j + 1) * P], sm[:, 2 * j:2 * j + 2, :].rearrange("p a t -> p (a t)"),
                                   ident)
            ins.then_inc(sem("a_pturned"), 1)
            stay_warm(pe, 6, 4)
            pe.wait_ge(sem("a_pcopied"), 1)
            for hh in range(2):
                for j in range(4):
                    pr = 4 * hh + j
                    ins = pe.matmul(ps[0:S, 5, pr * 16:(pr + 1) * 16], PT[:, j, hh * S:(hh + 1) * S],
                                    vblk[:, pr, :, :].rearrange("p a d -> p (a d)"), start=True, stop=True)
            ins.then_inc(sem("a_out"), 1)
            pe.wait_ge(sem("a_ocopied"), 1)
            pe.transpose(ps[:, 6, 0:S], o_s[:], C("ident", slice(0, S))[:, 0:S]).then_inc(sem("a_oturned"), 1)
            pe.wait_ge(sem("a_oT"), 1)
            pe.matmul(ps[:, 5, 128:256], oT[:].rearrange("p a s -> p (a s)"), a_w[:, 3 * D:4 * D],
                      start=True, stop=True).then_inc(sem("a_y"), 1)

            norm_pe(pe, 2)
            pe.wait_ge(sem("ln_xnT"), 3)
            loaded(pe, "par", "experts")
            pe.matmul(ps[:, 0, 0:EXPERTS], xnT[:], W("router"), start=True, stop=True).then_inc(sem("m_logits"), 1)

            def gate_up(e):
                b = e % 2
                if e >= 2:
                    pe.wait_ge(sem("m_h"), e - 1)
                for w, bank in ((gateT, 2 + b), (upT, 4 + b)):
                    for f in range(FT):
                        ins = pe.matmul(ps[:, bank, f * S:(f + 1) * S], w[:, (e * FT + f) * P:(e * FT + f + 1) * P],
                                        xnT[:, 0:S], start=True, stop=True)
                    ins.then_inc(sem("m_gate" if bank < 4 else "m_up"), 1)

            def down(e):
                pe.wait_ge(sem("m_h"), e + 1)
                for f in range(FT):
                    ins = pe.matmul(ps[:, DOWN_AT[e][0], DOWN_AT[e][1]:DOWN_AT[e][1] + D],
                                    hT[:, e % 2, f, :, :].rearrange("p a s -> p (a s)"), downT[:, e * FT + f, :],
                                    start=(f == 0), stop=(f == FT - 1))
                ins.then_inc(sem("m_down"), 1)

            gate_up(0)
            gate_up(1)
            pe.wait_ge(sem("m_chosen"), 1)
            pe.matmul(ps[:, 1, 0:2 * EXPERTS], C("ones", slice(0, S)), rt16[0:S, :], start=True,
                      stop=True).then_inc(sem("m_counts"), 1)
            for e in range(2, EXPERTS):
                down(e - 2)
                gate_up(e)
            down(EXPERTS - 2)
            down(EXPERTS - 1)

            norm_pe(pe, 3)
            pe.wait_ge(sem("ln_xnT"), 4)
            loaded(pe, "in1")
            fold_q_pe(pe, 1, 1, xnT)
            stay_warm(pe, 6, 8)
            pe.wait_ge(sem("g_copied"), 5)
            flash_pe(pe, 1)
            turn_u_pe(pe, 1)
            loaded(pe, "out1")
            project_pe(pe, 1, 1)
            stay_warm(pe, 6, 3)
            pe.wait_ge(sem("o1_ready"), 1)
            pe.transpose(ps[:, 7, 0:P], o1, ident).then_inc(sem("o1_turned"), 1)
            stay_warm(pe, 6, 2)
            pe.wait_ge(sem("o1T_ready"), 1)
            fold_q_pe(pe, 1, 2, o1T)
            stay_warm(pe, 6, 4)
            pe.wait_ge(sem("g_copied"), 8)
            for r in range(RT):
                ins = pe.matmul(ps[:, 3, r * S:(r + 1) * S], GT[:, r, :], o1T[:, 0:S], start=True, stop=True)
            ins.then_inc(sem("b_scores"), 1)
            pe.wait_ge(sem("f_wq"), 2)
            for f in range(FT):
                ins = pe.transpose(ps[:, 5, f * P:(f + 1) * P], wqi[:, f, :], ident)
            ins.then_inc(sem("f_wturned"), 1)
            stay_warm(pe, 6, 14)
            pe.wait_ge(sem("b_probs"), 1)
            pe.wait_ge(sem("f_wcopied"), 1)
            for j in range(4):
                ins = pe.transpose(ps[:, 4, j * P:(j + 1) * P], sm[:, 2 * j:2 * j + 2, :].rearrange("p a t -> p (a t)"),
                                   ident)
            ins.then_inc(sem("b_pturned"), 1)
            stay_warm(pe, 6, 4)
            pe.wait_ge(sem("b_pcopied"), 1)
            for jj in range(2):
                rows = slice(jj * S, (jj + 1) * S)
                pe.matmul(ps[:, jj, :], xn[rows, :], PT[rows, :, :].rearrange("p j c -> p (j c)"), start=True,
                          stop=True).then_inc(sem("b_u"), 1)
            project_pe(pe, 1, 2)

            norm_pe(pe, 4)
            pe.wait_ge(sem("ln_xnT"), 5)
            loaded(pe, "delta")
            for i in range(3):
                ins = pe.matmul(ps[:, 0, i * S:(i + 1) * S], d_w[:, i * D:(i + 1) * D], xnT[:, 0:S],
                                start=True, stop=True)
            ins.then_inc(sem("d_qkv"), 1)
            pe.matmul(ps[:, 1, 0:S], W("wb"), xnT[:, 0:S], start=True, stop=True).then_inc(sem("d_beta"), 1)
            pe.wait_ge(sem("d_sq"), 1)
            pe.matmul(ps[:, 2, 0:2 * S], C("block32"), sq, start=True, stop=True).then_inc(sem("d_norm"), 1)
            for g in range(8):
                pe.wait_ge(sem("d_z"), g + 1)
                w = S - 8 * g
                pe.matmul(ps[:, g, 0:8 * w], C("block32"), Z[:, g, 0:8 * w], start=True,
                          stop=True).then_inc(sem("d_a"), 1)
            pe.wait_ge(sem("d_subst"), S - 1)
            pe.matmul(ps[0:S, 0, 0:DH * S], qkh[:, 1, :], qexp.rearrange("p h t -> p (h t)"), start=True,
                      stop=True).then_inc(sem("d_b"), 1)
            pe.transpose(ps[0:S, 1, 0:D], R, ident).then_inc(sem("d_uturned"), 1)
            pe.wait_ge(sem("d_fir"), 1)
            for i, src in ((0, loc[:, 0, :]), (1, loc[:, 1, :]), (3, vpad[:, FIR_L - 1:])):
                ins = pe.transpose(ps[0:S, 2, i * D:(i + 1) * D], src, ident)
            pe.wait_ge(sem("d_bcopied"), 1)
            pe.wait_ge(sem("d_ucopied"), 1)
            for h in range(DH):
                ins = pe.matmul(ps[0:S, 2, 2 * D + h * DD:2 * D + (h + 1) * DD], Bm[:, h, :],
                                u_s[:, h * DD:(h + 1) * DD], start=True, stop=True)
            ins.then_inc(sem("d_branches"), 1)
            pe.wait_ge(sem("d_stats"), 1)
            for h in range(DH):
                ins = pe.transpose(ps[0:16, 3, h * S:(h + 1) * S], st[:, h, :, :].rearrange("p a b -> p (a b)"),
                                   C("ident", slice(0, S))[:, 0:S])
            ins.then_inc(sem("d_sturned"), 1)
            pe.matmul(ps[:, 4, 0:DH * S], d_w[:, 4 * D:5 * D], xnT[:, 0:S].unsqueeze(1).broadcast_to([P, DH, S]),
                      start=True, stop=False)
            pe.wait_ge(sem("d_scopied"), 1)
            pe.matmul(ps[:, 4, 0:DH * S], w1s[:], statsT.rearrange("p h t -> p (h t)"), start=False,
                      stop=True).then_inc(sem("d_hidden"), 1)
            pe.wait_ge(sem("d_gelu"), 1)
            for h in range(DH):
                ins = pe.matmul(ps[0:S, 5, 4 * h:4 * h + 4], hg[:, h, :], W("w2"), start=True, stop=True)
            ins.then_inc(sem("d_gate"), 1)
            pe.wait_ge(sem("d_mixed"), 1)
            pe.transpose(ps[:, 6, 0:S], om, C("ident", slice(0, S))[:, 0:S]).then_inc(sem("d_mturned"), 1)
            pe.wait_ge(sem("d_mcopied"), 1)
            pe.matmul(ps[:, 5, 128:256], oT[:].rearrange("p a s -> p (a s)"), d_w[:, 3 * D:4 * D],
                      start=True, stop=True).then_inc(sem("d_y"), 1)

            norm_pe(pe, 5)
            for i in range(2):
                pe.wait_ge(sem("f_amx"), i + 1)
                pe.transpose(ps[0:1, 1, 0:P], amx[:], ident).then_inc(sem("f_amxT"), 1)
                pe.wait_ge(sem("f_amxr"), i + 1)
                pe.matmul(ps[:, 2, 0:1], C("ones", slice(0, 1)), amxr[:], start=True,
                          stop=True).then_inc(sem("f_amxb"), 1)
                if i == 0:
                    pe.wait_ge(sem("f_xq"), 1)
                    for f in range(FT):
                        ins = pe.matmul(ps[:, 3, f * S:(f + 1) * S], winq[:, f, :], xq[:, 0:S], start=True, stop=True)
                    ins.then_inc(sem("f_hidden"), 1)
            pe.wait_ge(sem("f_hq"), 1)
            for f in range(FT):
                ins = pe.matmul(ps[0:S, 4, 0:D], hid[:, f, :], wqo[:, f, :], start=(f == 0), stop=(f == FT - 1))
            ins.then_inc(sem("f_y"), 1)

        @block.gpsimd
        def _(pool):
            steps = [0]

            def pseq(ins):
                steps[0] += 1
                ins.then_inc(sem("pool_step"), 1)
                pool.wait_ge(sem("pool_step"), steps[0])

            pool.memset(den[:], 0.0).then_inc(sem("cleared"), 1)
            pool.memset(U[:], 0.0).then_inc(sem("cleared"), 1)
            pool.memset(negmax[:, 0:RT], 3e38).then_inc(sem("cleared"), 1)
            for i in range(3):
                pool.memset(qkv_pad[i][:, 0:TAPS - 1], 0.0).then_inc(sem("pads"), 1)
            pool.memset(vpad[:, 0:FIR_L - 1], 0.0).then_inc(sem("pads"), 1)
            loaded(pool, "cst")
            norm_pool(pool, 0)
            for c in range(1, CH):
                keys, slot = slice(c * CK, (c + 1) * CK), c % MASK_SLOTS
                pool.wait_ge(sem(f"ld_chunk{c}"), 4 * 16)
                pool.wait_ge(sem("ctxT_ready"), c)
                pool.tensor_copy(ctxT_hi[:, keys], ctxT_raw[:, keys]).then_inc(sem("ctxT_upper"), 1)
                pool.wait_ge(sem("ctxT_upper"), c + 1)
                pool.tensor_tensor(ctxT_lo[:, keys], ctxT_raw[:, keys], ctxT_hi[:, keys].bitcast(F32),
                                   ALU.subtract).then_inc(sem("ctxT_ready"), 1)
                pool.wait_ge(sem("mask_ready"), c)
                pool.tensor_scalar(maskb[:, keys], mask_raw[:, slot * CK:(slot + 1) * CK], 0.0, MASKED,
                                   ALU.is_equal, ALU.mult).then_inc(sem("mask_ready"), 1)
            pool.wait_ge(sem("ch_scale"), 1)
            pool.wait_ge(sem("masked"), 3 * RT)
            pool.tensor_tensor(scale_diag, ident, ch_scale[:].broadcast_to([P, P]),
                               ALU.mult).then_inc(sem("scale_diag"), 1)

            def split_context(c):
                pool.wait_ge(sem("pv_done"), (c + 1) * RT)
                keys = slice(c * CK, (c + 1) * CK)
                pseq(pool.tensor_tensor(scaled.rearrange("p (k d) -> p k d", d=D),
                                        ctxN[:, keys].rearrange("p (k d) -> p k d", d=D),
                                        scale_rows.unsqueeze(1).broadcast_to([P, TC, D]), ALU.mult))
                upper, lower = (ctxN_parts[:, (2 * c + i) * CK:(2 * c + i + 1) * CK] for i in range(2))
                pseq(pool.tensor_copy(upper, scaled))
                pool.tensor_tensor(lower, scaled, upper, ALU.subtract).then_inc(sem("ctx_parts"), 1)
                pool.wait_ge(sem("ctx_parts"), c + 1)

            pool.wait_ge(sem("scale_rows"), 1)
            for c in range(2):
                split_context(c)
            for i in range(1, 5):
                if i == 2:
                    for c in range(2, 4):
                        split_context(c)
                if i == 3:
                    pool.wait_ge(sem("u_turned"), 2)
                    pool.memset(den[:], 0.0).then_inc(sem("cleared"), 1)
                    pool.memset(U[:], 0.0).then_inc(sem("cleared"), 1)
                norm_pool(pool, i)
                if i == 2:
                    for c in range(4, CH):
                        split_context(c)
                if i == 3:
                    pool.wait_ge(sem("f_scales"), 1)
                    pool.wait_ge(sem("m_down"), EXPERTS)
                    for k, (w, q) in enumerate(((win, wqi), (wout, wqo))):
                        up, back = (wsc[:, m, k * FT:(k + 1) * FT].unsqueeze(2).broadcast_to([P, FT, D])
                                    for m in range(2))
                        pseq(pool.tensor_tensor(q, w[:], up, ALU.mult))
                        pseq(pool.tensor_scalar(q, q, ROUND, ROUND, ALU.add, ALU.subtract))
                        pseq(pool.tensor_scalar(q, q, -128.0, 127.0, ALU.max, ALU.min))
                        pool.tensor_tensor(q, q, back, ALU.mult).then_inc(sem("f_wq"), 1)
            pool.wait_ge(sem("d_khat"), 1)
            for g in range(8):
                w = S - 8 * g
                pool.tensor_tensor(Z[:, g, 0:8 * w].rearrange("p (t u) -> p t u", t=8),
                                   qkh[:, 1, 8 * g:8 * g + 8].unsqueeze(2).broadcast_to([P, 8, w]),
                                   kbneg[:, 8 * g:].unsqueeze(1).broadcast_to([P, 8, w]),
                                   ALU.mult).then_inc(sem("d_z"), 1)
            pool.wait_ge(sem("d_v"), 1)
            windows = bass.AP(tensor=vpad[:].tensor, offset=vpad[:].offset,
                              ap=[list(vpad[:].ap[0]), [1, S], [1, FIR_L]])
            pseq(pool.tensor_tensor(firp, windows, W("fir_l").unsqueeze(1).broadcast_to([P, S, FIR_L]), ALU.mult))
            half = FIR_L // 2
            pool.tensor_tensor(firp[:, :, 0:half], firp[:, :, 0:half], firp[:, :, half:FIR_L],
                               ALU.add).then_inc(sem("d_firp"), 1)
            pool.wait_ge(sem("d_msq"), 1)
            pool.tensor_tensor(orn[:], oms[:], pows[:], ALU.pow).then_inc(sem("d_mrn"), 1)
            norm_pool(pool, 5)

        @block.scalar
        def _(act):
            steps = [0]

            def seq(ins):
                steps[0] += 1
                ins.then_inc(sem("act_step"), 1)
                act.wait_ge(sem("act_step"), steps[0])

            act.dma_start(wq[:], dram["wq0"]).then_inc(sem("ld_in0"), 16)
            act.dma_start(wkT[:], dram["wkT0"]).then_inc(sem("ld_in0"), 16)
            fold_q_act(act, 0)
            act.wait_ge(sem("cleared"), 3)
            flash_act(act, 0)
            turn_u_act(act, 0)

            act.wait_ge(sem("a_shifted"), 1)
            act.activation(sm, sm2, ACT.Exp, scale=float(1.0 / np.sqrt(AD))).then_inc(sem("a_exp"), 1)
            act.wait_ge(sem("a_pturned"), 1)
            act.copy(PT.rearrange("p j c -> p (j c)"), ps[:, 4, :]).then_inc(sem("a_pcopied"), 1)

            act.wait_ge(sem("m_nlog"), 1)
            act.activation(eprob[:], ps[:, 0, 0:EXPERTS], ACT.Exp, bias=nlog[:]).then_inc(sem("m_exp"), 1)
            for e in range(EXPERTS):
                act.wait_ge(sem("m_gate"), e + 1)
                if e >= 2:
                    act.wait_ge(sem("m_h"), e - 1)
                act.activation(sg[:, e % 2, :], ps[:, 2 + e % 2, 0:FT * S], ACT.Silu).then_inc(sem("m_silu"), 1)

            fold_q_act(act, 1)
            flash_act(act, 1)
            turn_u_act(act, 1)
            fold_q_act(act, 2)
            act.wait_ge(sem("b_shifted"), 1)
            act.activation(sm, sm2, ACT.Exp, scale=DK ** -0.5).then_inc(sem("b_exp"), 1)
            act.wait_ge(sem("b_pturned"), 1)
            act.copy(PT.rearrange("p j c -> p (j c)"), ps[:, 4, :]).then_inc(sem("b_pcopied"), 1)
            act.wait_ge(sem("b_u"), 2)
            act.copy(UT[:].rearrange("p (j a) c -> p j a c", a=2)[:, :, 1, :],
                     ps[:, 1, :].rearrange("p (j c) -> p j c", j=4)).then_inc(sem("ut_copied"), 1)

            act.wait_ge(sem("d_par0"), 1)
            seq(act.activation(tmpp[:, 1:2], tmpp[:, 0:1], ACT.Exp, scale=-1.0))
            act.activation(sres[:, 1, :], sres[:, 0, :], ACT.Exp, scale=-1.0).then_inc(sem("d_eres"), 1)
            act.wait_ge(sem("d_beta"), 1)
            act.activation(eb, ps[:, 1, 0:S], ACT.Exp, scale=-1.0).then_inc(sem("d_eb"), 1)
            act.activation(tmpp[:, 2:3], tmpp[:, 1:2], ACT.Ln, bias=1.0).then_inc(sem("d_ln"), 1)
            act.wait_ge(sem("d_conv"), 1)
            act.activation(vpad[:, FIR_L - 1:], cv[:, 2, :], ACT.Silu).then_inc(sem("d_v"), 1)
            act.activation(qkc, cv[:, 0:2, :], ACT.Silu).then_inc(sem("d_qk"), 1)
            act.wait_ge(sem("d_nrm"), 1)
            act.activation(rn.rearrange("p a t -> p (a t)"), nrm, ACT.Sqrt).then_inc(sem("d_sqrt"), 1)
            act.wait_ge(sem("d_l2"), 1)
            act.activation(st[:, :, :, 3].rearrange("p h b -> p b h"),
                           mom[:, 2, :].rearrange("p (b h) -> p b h", b=4), ACT.Sqrt).then_inc(sem("d_stats"), 1)
            act.wait_ge(sem("d_hidden"), 1)
            act.activation(hg.rearrange("p h t -> p (h t)"), ps[:, 4, 0:DH * S], ACT.Gelu,
                           bias=W("b1")).then_inc(sem("d_gelu"), 1)
            act.wait_ge(sem("d_gshift"), 1)
            act.activation(gsm[:], gsm[:], ACT.Exp).then_inc(sem("d_gexp"), 1)

            for f in range(FT):
                if f == 0:
                    act.wait_ge(sem("f_hidden"), 1)
                ins = act.activation(hid[:, f, :], ps[:, 3, f * S:(f + 1) * S], ACT.Gelu,
                                     bias=par[:, PARAM["b_in"][0] + f:PARAM["b_in"][0] + f + 1])
            ins.then_inc(sem("f_gelu"), 1)

        @block.vector
        def _(dve):
            steps = [0]

            def seq(ins):
                steps[0] += 1
                ins.then_inc(sem("dve_step"), 1)
                dve.wait_ge(sem("dve_step"), steps[0])

            loaded(dve, "x", "cst")
            norm_dve(dve, seq, 0)
            fold_q_dve(dve, seq, 0)
            dve.wait_ge(sem("cleared"), 3)
            flash_dve(dve, 0)
            turn_u_dve(dve, seq, 0)
            project_dve(dve, 0)
            seq(dve.tensor_tensor(x[:], x[:], ps[:, 3, 0:D], ALU.add))

            norm_dve(dve, seq, 1)
            dve.wait_ge(sem("a_qkv"), 1)
            heads = ps[:, 0, 0:2 * D].rearrange("p (h d) -> p h d", d=AD)
            r1, r2 = rot1.rearrange("p (h d) -> p h d", d=AD), rot2.rearrange("p (h d) -> p h d", d=AD)
            hd = AD // 2
            dve.tensor_tensor(r1, heads, C("cos").unsqueeze(1).broadcast_to([P, 2 * AH, AD]), ALU.mult)
            dve.tensor_tensor(r2[:, :, 0:hd], heads[:, :, hd:AD],
                              C("sin")[:, 0:hd].unsqueeze(1).broadcast_to([P, 2 * AH, hd]), ALU.mult)
            seq(dve.tensor_tensor(r2[:, :, hd:AD], heads[:, :, 0:hd],
                                  C("sin")[:, hd:AD].unsqueeze(1).broadcast_to([P, 2 * AH, hd]), ALU.mult))
            dve.tensor_tensor(qk, rot1, rot2, ALU.add).then_inc(sem("a_rotated"), 1)
            seq(dve.tensor_tensor(vblk[:], ps[:, 1, 0:D].rearrange("p (j a d) -> p j a d", j=PAIRS, a=2),
                                  C("half").unsqueeze(1).unsqueeze(3).broadcast_to([P, PAIRS, 2, AD]), ALU.mult))
            dve.wait_ge(sem("a_turned"), 1)
            dve.tensor_copy(aqT, ps[:, 2, 0:P])
            dve.tensor_tensor(kexp, ps[:, 2, P:P + S].unsqueeze(1).broadcast_to([P, AH, S]),
                              C("head8").unsqueeze(2).broadcast_to([P, AH, S]), ALU.mult).then_inc(sem("a_kexp"), 1)
            dve.wait_ge(sem("a_scores"), 1)
            sc = ps[:, 3, :].rearrange("p (h t) -> p h t", h=8)
            seq(dve.scalar_tensor_tensor(sm, sc, 0.0, C("later").unsqueeze(1).broadcast_to([P, 8, S]),
                                         ALU.is_equal, ALU.max))
            seq(dve.scalar_tensor_tensor(sm2, sm, NEVER, sc, ALU.mult, ALU.add))

            def shift(name):
                seq(dve.tensor_reduce(smx[:], sm2, AX, ALU.max))
                dve.tensor_tensor(sm2, sm2, smx[:].unsqueeze(2).broadcast_to([P, 8, S]),
                                  ALU.subtract).then_inc(sem(name), 1)

            def normalise(exp_name, name):
                dve.wait_ge(sem(exp_name), 1)
                seq(dve.tensor_reduce(ssum[:], sm, AX, ALU.add))
                seq(dve.reciprocal(smx[:], ssum[:]))
                dve.tensor_tensor(sm, sm, smx[:].unsqueeze(2).broadcast_to([P, 8, S]),
                                  ALU.mult).then_inc(sem(name), 1)

            shift("a_shifted")
            normalise("a_exp", "a_probs")
            dve.wait_ge(sem("a_out"), 1)
            dve.tensor_copy(o_s[:], ps[0:S, 5, 0:D]).then_inc(sem("a_ocopied"), 1)
            dve.wait_ge(sem("a_oturned"), 1)
            dve.tensor_copy(oT[:], ps[:, 6, 0:S].unsqueeze(1).broadcast_to([P, 2, S])).then_inc(sem("a_oT"), 1)
            dve.wait_ge(sem("a_y"), 1)
            seq(dve.tensor_tensor(x[:], x[:], ps[:, 5, 128:256], ALU.add))

            norm_dve(dve, seq, 2)
            dve.wait_ge(sem("m_logits"), 1)
            dve.tensor_reduce(nlog[:], ps[:, 0, 0:EXPERTS], AX, ALU.max, negate=True).then_inc(sem("m_nlog"), 1)
            dve.wait_ge(sem("m_exp"), 1)
            seq(dve.max(top8[:], eprob[:]))
            seq(dve.max_index(topi[:], top8[:], eprob[:]))
            seq(dve.tensor_copy(topf[:], topi[:]))
            for k in range(2):
                dve.tensor_scalar(chosen[:, k, :], C("iota8"), topf[:, k:k + 1], None, ALU.is_equal)
                seq(dve.tensor_scalar(share[:, k, :], C("iota8"), topf[:, k:k + 1], top8[:, k:k + 1],
                                      ALU.is_equal, ALU.mult))
            dve.tensor_tensor(rt16[:, 0:EXPERTS], chosen[:, 0, :], chosen[:, 1, :], ALU.add)
            seq(dve.tensor_tensor(pairsum[:, 0:1], top8[:, 0:1], top8[:, 1:2], ALU.add))
            dve.tensor_tensor(share[:, 2, :], share[:, 0, :], share[:, 1, :], ALU.add)
            seq(dve.reciprocal(pairsum[:, 1:2], pairsum[:, 0:1]))
            dve.tensor_scalar(rt16[:, EXPERTS:], share[:, 2, :], pairsum[:, 1:2], None,
                              ALU.mult).then_inc(sem("m_chosen"), 1)

            def hidden(e):
                dve.wait_ge(sem("m_up"), e + 1)
                dve.wait_ge(sem("m_silu"), e + 1)
                if e >= 2:
                    dve.wait_ge(sem("m_down"), e - 1)
                for a in range(2):
                    ins = dve.tensor_tensor(hT[:, e % 2, :, a, :], sg[:, e % 2, :].rearrange("p (f s) -> p f s", f=FT),
                                            ps[:, 4 + e % 2, 0:FT * S].rearrange("p (f s) -> p f s", f=FT), ALU.mult)
                ins.then_inc(sem("m_h"), 1)

            hidden(0)
            hidden(1)
            dve.wait_ge(sem("m_counts"), 1)
            seq(dve.tensor_scalar(meanw[:], ps[:, 1, 0:EXPERTS], 1.0, None, ALU.max))
            seq(dve.reciprocal(coef[:], meanw[:]))
            seq(dve.tensor_tensor(meanw[:], coef[:], ps[:, 1, EXPERTS:2 * EXPERTS], ALU.mult))
            seq(dve.tensor_tensor(coef[:], meanw[:], rt16[:, 0:EXPERTS], ALU.mult))

            def add_experts(es, done):
                dve.wait_ge(sem("m_down"), done)
                for e in es:
                    bank, col = DOWN_AT[e]
                    seq(dve.scalar_tensor_tensor(x[:], ps[:, bank, col:col + D], coef[:, e:e + 1], x[:], ALU.mult,
                                                 ALU.add))

            hidden(2)
            hidden(3)
            loaded(dve, "ffn")
            for i, w in enumerate((win, wout)):
                seq(dve.tensor_reduce(wamx[:, i * FT:(i + 1) * FT], w[:], AX, ALU.max, apply_absolute_value=True))
                hidden(4 + i)
            seq(dve.tensor_scalar(wamx[:], wamx[:], 1e-8, None, ALU.max))
            seq(dve.reciprocal(wsc[:, 0, :], wamx[:]))
            seq(dve.tensor_scalar(wsc[:, 0, :], wsc[:, 0, :], 127.0, None, ALU.mult))
            dve.reciprocal(wsc[:, 1, :], wsc[:, 0, :]).then_inc(sem("f_scales"), 1)
            hidden(6)
            add_experts(range(0, 3), 4)
            hidden(7)
            add_experts(range(3, 4), 4)
            add_experts(range(4, 7), 7)
            add_experts(range(7, 8), 8)

            norm_dve(dve, seq, 3)
            fold_q_dve(dve, seq, 1)
            dve.wait_ge(sem("cleared"), 5)
            flash_dve(dve, 1)
            turn_u_dve(dve, seq, 1)
            project_dve(dve, 1)
            seq(dve.tensor_tensor(o1, xn[:], ps[:, 3, 0:D], ALU.add))
            dve.tensor_tensor(o1, o1, W("bo"), ALU.add).then_inc(sem("o1_ready"), 1)
            dve.wait_ge(sem("o1_turned"), 1)
            dve.tensor_copy(o1T, ps[:, 7, 0:P]).then_inc(sem("o1T_ready"), 1)
            fold_q_dve(dve, seq, 2)
            dve.wait_ge(sem("b_scores"), 1)
            sc = ps[:, 3, :].rearrange("p (h t) -> p h t", h=8)
            seq(dve.tensor_reduce(smx[:], sc, AX, ALU.max))
            dve.tensor_tensor(sm2, sc, smx[:].unsqueeze(2).broadcast_to([P, 8, S]),
                              ALU.subtract).then_inc(sem("b_shifted"), 1)
            dve.wait_ge(sem("f_wturned"), 1)
            dve.tensor_copy(winq.rearrange("p f c -> p (f c)"), ps[:, 5, :]).then_inc(sem("f_wcopied"), 1)
            normalise("b_exp", "b_probs")
            dve.wait_ge(sem("b_u"), 1)
            dve.tensor_copy(UT[:].rearrange("p (j a) c -> p j a c", a=2)[:, :, 0, :],
                            ps[:, 0, :].rearrange("p (j c) -> p j c", j=4)).then_inc(sem("ut_copied"), 1)
            project_dve(dve, 2)
            seq(dve.tensor_tensor(x[:], x[:], ps[:, 3, 0:D], ALU.add))
            seq(dve.tensor_tensor(x[:], x[:], W("bo"), ALU.add))

            norm_dve(dve, seq, 4)
            seq(dve.tensor_scalar(tmpp[:, 0:1], W("temp"), -1.0, None, ALU.mult))
            seq(dve.tensor_tensor(tmpp[:, 0:1], tmpp[:, 0:1], W("temp"), ALU.max))
            dve.tensor_copy(sres[:, 0, :], W("res")).then_inc(sem("d_par0"), 1)
            dve.wait_ge(sem("pads"), 4)
            dve.wait_ge(sem("d_qkv"), 1)
            for i in range(3):
                ins = dve.tensor_copy(qkv_pad[i][:, TAPS - 1:], ps[:, 0, i * S:(i + 1) * S])
            seq(ins)
            for k in range(TAPS):
                for i, name in enumerate(("conv_q", "conv_k", "conv_v")):
                    a = PARAM[name][0] + k
                    if k == 0:
                        ins = dve.tensor_scalar(cv[:, i, :], qkv_pad[i][:, k:k + S], par[:, a:a + 1], None, ALU.mult)
                    else:
                        ins = dve.scalar_tensor_tensor(cv[:, i, :], qkv_pad[i][:, k:k + S], par[:, a:a + 1],
                                                       cv[:, i, :], ALU.mult, ALU.add)
                if k < TAPS - 1:
                    seq(ins)
            ins.then_inc(sem("d_conv"), 1)
            dve.wait_ge(sem("d_eb"), 1)
            seq(dve.tensor_scalar(eb, eb, 1.0, None, ALU.add))
            seq(dve.reciprocal(beta, eb))
            dve.wait_ge(sem("d_eres"), 1)
            seq(dve.tensor_scalar(sres[:, 1, :], sres[:, 1, :], 1.0, None, ALU.add))
            seq(dve.reciprocal(sres[:, 2, :], sres[:, 1, :]))
            dve.wait_ge(sem("d_ln"), 1)
            seq(dve.scalar_tensor_tensor(tmpp[:, 3:4], W("temp"), 0.0, tmpp[:, 2:3], ALU.max, ALU.add))
            seq(dve.tensor_scalar(tmpp[:, 3:4], tmpp[:, 3:4], 1e-6, None, ALU.add))
            seq(dve.reciprocal(rtemp[:], tmpp[:, 3:4]))
            dve.wait_ge(sem("d_qk"), 1)
            dve.tensor_tensor(sq, qkc.rearrange("p a t -> p (a t)"), qkc.rearrange("p a t -> p (a t)"),
                              ALU.mult).then_inc(sem("d_sq"), 1)
            dve.wait_ge(sem("d_norm"), 1)
            dve.tensor_scalar(nrm, ps[:, 2, 0:2 * S], 1e-12, None, ALU.add).then_inc(sem("d_nrm"), 1)
            dve.wait_ge(sem("d_v"), 1)
            seq(dve.tensor_tensor(R, vpad[:, FIR_L - 1:], beta, ALU.mult))
            dve.wait_ge(sem("d_sqrt"), 1)
            seq(dve.reciprocal(rn, rn))
            seq(dve.tensor_tensor(qkh, qkc, rn, ALU.mult))
            dve.scalar_tensor_tensor(kbneg, qkh[:, 1, :], -1.0, beta, ALU.mult,
                                     ALU.mult).then_inc(sem("d_khat"), 1)
            seq(dve.tensor_tensor(qexp, qkh[:, 0, :].unsqueeze(1).broadcast_to([P, DH, S]),
                                  C("head32").unsqueeze(2).broadcast_to([P, DH, S]), ALU.mult))
            for k in range(FIR_S):
                a = PARAM["fir_s"][0] + k
                win_ = vpad[:, FIR_L - FIR_S + k:FIR_L - FIR_S + k + S]
                if k == 0:
                    seq(dve.tensor_scalar(loc[:, 0, :], win_, par[:, a:a + 1], None, ALU.mult))
                else:
                    seq(dve.scalar_tensor_tensor(loc[:, 0, :], win_, par[:, a:a + 1], loc[:, 0, :],
                                                 ALU.mult, ALU.add))
            for t in range(S - 1):
                if t % 8 == 0:
                    dve.wait_ge(sem("d_a"), t // 8 + 1)
                w = S - 8 * (t // 8)
                a = (t % 8) * w + t % 8 + 1
                dve.scalar_tensor_tensor(R[:, t + 1:], ps[:, t // 8, a:a + S - 1 - t], R[:, t:t + 1], R[:, t + 1:],
                                         ALU.mult, ALU.add).then_inc(sem("d_subst"), 1)
                dve.wait_ge(sem("d_subst"), t + 1)
            dve.wait_ge(sem("d_firp"), 1)
            dve.tensor_reduce(loc[:, 1, :], firp[:, :, 0:FIR_L // 2], AX, ALU.add).then_inc(sem("d_fir"), 1)
            dve.wait_ge(sem("d_b"), 1)
            dve.tensor_tensor(Bm, ps[0:S, 0, 0:DH * S].rearrange("p (h t) -> p h t", h=DH),
                              C("upto", slice(0, S)).unsqueeze(1).broadcast_to([S, DH, S]),
                              ALU.mult).then_inc(sem("d_bcopied"), 1)
            dve.wait_ge(sem("d_uturned"), 1)
            dve.tensor_copy(u_s, ps[0:S, 1, 0:D]).then_inc(sem("d_ucopied"), 1)
            dve.wait_ge(sem("d_branches"), 1)
            seq(dve.tensor_copy(br.rearrange("p b c -> p (b c)"), ps[0:S, 2, :]))
            g16 = br.rearrange("p b (h d) -> p (b h) d", h=DH)
            c16 = cen.rearrange("p b (h d) -> p (b h) d", h=DH)

            def stat(k):
                return st[:, :, :, k].rearrange("p h b -> p b h")

            def m16(k):
                return mom[:, k, :].rearrange("p (b h) -> p b h", b=4)

            seq(dve.tensor_reduce(mom[:, 0, :], g16, AX, ALU.add))
            dve.tensor_reduce(mom[:, 1, :], g16, AX, ALU.add, apply_absolute_value=True)
            seq(dve.tensor_scalar(mom[:, 0, :], mom[:, 0, :], 1.0 / DD, None, ALU.mult))
            dve.tensor_scalar(stat(0), m16(0), 1.0, None, ALU.mult)
            seq(dve.tensor_tensor(c16, g16, mom[:, 0, :].unsqueeze(2).broadcast_to([S, 16, DD]), ALU.subtract))
            dve.tensor_scalar(stat(2), m16(1), 1.0 / DD, None, ALU.mult)
            seq(dve.tensor_tensor(cen, cen, cen, ALU.mult))
            seq(dve.tensor_reduce(mom[:, 1, :], c16, AX, ALU.add))
            dve.tensor_scalar(stat(1), m16(1), 1.0 / DD, None, ALU.mult)
            seq(dve.tensor_tensor(prod, br, br, ALU.mult))
            dve.tensor_reduce(mom[:, 2, :], prod.rearrange("p b (h d) -> p (b h) d", h=DH), AX,
                              ALU.add).then_inc(sem("d_l2"), 1)
            dve.wait_ge(sem("d_sturned"), 1)
            dve.tensor_copy(statsT.rearrange("p h t -> p (h t)"), ps[0:16, 3, 0:DH * S]).then_inc(
                sem("d_scopied"), 1)
            dve.wait_ge(sem("d_gate"), 1)
            seq(dve.tensor_tensor(gsm[:], ps[0:S, 5, 0:16].rearrange("p (h b) -> p h b", h=DH),
                                  W("b2", slice(0, S)).unsqueeze(1).broadcast_to([S, DH, 4]), ALU.add))
            seq(dve.tensor_scalar(gsm[:], gsm[:], rtemp[0:S, :], None, ALU.mult))
            seq(dve.tensor_reduce(gmx[:, 0, :], gsm[:], AX, ALU.max))
            dve.tensor_tensor(gsm[:], gsm[:], gmx[:, 0, :].unsqueeze(2).broadcast_to([S, DH, 4]),
                              ALU.subtract).then_inc(sem("d_gshift"), 1)
            dve.wait_ge(sem("d_gexp"), 1)
            seq(dve.tensor_reduce(gmx[:, 0, :], gsm[:], AX, ALU.add))
            seq(dve.reciprocal(gmx[:, 1, :], gmx[:, 0, :]))
            seq(dve.tensor_tensor(gsm[:], gsm[:], gmx[:, 1, :].unsqueeze(2).broadcast_to([S, DH, 4]), ALU.mult))
            seq(dve.tensor_scalar(gsm[:], gsm[:], 1.0 - 2.0 * FLOOR, None, ALU.mult))
            seq(dve.tensor_scalar(gsm[:, :, 0:2], gsm[:, :, 0:2], FLOOR, None, ALU.add))
            seq(dve.tensor_tensor(gsm[:, :, 0], gsm[:, :, 0], sres[0:S, 2, :], ALU.add))
            for b in range(4):
                ins = dve.tensor_tensor(prod[:, b, :].rearrange("p (h d) -> p h d", h=DH),
                                        br[:, b, :].rearrange("p (h d) -> p h d", h=DH),
                                        gsm[:, :, b:b + 1].broadcast_to([S, DH, DD]), ALU.mult)
            seq(ins)
            seq(dve.tensor_tensor(prod[:, 0:2, :], prod[:, 0:2, :], prod[:, 2:4, :], ALU.add))
            seq(dve.tensor_tensor(om, prod[:, 0, :], prod[:, 1, :], ALU.add))
            dve.memset(pows[:], -0.5)
            seq(dve.tensor_tensor(osq, om, om, ALU.mult))
            seq(dve.tensor_reduce(oms[:], osq.rearrange("p (h d) -> p h d", h=DH), AX, ALU.add))
            dve.tensor_scalar(oms[:], oms[:], 1.0 / DD, 1e-5, ALU.mult, ALU.add).then_inc(sem("d_msq"), 1)
            dve.wait_ge(sem("d_mrn"), 1)
            seq(dve.tensor_tensor(om.rearrange("p (h d) -> p h d", h=DH), om.rearrange("p (h d) -> p h d", h=DH),
                                  orn[:].unsqueeze(2).broadcast_to([S, DH, DD]), ALU.mult))
            dve.tensor_tensor(om, om, W("rms_w", slice(0, S)), ALU.mult).then_inc(sem("d_mixed"), 1)
            dve.wait_ge(sem("d_mturned"), 1)
            dve.tensor_copy(oT[:], ps[:, 6, 0:S].unsqueeze(1).broadcast_to([P, 2, S])).then_inc(sem("d_mcopied"), 1)
            dve.wait_ge(sem("d_y"), 1)
            seq(dve.tensor_tensor(x[:], x[:], ps[:, 5, 128:256], ALU.add))

            norm_dve(dve, seq, 5)

            def quantise(i, src, dst, name):
                dve.tensor_reduce(amx[:], src, mybir.AxisListType.XY if i else AX, ALU.max,
                                  apply_absolute_value=True).then_inc(sem("f_amx"), 1)
                dve.wait_ge(sem("f_amxT"), i + 1)
                dve.tensor_reduce(amxr[:], ps[0:1, 1, 0:P], AX, ALU.max).then_inc(sem("f_amxr"), 1)
                dve.wait_ge(sem("f_amxb"), i + 1)
                seq(dve.tensor_scalar(qs[:, 0:1], ps[:, 2, 0:1], 1e-8, None, ALU.max))
                seq(dve.reciprocal(qs[:, 1:2], qs[:, 0:1]))
                seq(dve.tensor_scalar(qs[:, 1:2], qs[:, 1:2], 32767.0, None, ALU.mult))
                seq(dve.reciprocal(qs[:, 2:3], qs[:, 1:2]))
                seq(dve.tensor_scalar(dst, src, qs[:, 1:2], ROUND, ALU.mult, ALU.add))
                seq(dve.tensor_scalar(dst, dst, ROUND, 32767.0, ALU.subtract, ALU.min))
                dve.tensor_scalar(dst, dst, -32768.0, qs[:, 2:3], ALU.max, ALU.mult).then_inc(sem(name), 1)

            quantise(0, xnT[:], xq, "f_xq")
            dve.wait_ge(sem("f_gelu"), 1)
            quantise(1, hid, hid, "f_hq")
            dve.wait_ge(sem("f_y"), 1)
            seq(dve.tensor_tensor(out_s, x[0:S, :], ps[0:S, 4, 0:D], ALU.add))
            dve.tensor_tensor(out_s, out_s, W("b_out", slice(0, S)), ALU.add).then_inc(sem("result"), 1)


def kernel(**inputs):
    import concourse.bacc as bacc
    from concourse.bass_utils import run_bass_kernel_spmd

    a = {k: np.asarray(v) for k, v in inputs.items()}

    def rows(name, width):
        return np.broadcast_to(a[name].reshape(1, width), (P, width))

    par = {
        "conv_q": a["L1_attn_conv_w_q"], "conv_k": a["L1_attn_conv_w_k"], "conv_v": a["L1_attn_conv_w_v"],
        "fir_s": a["L1_attn_fir_short_w"].reshape(D, FIR_S), "fir_l": a["L1_attn_fir_long_w"].reshape(D, FIR_L),
        "b1": a["L1_attn_mlp_b1"].reshape(D, 1), "b_in": a["L1_ffn_b_in"].reshape(FT, P).T,
        "rms_w": np.tile(rows("L1_attn_rms_w", DD), (1, DH)), "bo": rows("L1_xattn_bo", D),
        "b_out": rows("L1_ffn_b_out", D), "b2": rows("L1_attn_mlp_b2", 4), "temp": rows("L1_attn_logit_temp", 1),
        "res": rows("L1_attn_conv_res_logit", DH), "wb": np.repeat(a["L1_attn_Wb"], DD, axis=1),
        "w2": a["L1_attn_mlp_w2"], "router": a["L0_ffn_router_w"].T,
    }

    def tiles(w):
        return w.reshape(-1, P, w.shape[1]).transpose(1, 0, 2)

    ctx = a["ctx_1024"][0]
    arrays = {
        "x": np.concatenate([a["x"][0], a["x"][0]], 0),
        "cst": constants(),
        "par": np.concatenate([par[k] for k in PARAM], 1),
        "ctxT": ctx.T, "ctxN": tiles(ctx).reshape(P, KT * D), "mask": a["mask_SxS2_ik0"],
        "a_w": np.concatenate([a["L0_attn_qkv"].T, a["L0_attn_wo"].T], 1),
        "gateT": a["L0_ffn_gate_w"].reshape(EXPERTS * FF, D).T, "upT": a["L0_ffn_up_w"].reshape(EXPERTS * FF, D).T,
        "downT": tiles(a["L0_ffn_down_w"].transpose(0, 2, 1).reshape(EXPERTS * FF, D)),
        "d_w": np.concatenate([a["L1_attn_Wq"], a["L1_attn_Wk"], a["L1_attn_Wv"], a["L1_attn_Wo"],
                               a["L1_attn_mlp_w1"][0:D]], 1),
        "w1s": a["L1_attn_mlp_w1"][D:],
        "win": tiles(a["L1_ffn_W_in"].T), "wout": tiles(a["L1_ffn_W_out"]),
    }
    for i, names in enumerate((("L0_xattn_W_q", "L0_xattn_W_k", "L0_xattn_W_v", "L0_xattn_W_o"),
                               ("L1_xattn_Wq", "L1_xattn_Wk", "L1_xattn_Wv", "L1_xattn_Wo"))):
        arrays[f"wq{i}"] = a[names[0]]
        arrays[f"wkT{i}"] = tiles(a[names[1]].T)
        arrays[f"wv{i}"] = a[names[2]]
        arrays[f"wo{i}"] = tiles(a[names[3]])

    nc = bacc.Bacc("TRN2", target_bir_lowering=False, num_devices=1)
    dram, feed = {}, {}
    for name, v in arrays.items():
        v = np.ascontiguousarray(v)
        feed[f"in_{name}"] = v
        dram[name] = nc.dram_tensor(f"in_{name}", v.shape, mybir.dt.from_np(v.dtype), kind="ExternalInput").ap()
    dram["out"] = nc.dram_tensor("out", (S, D), F32, kind="ExternalOutput").ap()
    build(nc, dram)
    r = run_bass_kernel_spmd(nc, [feed], core_ids=[0])
    return r.results[0]["out"].reshape(1, S, D)
```

```python
from contextlib import ExitStack

import numpy as np

import concourse.bass as bass
from concourse import mybir

P = 128
S = 64
D = 128
H = 16
DK = 64
PAIRS = H // 2
NK = 6272
KT = NK // P
CH = 7
TC = KT // CH
CK = TC * P
HALF = CK // 2
RT = H * S // P
EXPERTS = 8
FF = 512
FT = FF // P
AH, AD = 16, 8
DH, DD = 4, 32
FIR_S, FIR_L, TAPS = 5, 64, 4
SCALE_STEP = (CH - 1) * RT + 3
QK_BANKS = ((0, 1), (2, 7))
DOWN_AT = [(6 + e // 4, e % 4 * D) for e in range(EXPERTS - 1)] + [(0, D)]
WARM = [0, 6, 6, 14, 6, 6]
FLOOR = 0.08
MASKED = -1e20
MASK_SLOTS = 5
NEVER = -1e30
LN_EPS = 1e-5
HALF_SCALE = 2.0 ** 15
CTX_SCALE = 2.0 ** 14
ROUND = 12582912.0

ALU = mybir.AluOpType
ACT = mybir.ActivationFunctionType
AX = mybir.AxisListType.X
F32 = mybir.dt.float32
BF16 = mybir.dt.bfloat16
F16 = mybir.dt.float16
I32 = mybir.dt.int32
U32 = mybir.dt.uint32
F32R = mybir.dt.float32r

CONST = {}
_at = 0
for _name, _width in [("ident", P), ("ones", P), ("block32", P), ("later", S), ("upto", S), ("head8", AH),
                      ("half", 2), ("cos", AD), ("sin", AD), ("head32", DH), ("iota8", EXPERTS),
                      ("power", 1)]:
    CONST[_name] = (_at, _at + _width)
    _at += _width
CONST_W = _at

PARAM = {}
_at = 0
for _name, _width in [("conv_q", TAPS), ("conv_k", TAPS), ("conv_v", TAPS), ("fir_s", FIR_S), ("fir_l", FIR_L),
                      ("b1", 1), ("b_in", FT), ("rms_w", D), ("bo", D), ("b_out", D), ("b2", 4), ("temp", 1),
                      ("res", DH), ("wb", D), ("w2", 4), ("router", EXPERTS)]:
    PARAM[_name] = (_at, _at + _width)
    _at += _width
PARAM_W = _at


def constants():
    t = np.zeros((P, CONST_W), np.float32)

    def put(name, value):
        a, b = CONST[name]
        t[:, a:b] = value

    p = np.arange(P)[:, None]
    tok = p % S
    put("ident", np.eye(P))
    put("ones", 1.0)
    put("block32", p // DD == np.arange(P)[None] // DD)
    put("later", np.arange(S)[None] > tok)
    put("upto", tok <= np.arange(S)[None])
    put("head8", p // AD == np.arange(AH)[None])
    put("half", p // S == np.arange(2)[None])
    inv = (1.0 / 10000.0 ** (np.arange(0, AD, 2, dtype=np.float32) / AD)).astype(np.float32)
    ang = tok.astype(np.float32) * inv[None]
    put("cos", np.concatenate([np.cos(ang), np.cos(ang)], 1))
    put("sin", np.concatenate([-np.sin(ang), np.sin(ang)], 1))
    put("head32", p // DD == np.arange(DH)[None])
    put("iota8", np.arange(EXPERTS)[None])
    put("power", -0.5)
    return t


def build(nc, dram):
    with ExitStack() as ctx:
        def sb(name, shape, dt=F32):
            return ctx.enter_context(nc.sbuf_tensor(name, shape, dt))

        sems = {}

        def sem(name):
            if name not in sems:
                sems[name] = ctx.enter_context(nc.semaphore(name))
            return sems[name]

        ps = ctx.enter_context(nc.psum_tensor("ps", [P, 8, 512], F32))

        cst = sb("cst", [P, CONST_W])
        par = sb("par", [P, PARAM_W])
        x = sb("x", [P, D])
        ctxN = sb("ctxN", [P, KT * D])
        ctxT_hi = sb("ctxT_hi", [P, NK], F32R)
        ctxT_lo = sb("ctxT_lo", [P, NK], F32R)
        maskb = sb("maskb", [P, NK], BF16)
        ctxN_parts = ctxN[:].bitcast(F16)
        scale_diag = maskb[:, 0:2 * D].bitcast(F32)
        scale_rows = maskb[:, 2 * D:4 * D].bitcast(F32)
        scaled = maskb[:, CK:3 * CK].bitcast(F32)
        ch_amax = sb("ch_amax", [P, CH + 1])
        ch_scale = sb("ch_scale", [P, 1])
        ch_back = sb("ch_back", [P, 1])
        wq = sb("wq", [P, H * DK])
        wkT = sb("wkT", [P, PAIRS, D])
        w_qT = wq[:].rearrange("p (j d) -> p j d", j=PAIRS)
        w_qk = (w_qT, wkT)
        wv = sb("wv", [P, H * DK])
        wo = sb("wo", [P, PAIRS, D])
        a_w = sb("a_w", [P, 4 * D])
        moe = sb("moe", [P, 3 * EXPERTS * FF])
        gateT, upT = moe[:, 0:EXPERTS * FF], moe[:, EXPERTS * FF:2 * EXPERTS * FF]
        downT = moe[:, 2 * EXPERTS * FF:].rearrange("p (f d) -> p f d", d=D)
        ctxT_raw = moe[:, 0:NK]
        mask_raw = moe[:, NK:NK + MASK_SLOTS * CK].bitcast(I32)
        d_w = sb("d_w", [P, 5 * D])
        w1s = sb("w1s", [16, D])
        win = sb("win", [P, FT, D])
        wout = sb("wout", [P, FT, D])

        def C(name, rows=slice(0, P)):
            return cst[rows, CONST[name][0]:CONST[name][1]]

        def W(name, rows=slice(0, P)):
            return par[rows, PARAM[name][0]:PARAM[name][1]]

        ident = C("ident")

        regions = [[moe, EXPERTS * FF, 3 * EXPERTS * FF]]

        def late(rows, *shape):
            n = int(np.prod(shape))
            region = next(g for g in regions if g[2] - g[1] >= n)
            v = region[0][0:rows, region[1]:region[1] + n]
            region[1] += n
            return v.rearrange("p (a b) -> p a b", a=shape[0]) if len(shape) > 1 else v

        stats6 = sb("stats6", [P, 6])
        mv = sb("mv", [P, 2])
        veps = sb("veps", [P, 1])
        rstd = sb("rstd", [P, 1])
        xn = sb("xn", [P, D])
        xnT = sb("xnT", [P, P])
        GT_hi = sb("GT_hi", [P, RT, P], F32R)
        GT_lo = sb("GT_lo", [P, RT, P], F32R)
        probs = sb("probs", [P, 2, CK])
        probsT = sb("probsT", [P, 2, CK])
        probsT_parts = probsT[:].rearrange("p b k -> p (b k)").bitcast(F16).rearrange("p (b h k) -> p b h k", b=2, h=2)
        rowmax = sb("rowmax", [P, 2])
        negmax = sb("negmax", [P, (CH + 1) * RT])
        alpha = sb("alpha", [P, CH * RT])
        chunksum = sb("chunksum", [P, CH * RT])
        den = sb("den", [P, RT])
        rden = sb("rden", [P, RT])
        U = sb("U", [P, RT, D])
        GT = U
        UT = sb("UT", [P, RT, P])
        OT = sb("OT", [P, PAIRS, 2, S])
        QT = OT[:, 0:4, :, :].rearrange("p j a s -> p (j a) s")
        qk = probsT[:, 1, 0:2 * D]
        vblk = sb("vblk", [P, PAIRS, 2, AD])
        aqT = probsT[:, 1, 2 * D:3 * D]
        kexp = UT[:].rearrange("p r (a t) -> p (r a) t", a=2)
        sm = probs[:, 0, 0:8 * S].rearrange("p (h t) -> p h t", h=8)
        sm2 = probs[:, 1, 0:8 * S].rearrange("p (h t) -> p h t", h=8)
        smx = sb("smx", [P, 8])
        ssum = sb("ssum", [P, 8])
        PT = probsT[:, 0, 0:4 * P].rearrange("p (j c) -> p j c", j=4)
        rot1 = PT[:, 0:2, :].rearrange("p a b -> p (a b)")
        rot2 = PT[:, 2:4, :].rearrange("p a b -> p (a b)")
        o_s = sb("o_s", [S, D])
        oT = sb("oT", [P, 2, S])
        nlog = sb("nlog", [P, 1])
        eprob = sb("eprob", [P, EXPERTS])
        top8 = sb("top8", [P, 8])
        topi = sb("topi", [P, 8], U32)
        topf = sb("topf", [P, 8])
        chosen = sb("chosen", [P, 2, EXPERTS])
        rt16 = sb("rt16", [P, 2 * EXPERTS])
        pairsum = sb("pairsum", [P, 2])
        meanw = sb("meanw", [P, EXPERTS])
        coef = sb("coef", [P, EXPERTS])
        share = sb("share", [P, 3, EXPERTS])
        sg = probs[:, :, 0:FT * S]
        hT = probsT[:, :, 0:FT * P].rearrange("p b (f a s) -> p b f a s", f=FT, a=2)
        o1 = late(P, D)
        o1T = late(P, P)
        qkv_pad = [sb(f"pad{i}", [P, TAPS - 1 + S]) for i in range(3)]
        cv = late(P, 3, S)
        vpad = sb("vpad", [P, FIR_L - 1 + S])
        qkc = late(P, 2, S)
        sq = late(P, 2 * S)
        nrm = late(P, 2 * S)
        rn = late(P, 2, S)
        qkh = late(P, 2, S)
        eb = late(P, S)
        beta = late(P, S)
        kbneg = late(P, S)
        R = late(P, S)
        Z = ctxN[:, 0:S * S].rearrange("p (g c) -> p g c", g=8)
        firp = gateT[:, 0:S * FIR_L].rearrange("p (t k) -> p t k", t=S)
        loc = late(P, 2, S)
        qexp = late(P, DH, S)
        Bm = late(S, DH, S)
        u_s = late(S, D)
        br = late(S, 4, D)
        cen = late(S, 4, D)
        st = sb("st", [S, DH, 4, 4])
        mom = sb("mom", [S, 3, 16])
        statsT = late(16, DH, S)
        hg = late(P, DH, S)
        gsm = sb("gsm", [S, DH, 4])
        gadd = sb("gadd", [S, DH, 4])
        gmx = sb("gmx", [S, 2, DH])
        tmpp = sb("tmpp", [P, 4])
        rtemp = sb("rtemp", [P, 1])
        sres = sb("sres", [P, 3, DH])
        prod = late(S, 4, D)
        om = late(S, D)
        osq = late(S, D)
        oms = sb("oms", [S, DH])
        orn = sb("orn", [S, DH])
        pows = sb("pows", [S, DH])
        wamx = sb("wamx", [P, 2 * FT])
        wsc = sb("wsc", [P, 2, 2 * FT])
        wqi = late(P, FT, D)
        wqo = late(P, FT, D)
        winq = late(P, FT, P)
        amx = sb("amx", [P, 1])
        amxr = sb("amxr", [1, 1])
        qs = sb("qs", [P, 3])
        xq = late(P, P)
        hid = late(P, FT, S)
        out_s = late(S, D)

        block = ctx.enter_context(nc.Block())

        DMAS = {"x": 1, "cst": 1, "par": 1, "in0": 2, "out0": 2, "in1": 2, "out1": 2, "small_attn": 1, "experts": 3,
                "delta": 2, "ffn": 2}

        def loaded(eng, *names):
            for name in names:
                eng.wait_ge(sem("ld_" + name), 16 * DMAS[name])

        @block.sync
        def _(sp):
            def load(name, dst, src):
                sp.dma_start(dst, dram[src]).then_inc(sem("ld_" + name), 16)

            load("x", x[:], "x")
            load("cst", cst[:], "cst")
            for c in range(CH):
                keys, slot = slice(c * CK, (c + 1) * CK), c % MASK_SLOTS
                landed = sem(f"ld_chunk{c}")
                sp.dma_start(ctxT_raw[:, keys], dram["ctxT"][:, keys]).then_inc(landed, 16)
                if c >= MASK_SLOTS:
                    sp.wait_ge(sem("mask_ready"), c - MASK_SLOTS + 1)
                for a in range(2):
                    sp.dma_start(mask_raw[a * S:(a + 1) * S, slot * CK:(slot + 1) * CK],
                                 dram["mask"][:, keys]).then_inc(landed, 16)
                sp.dma_start(ctxN[:, keys], dram["ctxN"][:, keys]).then_inc(landed, 16)
                if c == 0:
                    load("par", par[:], "par")
            for name, t, src in (("out0", wv, "wv0"), ("out0", wo, "wo0"), ("ffn", win, "win"), ("ffn", wout, "wout"),
                                 ("small_attn", a_w, "a_w"), ("delta", d_w, "d_w"), ("delta", w1s, "w1s")):
                load(name, t[:], src)
            sp.wait_ge(sem("ctxT_ready"), CH)
            sp.wait_ge(sem("mask_ready"), CH)
            load("experts", gateT, "gateT")
            load("experts", upT, "upT")
            load("experts", downT, "downT")
            sp.wait_ge(sem("g_ready"), 2)
            load("in1", w_qT, "wqT1")
            load("in1", wkT[:], "wkT1")
            sp.wait_ge(sem("y_ready"), 1)
            load("out1", wv[:], "wv1")
            load("out1", wo[:], "wo1")
            sp.wait_ge(sem("result"), 1)
            sp.dma_start(dram["out"], out_s).then_inc(sem("stored"), 16)
            sp.wait_ge(sem("stored"), 16)

        def flash_pe(pe, L):
            base = L * CH * RT
            scores_ready, exp_done = sem("scores_ready"), sem("exp_done")
            turned = [sem("turned_lo"), sem("turned_hi")]
            copied = [sem("copied_lo"), sem("copied_hi")]
            pv_done, u_added = sem("pv_done"), sem("u_added")

            def scores(c, r):
                n, b, first = c * RT + r, r % 2, isinstance(c, int) and c == 0
                if not (first and r < 2):
                    pe.wait_ge(exp_done if L else sem("masked"), base + n - 1)
                if first and r == RT // 2:
                    pe.wait_ge(sem("g_copied"), 2 * L + 2)
                if r == 0 and L == 0:
                    pe.wait_ge(sem("ctxT_ready"), c + 1)
                for h in range(2):
                    if h == 1 and not (first and r < 4):
                        pe.wait_ge(u_added, base + n - 3)
                    out = ps[:, 2 * b + h, 0:HALF]
                    keys = bass.ds(c * CK + h * HALF, HALF)
                    pe.matmul(out, GT_hi[:, r, :], ctxT_hi[:, keys], start=True, stop=False)
                    pe.matmul(out, GT_hi[:, r, :], ctxT_lo[:, keys], start=False, stop=False)
                    ins = pe.matmul(out, GT_lo[:, r, :], ctxT_hi[:, keys], start=False, stop=True)
                ins.then_inc(scores_ready, 1)

            def turn(c, r):
                n, b = c * RT + r, r % 2
                pe.wait_ge(exp_done, base + n + 1)
                for part, tiles in enumerate((range(0, 4), range(4, TC))):
                    for k in tiles:
                        ins = pe.transpose(ps[:, 4 + part, (k % 4) * P:(k % 4 + 1) * P],
                                           probs[:, b, k * P:(k + 1) * P], ident)
                    ins.then_inc(turned[part], 1)

            def pv(c, r, alone=False):
                n, b, first = c * RT + r, r % 2, isinstance(c, int) and c == 0
                if L == 1 and first and r == 0:
                    pe.wait_ge(sem("ctx_parts"), CH)
                if alone:
                    pe.wait_ge(u_added, base + n - 1)
                if L == 0 and isinstance(n, int) and n == SCALE_STEP:
                    pe.wait_ge(sem("scale_diag"), 1)
                    pe.matmul(ps[:, 6 + b, D:2 * D], C("ones"), scale_diag, start=True, stop=True)
                if L == 0:
                    for k in range(TC):
                        if k % 4 == 0:
                            pe.wait_ge(copied[k // 4], base + n + 1)
                        ins = pe.matmul(ps[:, 6 + b, 0:D], probsT[:, b, k * P:(k + 1) * P],
                                        ctxN[:, bass.ds((c * TC + k) * D, D)], start=(k == 0), stop=(k == TC - 1))
                    ins.then_inc(pv_done, 1)
                    return
                parts = ctxN_parts[:, bass.ds(2 * c * CK, 2 * CK)]
                for p_part, c_part in ((0, 0), (0, 1), (1, 0)):
                    for k in range(TC):
                        if k % 4 == 0 and (p_part, c_part) == (0, 0):
                            pe.wait_ge(sem("uppers"), 2 * n + 1 + k // 4)
                        if k % 4 == 0 and p_part == 1:
                            pe.wait_ge(copied[k // 4], base + n + 1)
                        ins = pe.matmul(ps[:, 6 + b, 0:D], probsT_parts[:, b, p_part, k * P:(k + 1) * P],
                                        parts[:, c_part * CK + k * D:c_part * CK + (k + 1) * D],
                                        start=(c_part == 0 and p_part == 0 and k == 0),
                                        stop=(p_part == 1 and k == TC - 1))
                ins.then_inc(pv_done, 1)

            def chunk(c, last=False):
                for r in range(RT):
                    if r < RT - 2:
                        scores(c, r + 2)
                    elif not last:
                        scores(c + 1, r + 2 - RT)
                    pv(c, r, alone=last and r >= RT - 2)
                    if r < RT - 1:
                        turn(c, r + 1)
                    elif not last:
                        turn(c + 1, 0)

            scores(0, 0)
            scores(0, 1)
            stay_warm(pe, 6, 8 if L else 12)
            turn(0, 0)
            chunk(0)
            with pe.Fori(1, CH - 1) as c:
                chunk(c)
            chunk(CH - 1, last=True)

        def flash_act(act, L):
            base = L * CH * RT
            nm_ready, exp_done = sem("negmax_ready"), sem("exp_done")
            turned, copied, pv_done = sem("turned_lo"), sem("copied_lo"), sem("pv_done")

            def exps(c, r):
                n, b, first = c * RT + r, r % 2, isinstance(c, int) and c == 0
                act.wait_ge(nm_ready, base + n + 1)
                new = negmax[:, bass.ds(n + RT, 1)]
                act.activation(alpha[:, bass.ds(n, 1)], negmax[:, bass.ds(n, 1)], ACT.Exp, bias=new, scale=-1.0)
                pr = probs[:, b, :].rearrange("p (h k) -> p h k", h=2)
                if L and not (first and r < 2):
                    act.wait_ge(sem("turned_hi"), base + n - 1)
                act.activation(pr, ps[:, 2 * b:2 * b + 2, 0:HALF] if L else pr, ACT.Exp, bias=new, scale=DK ** -0.5,
                               accum_out=chunksum[:, bass.ds(n, 1)]).then_inc(exp_done, 1)

            def copy_lo(c, r):
                n, b, first = c * RT + r, r % 2, isinstance(c, int) and c == 0
                act.wait_ge(turned, base + n + 1)
                if not (first and r < 2):
                    act.wait_ge(pv_done, base + n - 1)
                if L == 1:
                    act.activation(probsT_parts[:, b, 0, 0:4 * P], ps[:, 4, :], ACT.Copy,
                                   scale=HALF_SCALE).then_inc(sem("uppers"), 1)
                    act.wait_ge(sem("turned_hi"), base + n + 1)
                    act.activation(probsT_parts[:, b, 0, 4 * P:CK], ps[:, 5, 0:(TC - 4) * P], ACT.Copy,
                                   scale=HALF_SCALE).then_inc(sem("uppers"), 1)
                    return
                act.copy(probsT[:, b, 0:4 * P], ps[:, 4, :]).then_inc(copied, 1)
                if L == 0:
                    act.wait_ge(sem("turned_hi"), base + n + 1)
                    act.copy(probsT[:, b, 4 * P:CK], ps[:, 5, 0:(TC - 4) * P]).then_inc(sem("copied_hi"), 1)

            def chunk(c, last=False):
                for r in range(RT):
                    copy_lo(c, r)
                    if r < RT - 1:
                        exps(c, r + 1)
                    elif not last:
                        exps(c + 1, 0)

            exps(0, 0)
            chunk(0)
            with act.Fori(1, CH - 1) as c:
                chunk(c)
            chunk(CH - 1, last=True)

        def flash_dve(dve, L):
            base = L * CH * RT
            scores_ready, nm_ready, rowmax_ready = sem("scores_ready"), sem("negmax_ready"), sem("rowmax")
            copied = [sem("copied_lo"), sem("copied_hi")]
            pv_done, u_added, den_added = sem("pv_done"), sem("u_added"), sem("den_added")

            def maximum(c, r):
                n, b, first = c * RT + r, r % 2, isinstance(c, int) and c == 0
                dve.wait_ge(scores_ready, base + n + 1)
                src = ps[:, 2 * b:2 * b + 2, 0:HALF]
                if L == 0:
                    if r == 0:
                        dve.wait_ge(sem("mask_ready"), c + 1)
                    if not (first and r < 2):
                        dve.wait_ge(sem("turned_hi"), base + n - 1)
                    masked = probs[:, b, :].rearrange("p (h k) -> p h k", h=2)
                    dve.tensor_tensor(masked, src, maskb[:, bass.ds(c * CK, CK)].rearrange("p (h k) -> p h k", h=2),
                                      ALU.add).then_inc(sem("masked"), 1)
                    dve.wait_ge(sem("masked"), base + n + 1)
                    src = masked
                dve.tensor_reduce(rowmax[:, b:b + 1], src, mybir.AxisListType.XY,
                                  ALU.max).then_inc(rowmax_ready, 1)
                dve.wait_ge(rowmax_ready, base + n + 1)
                dve.tensor_scalar(negmax[:, bass.ds(n + RT, 1)], rowmax[:, b:b + 1], -(DK ** -0.5),
                                  negmax[:, bass.ds(n, 1)], ALU.mult, ALU.min).then_inc(nm_ready, 1)

            def add(c, r):
                n, b, first = c * RT + r, r % 2, isinstance(c, int) and c == 0
                dve.wait_ge(sem("exp_done"), base + n + 1)
                if not first:
                    dve.wait_ge(den_added, base + n - RT + 1)
                dve.scalar_tensor_tensor(den[:, r:r + 1], den[:, r:r + 1], alpha[:, bass.ds(n, 1)],
                                         chunksum[:, bass.ds(n, 1)], ALU.mult, ALU.add).then_inc(den_added, 1)
                dve.wait_ge(pv_done, base + n + 1)
                if L == 0 and isinstance(n, int) and n == SCALE_STEP:
                    dve.tensor_copy(scale_rows, ps[:, 6 + b, D:2 * D]).then_inc(sem("scale_rows"), 1)
                if not first:
                    dve.wait_ge(u_added, base + n - RT + 1)
                dve.scalar_tensor_tensor(U[:, r, :], U[:, r, :], alpha[:, bass.ds(n, 1)],
                                         ps[:, 6 + b, 0:D], ALU.mult, ALU.add).then_inc(u_added, 1)

            def scale(r):
                dve.wait_ge(den_added, base + (CH - 1) * RT + r + 1)
                dve.reciprocal(rden[:, r:r + 1], den[:, r:r + 1]).then_inc(sem("den_inverted"), 1)
                dve.wait_ge(u_added, base + (CH - 1) * RT + r + 1)
                dve.wait_ge(sem("den_inverted"), L * RT + r + 1)
                dve.tensor_scalar(U[:, r, :], U[:, r, :], rden[:, r:r + 1], None, ALU.mult).then_inc(
                    sem("u_scaled"), 1)

            def lowers(c, r):
                n, b = c * RT + r, r % 2
                for part, (a, w) in enumerate(((0, 4 * P), (4 * P, CK - 4 * P))):
                    dve.wait_ge(sem("uppers"), 2 * n + part + 1)
                    dve.scalar_tensor_tensor(probsT_parts[:, b, 1, a:a + w], ps[:, 4 + part, 0:w], HALF_SCALE,
                                             probsT_parts[:, b, 0, a:a + w], ALU.mult,
                                             ALU.subtract).then_inc(copied[part], 1)

            def chunk(c, first=False, last=False):
                for r in range(RT):
                    if r < RT - 1:
                        maximum(c, r + 1)
                    elif not last:
                        maximum(c + 1, 0)
                    if r > 0:
                        add(c, r - 1)
                    elif not first:
                        add(c - 1, RT - 1)
                    if L == 1:
                        lowers(c, r)
                    elif r == 1 and not last:
                        channel_max(c + 1)
                    elif r == 4 and first:
                        channel_max(0)
                    elif r == 0 and last:
                        channel_scales()
                    if last and r > 0:
                        scale(r - 1)

            def channel_max(c):
                dve.wait_ge(sem("ctxT_ready"), c + 1)
                dve.tensor_reduce(ch_amax[:, bass.ds(c, 1)], ctxT_hi[:, bass.ds(c * CK, CK)].bitcast(F32), AX,
                                  ALU.max, apply_absolute_value=True).then_inc(sem("ch_max"), 1)

            def channel_scales():
                whole = ch_amax[:, CH:CH + 1]
                steps = iter(range(CH + 1, CH + 6))
                dve.wait_ge(sem("ch_max"), CH)
                dve.tensor_reduce(whole, ch_amax[:, 0:CH], AX, ALU.max).then_inc(sem("ch_max"), 1)
                dve.wait_ge(sem("ch_max"), next(steps))
                dve.tensor_scalar(whole, whole, 1e-20, None, ALU.max).then_inc(sem("ch_max"), 1)
                dve.wait_ge(sem("ch_max"), next(steps))
                dve.tensor_scalar(whole.bitcast(I32), whole.bitcast(I32), 0x7F800000, None,
                                  ALU.bitwise_and).then_inc(sem("ch_max"), 1)
                dve.wait_ge(sem("ch_max"), next(steps))
                dve.reciprocal(ch_scale[:], whole).then_inc(sem("ch_max"), 1)
                dve.tensor_scalar(ch_back[:], whole, 1.0 / (CTX_SCALE * HALF_SCALE), None,
                                  ALU.mult).then_inc(sem("ch_back"), 1)
                dve.wait_ge(sem("ch_max"), next(steps))
                dve.tensor_scalar(ch_scale[:], ch_scale[:], CTX_SCALE, None, ALU.mult).then_inc(sem("ch_scale"), 1)

            maximum(0, 0)
            chunk(0, first=True)
            with dve.Fori(1, CH - 1) as c:
                chunk(c)
            chunk(CH - 1, last=True)
            add(CH - 1, RT - 1)
            scale(RT - 1)

        def norm_dve(dve, seq, i):
            seq(dve.bn_stats(stats6[:], x[:]))
            seq(dve.bn_aggr(mv[:], stats6[:]))
            dve.tensor_scalar(veps[:], mv[:, 1:2], LN_EPS, None, ALU.add).then_inc(sem("ln_var"), 1)
            dve.wait_ge(sem("ln_rstd"), i + 1)
            dve.tensor_scalar(xn[:], x[:], mv[:, 0:1], rstd[:], ALU.subtract, ALU.mult).then_inc(sem("ln_xn"), 1)
            dve.wait_ge(sem("ln_turned"), i + 1)
            dve.tensor_copy(xnT[:], ps[:, 7, 0:P]).then_inc(sem("ln_xnT"), 1)
            dve.wait_ge(sem("ln_xnT"), i + 1)

        def norm_pool(pool, i):
            pool.wait_ge(sem("ln_var"), i + 1)
            pool.tensor_tensor(rstd[:], veps[:], C("power"), ALU.pow).then_inc(sem("ln_rstd"), 1)

        def stay_warm(pe, bank, k):
            for _ in range(k):
                pe.matmul(ps[:, bank, 0:P], ident, ident, start=True, stop=True)

        def norm_pe(pe, i):
            if i:
                stay_warm(pe, 2, WARM[i])
            pe.wait_ge(sem("ln_xn"), i + 1)
            pe.transpose(ps[:, 7, 0:P], xn[:], ident).then_inc(sem("ln_turned"), 1)
            stay_warm(pe, 2, 2)

        def fold_q_pe(pe, i, src):
            if i == 0:
                for j in range(PAIRS):
                    ins = pe.matmul(ps[:, j // 4, j % 4 * S:(j % 4 + 1) * S], wq[:, j * P:(j + 1) * P], src[:, 0:S],
                                    start=True, stop=True)
                ins.then_inc(sem("q_ready"), 1)
                stay_warm(pe, 6, 5)
                pe.wait_ge(sem("q_copied"), 2)
            for par_ in range(2):
                rows = slice(par_ * DK, (par_ + 1) * DK)
                for j in range(PAIRS):
                    out = ps[:, 4 + par_, j * S:(j + 1) * S]
                    if i == 0:
                        ins = pe.matmul(out, wkT[rows, j, :], QT[rows, j, :], start=True, stop=True)
                    else:
                        ins = pe.matmul(out, w_qk[par_][:, j, :], src[:, 0:S], start=True, stop=True)
                ins.then_inc(sem("g_ready"), 1)

        def fold_weights_pe(pe):
            for par_ in range(2):
                rows = slice(par_ * DK, (par_ + 1) * DK)
                for j in range(PAIRS):
                    ins = pe.matmul(ps[:, QK_BANKS[par_][j // 4], j % 4 * D:(j % 4 + 1) * D], w_qT[rows, j, :],
                                    wkT[rows, j, :], start=True, stop=True)
            ins.then_inc(sem("w_folded"), 1)

        def fold_weights_act(act):
            act.wait_ge(sem("w_folded"), 1)
            for par_ in range(2):
                for half in range(2):
                    ins = act.copy(w_qk[par_][:, 4 * half:4 * half + 4, :].rearrange("p j d -> p (j d)"),
                                   ps[:, QK_BANKS[par_][half], :])
            ins.then_inc(sem("w_qk_ready"), 1)

        def fold_q_dve(dve, seq, i):
            if i == 0:
                dve.wait_ge(sem("q_ready"), 1)
                dve.tensor_copy(QT[:, 0:4, :].rearrange("p j s -> p (j s)"), ps[:, 0, 0:4 * S]).then_inc(
                    sem("q_copied"), 1)
                dve.wait_ge(sem("ld_chunk0"), 4 * 16)
                dve.tensor_copy(ctxT_hi[:, 0:CK], ctxT_raw[:, 0:CK]).then_inc(sem("ctxT_upper"), 1)
                dve.tensor_scalar(maskb[:, 0:CK], mask_raw[:, 0:CK], 0.0, MASKED, ALU.is_equal,
                                  ALU.mult).then_inc(sem("mask_ready"), 1)
                dve.wait_ge(sem("ctxT_upper"), 1)
                dve.tensor_tensor(ctxT_lo[:, 0:CK], ctxT_raw[:, 0:CK], ctxT_hi[:, 0:CK].bitcast(F32),
                                  ALU.subtract).then_inc(sem("ctxT_ready"), 1)
            dve.wait_ge(sem("g_ready"), 2 * i + 1)
            if i == 2:
                dve.tensor_copy(GT[:, 0:4, :].rearrange("p r c -> p (r c)"), ps[:, 4, :]).then_inc(
                    sem("g_copied"), 1)
                return
            seq(dve.tensor_copy(GT_hi[:, 0:4, :].rearrange("p r c -> p (r c)"), ps[:, 4, :]))
            for half in range(2):
                if half == 1:
                    dve.wait_ge(sem("g_upper"), i + 1)
                hi = GT_hi[:, 4 * half:4 * half + 4, :].rearrange("p r c -> p (r c)").bitcast(F32)
                dve.tensor_tensor(GT_lo[:, 4 * half:4 * half + 4, :].rearrange("p r c -> p (r c)"),
                                  ps[:, 4 + half, :], hi, ALU.subtract).then_inc(sem("g_copied"), 1)

        def fold_q_act(act, i):
            if i == 0:
                act.wait_ge(sem("q_ready"), 1)
                act.copy(QT[:, 4:8, :].rearrange("p j s -> p (j s)"), ps[:, 1, 0:4 * S]).then_inc(
                    sem("q_copied"), 1)
            act.wait_ge(sem("g_ready"), 2 * i + 2)
            act.copy((GT if i == 2 else GT_hi)[:, 4:8, :].rearrange("p r c -> p (r c)"), ps[:, 5, :]).then_inc(
                sem("g_upper"), 1)

        def project_pe(pe, L, i):
            stay_warm(pe, 6, 4)
            pe.wait_ge(sem("ut_copied"), 2 * i + 2)
            for j in range(PAIRS):
                for par_ in range(2):
                    h, g = 2 * j + par_, par_ * PAIRS + j
                    ins = pe.matmul(ps[par_ * DK:(par_ + 1) * DK, 2 - j // 4, j % 4 * S:(j % 4 + 1) * S],
                                    wv[:, h * DK:(h + 1) * DK], UT[:, g // 2, (g % 2) * S:(g % 2 + 1) * S],
                                    start=True, stop=True)
                if j % (PAIRS // 2) == PAIRS // 2 - 1:
                    ins.then_inc(sem("o_ready"), 1)
            stay_warm(pe, 6, 1)
            for j in range(PAIRS):
                if j == 0:
                    pe.wait_ge(sem("o_copied"), i + 1)
                if j == PAIRS // 2:
                    pe.wait_ge(sem("o_copied_act"), i + 1)
                ins = pe.matmul(ps[:, 3, 0:D], OT[:, j, :, :].rearrange("p a s -> p (a s)"), wo[:, j, :],
                                start=(j == 0), stop=(j == PAIRS - 1))
            ins.then_inc(sem("y_ready"), 1)

        def output_half(half):
            js = slice(half * PAIRS // 2, (half + 1) * PAIRS // 2)
            return OT[:, js, :, :], (ps[:, 2 - half, 0:4 * S].rearrange("p (j s) -> p j s", j=4).unsqueeze(2)
                                     .broadcast_to([P, PAIRS // 2, 2, S]))

        def project_dve(dve, i):
            dve.wait_ge(sem("o_ready"), 2 * i + 1)
            dve.tensor_copy(*output_half(0)).then_inc(sem("o_copied"), 1)
            dve.wait_ge(sem("y_ready"), i + 1)

        def project_act(act, i):
            act.wait_ge(sem("o_ready"), 2 * i + 2)
            act.copy(*output_half(1)).then_inc(sem("o_copied_act"), 1)

        def turn_u_pe(pe, L):
            for r in range(RT):
                pe.wait_ge(sem("u_scaled"), L * RT + r + 1)
                ins = pe.transpose(ps[:, r // 4, (r % 4) * P:(r % 4 + 1) * P], U[:, r, :], ident)
                if r % 4 == 3:
                    ins.then_inc(sem("u_turned"), 1)

        def turn_u_dve(dve, seq, L):
            dve.wait_ge(sem("u_turned"), 2 * L + 1)
            ut, src = UT[:, 0:4, :].rearrange("p r c -> p (r c)"), ps[:, 0, :]
            if L == 1:
                dve.tensor_scalar(ut, src, ch_back[:], None, ALU.mult).then_inc(sem("ut_copied"), 1)
            else:
                dve.tensor_copy(ut, src).then_inc(sem("ut_copied"), 1)

        def turn_u_act(act, L):
            act.wait_ge(sem("u_turned"), 2 * L + 2)
            ut, src = UT[:, 4:8, :].rearrange("p r c -> p (r c)"), ps[:, 1, :]
            if L == 1:
                act.activation(ut, src, ACT.Copy, scale=ch_back[:]).then_inc(sem("ut_copied"), 1)
            else:
                act.copy(ut, src).then_inc(sem("ut_copied"), 1)

        def windows(padded, taps):
            v = padded[:]
            return bass.AP(tensor=v.tensor, offset=v.offset, ap=[list(v.ap[0]), [1, S], [1, taps]])

        def key_products(eng, g):
            w = S - 8 * g
            return eng.tensor_tensor(Z[:, g, 0:8 * w].rearrange("p (t u) -> p t u", t=8),
                                     qkh[:, 1, 8 * g:8 * g + 8].unsqueeze(2).broadcast_to([P, 8, w]),
                                     kbneg[:, 8 * g:].unsqueeze(1).broadcast_to([P, 8, w]), ALU.mult)

        @block.tensor
        def _(pe):
            pe.wait_ge(sem("cleared"), 2)
            for _ in range(12):
                pe.matmul(ps[:, 6, 0:P], U[:, 0, :], U[:, 0, :], start=True, stop=True)
            loaded(pe, "cst", "in0")
            norm_pe(pe, 0)
            pe.wait_ge(sem("ln_xnT"), 1)
            fold_q_pe(pe, 0, xnT)
            stay_warm(pe, 6, 4)
            pe.wait_ge(sem("g_copied"), 1)
            flash_pe(pe, 0)
            turn_u_pe(pe, 0)
            loaded(pe, "out0")
            project_pe(pe, 0, 0)

            norm_pe(pe, 1)
            pe.wait_ge(sem("ln_xnT"), 2)
            loaded(pe, "small_attn")
            pe.matmul(ps[:, 0, 0:2 * D], xnT[:], a_w[:, 0:2 * D], start=True, stop=True)
            pe.matmul(ps[:, 1, 0:D], xnT[:], a_w[:, 2 * D:3 * D], start=True, stop=True).then_inc(sem("a_qkv"), 1)
            stay_warm(pe, 6, 6)
            pe.wait_ge(sem("a_rotated"), 1)
            pe.transpose(ps[:, 2, 0:P], qk[:, 0:D], ident)
            pe.transpose(ps[:, 2, P:2 * P], qk[:, D:2 * D], ident).then_inc(sem("a_turned"), 1)
            stay_warm(pe, 6, 6)
            pe.wait_ge(sem("a_kexp"), 1)
            for hh in range(2):
                ins = pe.matmul(ps[hh * S:(hh + 1) * S, 3, :], aqT[:, hh * S:(hh + 1) * S],
                                kexp[:, 8 * hh:8 * hh + 8, :], start=True, stop=True)
            ins.then_inc(sem("a_scores"), 1)
            loaded(pe, "in1")
            fold_weights_pe(pe)
            stay_warm(pe, 6, 8)
            pe.wait_ge(sem("a_probs"), 1)
            for j in range(4):
                ins = pe.transpose(ps[:, 4, j * P:(j + 1) * P], sm[:, 2 * j:2 * j + 2, :].rearrange("p a t -> p (a t)"),
                                   ident)
            ins.then_inc(sem("a_pturned"), 1)
            stay_warm(pe, 6, 4)
            pe.wait_ge(sem("a_pcopied"), 1)
            for hh in range(2):
                for j in range(4):
                    pr = 4 * hh + j
                    ins = pe.matmul(ps[0:S, 5, pr * 16:(pr + 1) * 16], PT[:, j, hh * S:(hh + 1) * S],
                                    vblk[:, pr, :, :].rearrange("p a d -> p (a d)"), start=True, stop=True)
            ins.then_inc(sem("a_out"), 1)
            pe.wait_ge(sem("a_ocopied"), 1)
            pe.transpose(ps[:, 6, 0:S], o_s[:], C("ident", slice(0, S))[:, 0:S]).then_inc(sem("a_oturned"), 1)
            pe.wait_ge(sem("a_oT"), 1)
            pe.matmul(ps[:, 5, 128:256], oT[:].rearrange("p a s -> p (a s)"), a_w[:, 3 * D:4 * D],
                      start=True, stop=True).then_inc(sem("a_y"), 1)

            pe.wait_ge(sem("w_qk_ready"), 1)
            norm_pe(pe, 2)
            pe.wait_ge(sem("ln_xnT"), 3)
            loaded(pe, "par", "experts")
            pe.matmul(ps[:, 0, 0:EXPERTS], xnT[:], W("router"), start=True, stop=True).then_inc(sem("m_logits"), 1)

            def gate_up(e):
                b = e % 2
                if e >= 2:
                    pe.wait_ge(sem("m_h"), e - 1)
                for w, bank in ((gateT, 2 + b), (upT, 4 + b)):
                    for f in range(FT):
                        ins = pe.matmul(ps[:, bank, f * S:(f + 1) * S], w[:, (e * FT + f) * P:(e * FT + f + 1) * P],
                                        xnT[:, 0:S], start=True, stop=True)
                    ins.then_inc(sem("m_gate" if bank < 4 else "m_up"), 1)

            def down(e):
                pe.wait_ge(sem("m_h"), e + 1)
                for f in range(FT):
                    ins = pe.matmul(ps[:, DOWN_AT[e][0], DOWN_AT[e][1]:DOWN_AT[e][1] + D],
                                    hT[:, e % 2, f, :, :].rearrange("p a s -> p (a s)"), downT[:, e * FT + f, :],
                                    start=(f == 0), stop=(f == FT - 1))
                ins.then_inc(sem("m_down"), 1)

            gate_up(0)
            gate_up(1)
            pe.wait_ge(sem("m_chosen"), 1)
            pe.matmul(ps[:, 1, 0:2 * EXPERTS], C("ones", slice(0, S)), rt16[0:S, :], start=True,
                      stop=True).then_inc(sem("m_counts"), 1)
            for e in range(2, EXPERTS):
                down(e - 2)
                gate_up(e)
            down(EXPERTS - 2)
            down(EXPERTS - 1)

            norm_pe(pe, 3)
            pe.wait_ge(sem("ln_xnT"), 4)
            fold_q_pe(pe, 1, xnT)
            pe.wait_ge(sem("g_copied"), 3)
            flash_pe(pe, 1)
            turn_u_pe(pe, 1)
            loaded(pe, "out1")
            project_pe(pe, 1, 1)
            stay_warm(pe, 6, 3)
            pe.wait_ge(sem("o1_ready"), 1)
            pe.transpose(ps[:, 7, 0:P], o1, ident).then_inc(sem("o1_turned"), 1)
            stay_warm(pe, 6, 2)
            pe.wait_ge(sem("o1T_ready"), 1)
            fold_q_pe(pe, 2, o1T)
            stay_warm(pe, 6, 1)
            pe.wait_ge(sem("g_copied"), 5)
            for r in range(RT):
                if r == RT // 2:
                    pe.wait_ge(sem("g_upper"), 3)
                ins = pe.matmul(ps[:, 3, r * S:(r + 1) * S], GT[:, r, :], o1T[:, 0:S], start=True, stop=True)
            ins.then_inc(sem("b_scores"), 1)
            pe.wait_ge(sem("f_wq"), 2)
            for f in range(FT):
                ins = pe.transpose(ps[:, 5, f * P:(f + 1) * P], wqi[:, f, :], ident)
            ins.then_inc(sem("f_wturned"), 1)
            stay_warm(pe, 6, 14)
            pe.wait_ge(sem("b_probs"), 1)
            pe.wait_ge(sem("f_wcopied"), 1)
            for j in range(4):
                ins = pe.transpose(ps[:, 4, j * P:(j + 1) * P], sm[:, 2 * j:2 * j + 2, :].rearrange("p a t -> p (a t)"),
                                   ident)
            ins.then_inc(sem("b_pturned"), 1)
            stay_warm(pe, 6, 4)
            pe.wait_ge(sem("b_pcopied"), 1)
            for jj in range(2):
                rows = slice(jj * S, (jj + 1) * S)
                pe.matmul(ps[:, jj, :], xn[rows, :], PT[rows, :, :].rearrange("p j c -> p (j c)"), start=True,
                          stop=True).then_inc(sem("b_u"), 1)
            project_pe(pe, 1, 2)

            norm_pe(pe, 4)
            pe.wait_ge(sem("ln_xnT"), 5)
            loaded(pe, "delta")
            for i in range(3):
                ins = pe.matmul(ps[:, 0, i * S:(i + 1) * S], d_w[:, i * D:(i + 1) * D], xnT[:, 0:S],
                                start=True, stop=True)
            ins.then_inc(sem("d_qkv"), 1)
            pe.matmul(ps[:, 1, 0:S], W("wb"), xnT[:, 0:S], start=True, stop=True).then_inc(sem("d_beta"), 1)
            stay_warm(pe, 7, 15)
            pe.wait_ge(sem("d_sq"), 1)
            pe.matmul(ps[:, 2, 0:2 * S], C("block32"), sq, start=True, stop=True).then_inc(sem("d_norm"), 1)
            stay_warm(pe, 7, 10)
            for g in range(8):
                if g == 0:
                    pe.wait_ge(sem("d_khat"), 2)
                else:
                    pe.wait_ge(sem("d_z"), g)
                w = S - 8 * g
                pe.matmul(ps[:, g, 0:8 * w], C("block32"), Z[:, g, 0:8 * w], start=True,
                          stop=True).then_inc(sem("d_a"), 1)
            pe.wait_ge(sem("d_subst"), 38)
            pe.matmul(ps[0:S, 0, 0:DH * S], qkh[:, 1, :], qexp.rearrange("p h t -> p (h t)"), start=True,
                      stop=True).then_inc(sem("d_b"), 1)
            pe.transpose(ps[0:S, 2, 3 * D:4 * D], vpad[:, FIR_L - 1:], ident)
            stay_warm(pe, 3, 11)
            pe.wait_ge(sem("d_subst"), S - 1)
            pe.transpose(ps[0:S, 1, 0:D], R, ident).then_inc(sem("d_uturned"), 1)
            pe.transpose(ps[0:S, 2, 0:D], loc[:, 0, :], ident)
            pe.wait_ge(sem("d_bcopied"), 1)
            pe.wait_ge(sem("d_ucopied"), 1)
            for h in range(DH):
                pe.matmul(ps[0:S, 2, 2 * D + h * DD:2 * D + (h + 1) * DD], Bm[:, h, :],
                          u_s[:, h * DD:(h + 1) * DD], start=True, stop=True)
            pe.wait_ge(sem("d_fir"), 1)
            pe.transpose(ps[0:S, 2, D:2 * D], loc[:, 1, :], ident).then_inc(sem("d_branches"), 1)
            stay_warm(pe, 0, 18)
            pe.wait_ge(sem("d_stats"), 2)
            for h in range(DH):
                ins = pe.transpose(ps[0:16, 3, h * S:(h + 1) * S], st[:, h, :, :].rearrange("p a b -> p (a b)"),
                                   C("ident", slice(0, S))[:, 0:S])
            ins.then_inc(sem("d_sturned"), 1)
            pe.matmul(ps[:, 4, 0:DH * S], d_w[:, 4 * D:5 * D], xnT[:, 0:S].unsqueeze(1).broadcast_to([P, DH, S]),
                      start=True, stop=False)
            pe.wait_ge(sem("d_scopied"), 1)
            pe.matmul(ps[:, 4, 0:DH * S], w1s[:], statsT.rearrange("p h t -> p (h t)"), start=False,
                      stop=True).then_inc(sem("d_hidden"), 1)
            pe.wait_ge(sem("d_gelu"), 1)
            for h in range(DH):
                ins = pe.matmul(ps[0:S, 5, 4 * h:4 * h + 4], hg[:, h, :], W("w2"), start=True, stop=True)
            ins.then_inc(sem("d_gate"), 1)
            stay_warm(pe, 0, 14)
            pe.wait_ge(sem("d_mixed"), 1)
            pe.transpose(ps[:, 6, 0:S], om, C("ident", slice(0, S))[:, 0:S]).then_inc(sem("d_mturned"), 1)
            pe.wait_ge(sem("d_mcopied"), 1)
            pe.matmul(ps[:, 5, 128:256], oT[:].rearrange("p a s -> p (a s)"), d_w[:, 3 * D:4 * D],
                      start=True, stop=True).then_inc(sem("d_y"), 1)

            norm_pe(pe, 5)
            for i in range(2):
                pe.wait_ge(sem("f_amx"), i + 1)
                pe.transpose(ps[0:1, 1, 0:P], amx[:], ident).then_inc(sem("f_amxT"), 1)
                stay_warm(pe, 6, 2)
                pe.wait_ge(sem("f_amxr"), i + 1)
                pe.matmul(ps[:, 2, 0:1], C("ones", slice(0, 1)), amxr[:], start=True,
                          stop=True).then_inc(sem("f_amxb"), 1)
                stay_warm(pe, 6, 7)
                if i == 0:
                    pe.wait_ge(sem("f_xq"), 1)
                    for f in range(FT):
                        ins = pe.matmul(ps[:, 3, f * S:(f + 1) * S], winq[:, f, :], xq[:, 0:S], start=True, stop=True)
                    ins.then_inc(sem("f_hidden"), 1)
            pe.wait_ge(sem("f_hq"), 1)
            for f in range(FT):
                ins = pe.matmul(ps[0:S, 4, 0:D], hid[:, f, :], wqo[:, f, :], start=(f == 0), stop=(f == FT - 1))
            ins.then_inc(sem("f_y"), 1)

        @block.gpsimd
        def _(pool):
            steps = [0]

            def pseq(ins):
                steps[0] += 1
                ins.then_inc(sem("pool_step"), 1)
                pool.wait_ge(sem("pool_step"), steps[0])

            pool.memset(den[:], 0.0).then_inc(sem("cleared"), 1)
            pool.memset(U[:], 0.0).then_inc(sem("cleared"), 1)
            pool.memset(negmax[:, 0:RT], 3e38).then_inc(sem("cleared"), 1)
            for i in range(3):
                pool.memset(qkv_pad[i][:, 0:TAPS - 1], 0.0).then_inc(sem("pads"), 1)
            pool.memset(vpad[:, 0:FIR_L - 1], 0.0).then_inc(sem("pads"), 1)
            loaded(pool, "cst")
            norm_pool(pool, 0)
            for c in range(1, CH):
                keys, slot = slice(c * CK, (c + 1) * CK), c % MASK_SLOTS
                pool.wait_ge(sem(f"ld_chunk{c}"), 4 * 16)
                pool.wait_ge(sem("ctxT_ready"), c)
                pool.tensor_copy(ctxT_hi[:, keys], ctxT_raw[:, keys]).then_inc(sem("ctxT_upper"), 1)
                pool.wait_ge(sem("ctxT_upper"), c + 1)
                pool.tensor_tensor(ctxT_lo[:, keys], ctxT_raw[:, keys], ctxT_hi[:, keys].bitcast(F32),
                                   ALU.subtract).then_inc(sem("ctxT_ready"), 1)
                pool.wait_ge(sem("mask_ready"), c)
                pool.tensor_scalar(maskb[:, keys], mask_raw[:, slot * CK:(slot + 1) * CK], 0.0, MASKED,
                                   ALU.is_equal, ALU.mult).then_inc(sem("mask_ready"), 1)
            pool.wait_ge(sem("ch_scale"), 1)
            pool.wait_ge(sem("masked"), 3 * RT)
            pool.tensor_tensor(scale_diag, ident, ch_scale[:].broadcast_to([P, P]),
                               ALU.mult).then_inc(sem("scale_diag"), 1)

            def split_context(c):
                pool.wait_ge(sem("pv_done"), (c + 1) * RT)
                keys = slice(c * CK, (c + 1) * CK)
                pseq(pool.tensor_tensor(scaled.rearrange("p (k d) -> p k d", d=D),
                                        ctxN[:, keys].rearrange("p (k d) -> p k d", d=D),
                                        scale_rows.unsqueeze(1).broadcast_to([P, TC, D]), ALU.mult))
                upper, lower = (ctxN_parts[:, (2 * c + i) * CK:(2 * c + i + 1) * CK] for i in range(2))
                pseq(pool.tensor_copy(upper, scaled))
                pool.tensor_tensor(lower, scaled, upper, ALU.subtract).then_inc(sem("ctx_parts"), 1)
                pool.wait_ge(sem("ctx_parts"), c + 1)

            pool.wait_ge(sem("scale_rows"), 1)
            for c in range(2):
                split_context(c)
            for i in range(1, 5):
                if i == 2:
                    for c in range(2, 4):
                        split_context(c)
                if i == 3:
                    pool.wait_ge(sem("u_turned"), 2)
                    pool.memset(den[:], 0.0).then_inc(sem("cleared"), 1)
                    pool.memset(U[:], 0.0).then_inc(sem("cleared"), 1)
                norm_pool(pool, i)
                if i == 2:
                    for c in range(4, CH):
                        split_context(c)
                if i == 3:
                    pool.wait_ge(sem("f_scales"), 1)
                    pool.wait_ge(sem("m_down"), EXPERTS)
                    for k, (w, q) in enumerate(((win, wqi), (wout, wqo))):
                        up, back = (wsc[:, m, k * FT:(k + 1) * FT].unsqueeze(2).broadcast_to([P, FT, D])
                                    for m in range(2))
                        pseq(pool.tensor_tensor(q, w[:], up, ALU.mult))
                        pseq(pool.tensor_scalar(q, q, ROUND, ROUND, ALU.add, ALU.subtract))
                        pseq(pool.tensor_scalar(q, q, -128.0, 127.0, ALU.max, ALU.min))
                        pool.tensor_tensor(q, q, back, ALU.mult).then_inc(sem("f_wq"), 1)
            pool.wait_ge(sem("d_vcopied"), 1)
            taps = firp[:, :, 0:TAPS]
            pseq(pool.tensor_tensor(taps, windows(qkv_pad[2], TAPS),
                                    W("conv_v").unsqueeze(1).broadcast_to([P, S, TAPS]), ALU.mult))
            pseq(pool.tensor_tensor(taps[:, :, 0:2], taps[:, :, 0:2], taps[:, :, 2:4], ALU.add))
            pool.tensor_tensor(cv[:, 2, :], taps[:, :, 0], taps[:, :, 1], ALU.add).then_inc(sem("d_vconv"), 1)
            pool.wait_ge(sem("d_khat"), 1)
            for g in range(1, 8):
                key_products(pool, g).then_inc(sem("d_z"), 1)
            pool.wait_ge(sem("d_v"), 1)
            pseq(pool.tensor_tensor(firp, windows(vpad, FIR_L), W("fir_l").unsqueeze(1).broadcast_to([P, S, FIR_L]), ALU.mult))
            half = FIR_L // 2
            pseq(pool.tensor_tensor(firp[:, :, 0:half], firp[:, :, 0:half], firp[:, :, half:FIR_L], ALU.add))
            pool.tensor_tensor(firp[:, :, 0:half // 2], firp[:, :, 0:half // 2], firp[:, :, half // 2:half],
                               ALU.add).then_inc(sem("d_firp"), 1)
            pool.wait_ge(sem("d_msq"), 1)
            pool.tensor_tensor(orn[:], oms[:], pows[:], ALU.pow).then_inc(sem("d_mrn"), 1)
            norm_pool(pool, 5)

        @block.scalar
        def _(act):
            steps = [0]

            def seq(ins):
                steps[0] += 1
                ins.then_inc(sem("act_step"), 1)
                act.wait_ge(sem("act_step"), steps[0])

            act.dma_start(wq[:], dram["wq0"]).then_inc(sem("ld_in0"), 16)
            act.dma_start(wkT[:], dram["wkT0"]).then_inc(sem("ld_in0"), 16)
            fold_q_act(act, 0)
            act.wait_ge(sem("cleared"), 3)
            flash_act(act, 0)
            turn_u_act(act, 0)
            project_act(act, 0)

            act.wait_ge(sem("a_shifted"), 1)
            act.activation(sm, sm2, ACT.Exp, scale=float(1.0 / np.sqrt(AD))).then_inc(sem("a_exp"), 1)
            act.wait_ge(sem("a_pturned"), 1)
            act.copy(PT.rearrange("p j c -> p (j c)"), ps[:, 4, :]).then_inc(sem("a_pcopied"), 1)
            fold_weights_act(act)
            loaded(act, "par")
            seq(act.activation(tmpp[:, 0:1], W("temp"), ACT.Abs))
            seq(act.activation(tmpp[:, 1:2], tmpp[:, 0:1], ACT.Exp, scale=-1.0))
            act.activation(sres[:, 1, :], W("res"), ACT.Exp, scale=-1.0).then_inc(sem("d_eres"), 1)
            act.activation(tmpp[:, 2:3], tmpp[:, 1:2], ACT.Ln, bias=1.0).then_inc(sem("d_ln"), 1)

            act.wait_ge(sem("m_nlog"), 1)
            act.activation(eprob[:], ps[:, 0, 0:EXPERTS], ACT.Exp, bias=nlog[:]).then_inc(sem("m_exp"), 1)
            for e in range(EXPERTS):
                act.wait_ge(sem("m_gate"), e + 1)
                if e >= 2:
                    act.wait_ge(sem("m_h"), e - 1)
                act.activation(sg[:, e % 2, :], ps[:, 2 + e % 2, 0:FT * S], ACT.Silu).then_inc(sem("m_silu"), 1)

            fold_q_act(act, 1)
            flash_act(act, 1)
            turn_u_act(act, 1)
            project_act(act, 1)
            fold_q_act(act, 2)
            act.wait_ge(sem("b_shifted"), 1)
            act.activation(sm, sm2, ACT.Exp, scale=DK ** -0.5).then_inc(sem("b_exp"), 1)
            act.wait_ge(sem("b_pturned"), 1)
            act.copy(PT.rearrange("p j c -> p (j c)"), ps[:, 4, :]).then_inc(sem("b_pcopied"), 1)
            act.wait_ge(sem("b_u"), 2)
            act.copy(UT[:].rearrange("p (j a) c -> p j a c", a=2)[:, :, 1, :],
                     ps[:, 1, :].rearrange("p (j c) -> p j c", j=4)).then_inc(sem("ut_copied"), 1)
            project_act(act, 2)

            act.wait_ge(sem("d_beta"), 1)
            act.activation(eb, ps[:, 1, 0:S], ACT.Exp, scale=-1.0).then_inc(sem("d_eb"), 1)
            act.wait_ge(sem("d_conv"), 1)
            act.activation(qkc, cv[:, 0:2, :], ACT.Silu).then_inc(sem("d_qk"), 1)
            act.wait_ge(sem("d_vconv"), 1)
            act.activation(vpad[:, FIR_L - 1:], cv[:, 2, :], ACT.Silu).then_inc(sem("d_v"), 1)
            act.wait_ge(sem("d_nrm"), 1)
            act.activation(rn.rearrange("p a t -> p (a t)"), nrm, ACT.Sqrt).then_inc(sem("d_sqrt"), 1)
            act.wait_ge(sem("d_brcopied"), 1)
            act.activation(prod, br, ACT.Square).then_inc(sem("d_squares"), 1)
            act.wait_ge(sem("d_l2"), 1)
            act.activation(st[:, :, :, 3].rearrange("p h b -> p b h"),
                           mom[:, 2, :].rearrange("p (b h) -> p b h", b=4), ACT.Sqrt).then_inc(sem("d_stats"), 1)
            act.wait_ge(sem("d_hidden"), 1)
            act.activation(hg.rearrange("p h t -> p (h t)"), ps[:, 4, 0:DH * S], ACT.Gelu,
                           bias=W("b1")).then_inc(sem("d_gelu"), 1)
            act.wait_ge(sem("d_gshift"), 1)
            act.activation(gsm[:], gsm[:], ACT.Exp, scale=rtemp[0:S, :]).then_inc(sem("d_gexp"), 1)

            for f in range(FT):
                if f == 0:
                    act.wait_ge(sem("f_hidden"), 1)
                ins = act.activation(hid[:, f, :], ps[:, 3, f * S:(f + 1) * S], ACT.Gelu,
                                     bias=par[:, PARAM["b_in"][0] + f:PARAM["b_in"][0] + f + 1])
            ins.then_inc(sem("f_gelu"), 1)

        @block.vector
        def _(dve):
            steps = [0]

            def seq(ins):
                steps[0] += 1
                ins.then_inc(sem("dve_step"), 1)
                dve.wait_ge(sem("dve_step"), steps[0])

            loaded(dve, "x", "cst")
            norm_dve(dve, seq, 0)
            fold_q_dve(dve, seq, 0)
            dve.wait_ge(sem("cleared"), 3)
            flash_dve(dve, 0)
            turn_u_dve(dve, seq, 0)
            project_dve(dve, 0)
            seq(dve.tensor_tensor(x[:], x[:], ps[:, 3, 0:D], ALU.add))

            norm_dve(dve, seq, 1)
            dve.wait_ge(sem("a_qkv"), 1)
            heads = ps[:, 0, 0:2 * D].rearrange("p (h d) -> p h d", d=AD)
            r1, r2 = rot1.rearrange("p (h d) -> p h d", d=AD), rot2.rearrange("p (h d) -> p h d", d=AD)
            hd = AD // 2
            dve.tensor_tensor(r1, heads, C("cos").unsqueeze(1).broadcast_to([P, 2 * AH, AD]), ALU.mult)
            dve.tensor_tensor(r2[:, :, 0:hd], heads[:, :, hd:AD],
                              C("sin")[:, 0:hd].unsqueeze(1).broadcast_to([P, 2 * AH, hd]), ALU.mult)
            seq(dve.tensor_tensor(r2[:, :, hd:AD], heads[:, :, 0:hd],
                                  C("sin")[:, hd:AD].unsqueeze(1).broadcast_to([P, 2 * AH, hd]), ALU.mult))
            dve.tensor_tensor(qk, rot1, rot2, ALU.add).then_inc(sem("a_rotated"), 1)
            seq(dve.tensor_tensor(vblk[:], ps[:, 1, 0:D].rearrange("p (j a d) -> p j a d", j=PAIRS, a=2),
                                  C("half").unsqueeze(1).unsqueeze(3).broadcast_to([P, PAIRS, 2, AD]), ALU.mult))
            dve.wait_ge(sem("a_turned"), 1)
            dve.tensor_copy(aqT, ps[:, 2, 0:P])
            dve.tensor_tensor(kexp, ps[:, 2, P:P + S].unsqueeze(1).broadcast_to([P, AH, S]),
                              C("head8").unsqueeze(2).broadcast_to([P, AH, S]), ALU.mult).then_inc(sem("a_kexp"), 1)
            dve.wait_ge(sem("a_scores"), 1)
            sc = ps[:, 3, :].rearrange("p (h t) -> p h t", h=8)
            seq(dve.scalar_tensor_tensor(sm, sc, 0.0, C("later").unsqueeze(1).broadcast_to([P, 8, S]),
                                         ALU.is_equal, ALU.max))
            seq(dve.scalar_tensor_tensor(sm2, sm, NEVER, sc, ALU.mult, ALU.add))

            def shift(name):
                seq(dve.tensor_reduce(smx[:], sm2, AX, ALU.max))
                dve.tensor_tensor(sm2, sm2, smx[:].unsqueeze(2).broadcast_to([P, 8, S]),
                                  ALU.subtract).then_inc(sem(name), 1)

            def normalise(exp_name, name):
                dve.wait_ge(sem(exp_name), 1)
                seq(dve.tensor_reduce(ssum[:], sm, AX, ALU.add))
                seq(dve.reciprocal(smx[:], ssum[:]))
                dve.tensor_tensor(sm, sm, smx[:].unsqueeze(2).broadcast_to([P, 8, S]),
                                  ALU.mult).then_inc(sem(name), 1)

            shift("a_shifted")
            normalise("a_exp", "a_probs")
            dve.wait_ge(sem("a_out"), 1)
            dve.tensor_copy(o_s[:], ps[0:S, 5, 0:D]).then_inc(sem("a_ocopied"), 1)
            dve.wait_ge(sem("a_oturned"), 1)
            dve.tensor_copy(oT[:], ps[:, 6, 0:S].unsqueeze(1).broadcast_to([P, 2, S])).then_inc(sem("a_oT"), 1)
            dve.wait_ge(sem("a_y"), 1)
            seq(dve.tensor_tensor(x[:], x[:], ps[:, 5, 128:256], ALU.add))

            norm_dve(dve, seq, 2)
            dve.wait_ge(sem("m_logits"), 1)
            dve.tensor_reduce(nlog[:], ps[:, 0, 0:EXPERTS], AX, ALU.max, negate=True).then_inc(sem("m_nlog"), 1)
            dve.wait_ge(sem("m_exp"), 1)
            seq(dve.max(top8[:], eprob[:]))
            seq(dve.max_index(topi[:], top8[:], eprob[:]))
            seq(dve.tensor_copy(topf[:], topi[:]))
            for k in range(2):
                dve.tensor_scalar(chosen[:, k, :], C("iota8"), topf[:, k:k + 1], None, ALU.is_equal)
                seq(dve.tensor_scalar(share[:, k, :], C("iota8"), topf[:, k:k + 1], top8[:, k:k + 1],
                                      ALU.is_equal, ALU.mult))
            dve.tensor_tensor(rt16[:, 0:EXPERTS], chosen[:, 0, :], chosen[:, 1, :], ALU.add)
            seq(dve.tensor_tensor(pairsum[:, 0:1], top8[:, 0:1], top8[:, 1:2], ALU.add))
            dve.tensor_tensor(share[:, 2, :], share[:, 0, :], share[:, 1, :], ALU.add)
            seq(dve.reciprocal(pairsum[:, 1:2], pairsum[:, 0:1]))
            dve.tensor_scalar(rt16[:, EXPERTS:], share[:, 2, :], pairsum[:, 1:2], None,
                              ALU.mult).then_inc(sem("m_chosen"), 1)

            def hidden(e):
                dve.wait_ge(sem("m_up"), e + 1)
                dve.wait_ge(sem("m_silu"), e + 1)
                if e >= 2:
                    dve.wait_ge(sem("m_down"), e - 1)
                for a in range(2):
                    ins = dve.tensor_tensor(hT[:, e % 2, :, a, :], sg[:, e % 2, :].rearrange("p (f s) -> p f s", f=FT),
                                            ps[:, 4 + e % 2, 0:FT * S].rearrange("p (f s) -> p f s", f=FT), ALU.mult)
                ins.then_inc(sem("m_h"), 1)

            hidden(0)
            hidden(1)
            dve.wait_ge(sem("m_counts"), 1)
            seq(dve.tensor_scalar(meanw[:], ps[:, 1, 0:EXPERTS], 1.0, None, ALU.max))
            seq(dve.reciprocal(coef[:], meanw[:]))
            seq(dve.tensor_tensor(meanw[:], coef[:], ps[:, 1, EXPERTS:2 * EXPERTS], ALU.mult))
            seq(dve.tensor_tensor(coef[:], meanw[:], rt16[:, 0:EXPERTS], ALU.mult))

            def add_experts(es, done):
                dve.wait_ge(sem("m_down"), done)
                for e in es:
                    bank, col = DOWN_AT[e]
                    seq(dve.scalar_tensor_tensor(x[:], ps[:, bank, col:col + D], coef[:, e:e + 1], x[:], ALU.mult,
                                                 ALU.add))

            hidden(2)
            hidden(3)
            loaded(dve, "ffn")
            for i, w in enumerate((win, wout)):
                seq(dve.tensor_reduce(wamx[:, i * FT:(i + 1) * FT], w[:], AX, ALU.max, apply_absolute_value=True))
                hidden(4 + i)
            seq(dve.tensor_scalar(wamx[:], wamx[:], 1e-8, None, ALU.max))
            seq(dve.reciprocal(wsc[:, 0, :], wamx[:]))
            seq(dve.tensor_scalar(wsc[:, 0, :], wsc[:, 0, :], 127.0, None, ALU.mult))
            dve.reciprocal(wsc[:, 1, :], wsc[:, 0, :]).then_inc(sem("f_scales"), 1)
            hidden(6)
            dve.wait_ge(sem("d_eres"), 1)
            seq(dve.tensor_scalar(sres[:, 1, :], sres[:, 1, :], 1.0, None, ALU.add))
            seq(dve.reciprocal(sres[:, 2, :], sres[:, 1, :]))
            dve.wait_ge(sem("d_ln"), 1)
            seq(dve.scalar_tensor_tensor(tmpp[:, 3:4], W("temp"), 0.0, tmpp[:, 2:3], ALU.max, ALU.add))
            seq(dve.tensor_scalar(tmpp[:, 3:4], tmpp[:, 3:4], 1e-6, None, ALU.add))
            seq(dve.reciprocal(rtemp[:], tmpp[:, 3:4]))
            add_experts(range(0, 3), 4)
            hidden(7)
            add_experts(range(3, 4), 4)
            add_experts(range(4, 7), 7)
            add_experts(range(7, 8), 8)

            norm_dve(dve, seq, 3)
            fold_q_dve(dve, seq, 1)
            seq(dve.tensor_tensor(o1, xn[:], W("bo"), ALU.add))
            seq(dve.tensor_tensor(x[:], x[:], W("bo"), ALU.add))
            dve.wait_ge(sem("cleared"), 5)
            flash_dve(dve, 1)
            turn_u_dve(dve, seq, 1)
            project_dve(dve, 1)
            dve.tensor_tensor(o1, o1, ps[:, 3, 0:D], ALU.add).then_inc(sem("o1_ready"), 1)
            dve.wait_ge(sem("o1_turned"), 1)
            dve.tensor_copy(o1T, ps[:, 7, 0:P]).then_inc(sem("o1T_ready"), 1)
            fold_q_dve(dve, seq, 2)
            dve.wait_ge(sem("b_scores"), 1)
            sc = ps[:, 3, :].rearrange("p (h t) -> p h t", h=8)
            seq(dve.tensor_reduce(smx[:], sc, AX, ALU.max))
            dve.tensor_tensor(sm2, sc, smx[:].unsqueeze(2).broadcast_to([P, 8, S]),
                              ALU.subtract).then_inc(sem("b_shifted"), 1)
            dve.wait_ge(sem("f_wturned"), 1)
            dve.tensor_copy(winq.rearrange("p f c -> p (f c)"), ps[:, 5, :]).then_inc(sem("f_wcopied"), 1)
            normalise("b_exp", "b_probs")
            dve.wait_ge(sem("b_u"), 1)
            dve.tensor_copy(UT[:].rearrange("p (j a) c -> p j a c", a=2)[:, :, 0, :],
                            ps[:, 0, :].rearrange("p (j c) -> p j c", j=4)).then_inc(sem("ut_copied"), 1)
            project_dve(dve, 2)
            seq(dve.tensor_tensor(x[:], x[:], ps[:, 3, 0:D], ALU.add))

            norm_dve(dve, seq, 4)
            dve.wait_ge(sem("pads"), 4)
            dve.wait_ge(sem("d_qkv"), 1)
            dve.tensor_copy(qkv_pad[2][:, TAPS - 1:], ps[:, 0, 2 * S:3 * S]).then_inc(sem("d_vcopied"), 1)
            for i in range(2):
                ins = dve.tensor_copy(qkv_pad[i][:, TAPS - 1:], ps[:, 0, i * S:(i + 1) * S])
            seq(ins)
            for k in range(TAPS):
                for i, name in enumerate(("conv_q", "conv_k")):
                    a = PARAM[name][0] + k
                    if k == 0:
                        ins = dve.tensor_scalar(cv[:, i, :], qkv_pad[i][:, k:k + S], par[:, a:a + 1], None, ALU.mult)
                    else:
                        ins = dve.scalar_tensor_tensor(cv[:, i, :], qkv_pad[i][:, k:k + S], par[:, a:a + 1],
                                                       cv[:, i, :], ALU.mult, ALU.add)
                if k < TAPS - 1:
                    seq(ins)
            ins.then_inc(sem("d_conv"), 1)
            dve.wait_ge(sem("d_eb"), 1)
            seq(dve.tensor_scalar(eb, eb, 1.0, None, ALU.add))
            seq(dve.reciprocal(beta, eb))
            dve.wait_ge(sem("d_qk"), 1)
            dve.tensor_tensor(sq, qkc.rearrange("p a t -> p (a t)"), qkc.rearrange("p a t -> p (a t)"),
                              ALU.mult).then_inc(sem("d_sq"), 1)
            dve.wait_ge(sem("d_norm"), 1)
            dve.tensor_scalar(nrm, ps[:, 2, 0:2 * S], 1e-12, None, ALU.add).then_inc(sem("d_nrm"), 1)
            dve.wait_ge(sem("d_v"), 1)
            seq(dve.tensor_tensor(R, vpad[:, FIR_L - 1:], beta, ALU.mult))
            dve.wait_ge(sem("d_sqrt"), 1)
            seq(dve.reciprocal(rn[:, 1, :], rn[:, 1, :]))
            seq(dve.tensor_tensor(qkh[:, 1, :], qkc[:, 1, :], rn[:, 1, :], ALU.mult))
            dve.scalar_tensor_tensor(kbneg, qkh[:, 1, :], -1.0, beta, ALU.mult,
                                     ALU.mult).then_inc(sem("d_khat"), 1)
            dve.wait_ge(sem("d_khat"), 1)
            key_products(dve, 0).then_inc(sem("d_khat"), 1)
            seq(dve.reciprocal(rn[:, 0, :], rn[:, 0, :]))
            seq(dve.tensor_tensor(qkh[:, 0, :], qkc[:, 0, :], rn[:, 0, :], ALU.mult))
            seq(dve.tensor_tensor(qexp, qkh[:, 0, :].unsqueeze(1).broadcast_to([P, DH, S]),
                                  C("head32").unsqueeze(2).broadcast_to([P, DH, S]), ALU.mult))
            beside = steps[0]
            for t in range(S - 1):
                if t % 8 == 0:
                    dve.wait_ge(sem("d_a"), t // 8 + 1)
                w = S - 8 * (t // 8)
                a = (t % 8) * w + t % 8 + 1
                dve.scalar_tensor_tensor(R[:, t + 1:], ps[:, t // 8, a:a + S - 1 - t], R[:, t:t + 1], R[:, t + 1:],
                                         ALU.mult, ALU.add).then_inc(sem("d_subst"), 1)
                if t < FIR_S:
                    a = PARAM["fir_s"][0] + t
                    seen = vpad[:, FIR_L - FIR_S + t:FIR_L - FIR_S + t + S]
                    dve.wait_ge(sem("dve_step"), beside + t)
                    if t == 0:
                        ins = dve.tensor_scalar(loc[:, 0, :], seen, par[:, a:a + 1], None, ALU.mult)
                    else:
                        ins = dve.scalar_tensor_tensor(loc[:, 0, :], seen, par[:, a:a + 1], loc[:, 0, :], ALU.mult,
                                                       ALU.add)
                    ins.then_inc(sem("dve_step"), 1)
                dve.wait_ge(sem("d_subst"), t + 1)
            steps[0] = beside + FIR_S
            dve.wait_ge(sem("d_b"), 1)
            dve.tensor_tensor(Bm, ps[0:S, 0, 0:DH * S].rearrange("p (h t) -> p h t", h=DH),
                              C("upto", slice(0, S)).unsqueeze(1).broadcast_to([S, DH, S]),
                              ALU.mult).then_inc(sem("d_bcopied"), 1)
            dve.wait_ge(sem("d_uturned"), 1)
            dve.tensor_copy(u_s, ps[0:S, 1, 0:D]).then_inc(sem("d_ucopied"), 1)
            dve.wait_ge(sem("d_firp"), 1)
            dve.tensor_reduce(loc[:, 1, :], firp[:, :, 0:FIR_L // 4], AX, ALU.add).then_inc(sem("d_fir"), 1)
            dve.wait_ge(sem("d_branches"), 1)
            dve.tensor_copy(br.rearrange("p b c -> p (b c)"), ps[0:S, 2, :]).then_inc(sem("d_brcopied"), 1)
            dve.wait_ge(sem("d_brcopied"), 1)
            g16 = br.rearrange("p b (h d) -> p (b h) d", h=DH)
            c16 = cen.rearrange("p b (h d) -> p (b h) d", h=DH)

            def stat(k):
                return st[:, :, :, k].rearrange("p h b -> p b h")

            def m16(k):
                return mom[:, k, :].rearrange("p (b h) -> p b h", b=4)

            dve.tensor_reduce(mom[:, 0, :], g16, AX, ALU.add).then_inc(sem("d_brcopied"), 1)
            seq(dve.tensor_reduce(mom[:, 1, :], g16, AX, ALU.add, apply_absolute_value=True))
            dve.wait_ge(sem("d_brcopied"), 2)
            seq(dve.scalar_tensor_tensor(c16, mom[:, 0, :].unsqueeze(2).broadcast_to([S, 16, DD]), -1.0 / DD, g16,
                                         ALU.mult, ALU.add))
            dve.tensor_scalar(stat(0), m16(0), 1.0 / DD, None, ALU.mult)
            dve.tensor_scalar(stat(2), m16(1), 1.0 / DD, None, ALU.mult)
            seq(dve.tensor_tensor(cen, cen, cen, ALU.mult))
            dve.wait_ge(sem("d_squares"), 1)
            dve.tensor_reduce(mom[:, 2, :], prod.rearrange("p b (h d) -> p (b h) d", h=DH), AX,
                              ALU.add).then_inc(sem("d_l2"), 1)
            seq(dve.tensor_reduce(mom[:, 1, :], c16, AX, ALU.add))
            dve.tensor_scalar(stat(1), m16(1), 1.0 / DD, None, ALU.mult).then_inc(sem("d_stats"), 1)
            dve.memset(gadd[:, :, 2:4], 0.0)
            dve.memset(pows[:], -0.5)
            seq(dve.memset(gadd[:, :, 0:2], FLOOR))
            seq(dve.tensor_tensor(gadd[:, :, 0], gadd[:, :, 0], sres[0:S, 2, :], ALU.add))
            dve.wait_ge(sem("d_sturned"), 1)
            dve.tensor_copy(statsT.rearrange("p h t -> p (h t)"), ps[0:16, 3, 0:DH * S]).then_inc(
                sem("d_scopied"), 1)
            dve.wait_ge(sem("d_gate"), 1)
            seq(dve.tensor_tensor(gsm[:], ps[0:S, 5, 0:16].rearrange("p (h b) -> p h b", h=DH),
                                  W("b2", slice(0, S)).unsqueeze(1).broadcast_to([S, DH, 4]), ALU.add))
            seq(dve.tensor_reduce(gmx[:, 0, :], gsm[:], AX, ALU.max))
            dve.tensor_tensor(gsm[:], gsm[:], gmx[:, 0, :].unsqueeze(2).broadcast_to([S, DH, 4]),
                              ALU.subtract).then_inc(sem("d_gshift"), 1)
            dve.wait_ge(sem("d_gexp"), 1)
            seq(dve.tensor_reduce(gmx[:, 0, :], gsm[:], AX, ALU.add))
            seq(dve.reciprocal(gmx[:, 1, :], gmx[:, 0, :]))
            seq(dve.scalar_tensor_tensor(gsm[:], gsm[:], 1.0 - 2.0 * FLOOR,
                                         gmx[:, 1, :].unsqueeze(2).broadcast_to([S, DH, 4]), ALU.mult, ALU.mult))
            seq(dve.tensor_tensor(gsm[:], gsm[:], gadd[:], ALU.add))
            seq(dve.tensor_tensor(prod.rearrange("p b (h d) -> p b h d", h=DH),
                                  br.rearrange("p b (h d) -> p b h d", h=DH),
                                  gsm[:].rearrange("p h b -> p b h").unsqueeze(3).broadcast_to([S, 4, DH, DD]),
                                  ALU.mult))
            seq(dve.tensor_tensor(prod[:, 0:2, :], prod[:, 0:2, :], prod[:, 2:4, :], ALU.add))
            seq(dve.tensor_tensor(om, prod[:, 0, :], prod[:, 1, :], ALU.add))
            seq(dve.tensor_tensor(osq, om, om, ALU.mult))
            seq(dve.tensor_reduce(oms[:], osq.rearrange("p (h d) -> p h d", h=DH), AX, ALU.add))
            dve.tensor_scalar(oms[:], oms[:], 1.0 / DD, 1e-5, ALU.mult, ALU.add).then_inc(sem("d_msq"), 1)
            seq(dve.tensor_tensor(om, om, W("rms_w", slice(0, S)), ALU.mult))
            dve.wait_ge(sem("d_mrn"), 1)
            dve.tensor_tensor(om.rearrange("p (h d) -> p h d", h=DH), om.rearrange("p (h d) -> p h d", h=DH),
                              orn[:].unsqueeze(2).broadcast_to([S, DH, DD]), ALU.mult).then_inc(sem("d_mixed"), 1)
            dve.wait_ge(sem("d_mturned"), 1)
            dve.tensor_copy(oT[:], ps[:, 6, 0:S].unsqueeze(1).broadcast_to([P, 2, S])).then_inc(sem("d_mcopied"), 1)
            dve.wait_ge(sem("d_y"), 1)
            seq(dve.tensor_tensor(x[:], x[:], ps[:, 5, 128:256], ALU.add))

            norm_dve(dve, seq, 5)

            def quantise(i, src, dst, name):
                dve.tensor_reduce(amx[:], src, mybir.AxisListType.XY if i else AX, ALU.max,
                                  apply_absolute_value=True).then_inc(sem("f_amx"), 1)
                dve.wait_ge(sem("f_amxT"), i + 1)
                dve.tensor_reduce(amxr[:], ps[0:1, 1, 0:P], AX, ALU.max).then_inc(sem("f_amxr"), 1)
                dve.wait_ge(sem("f_amxb"), i + 1)
                seq(dve.tensor_scalar(qs[:, 0:1], ps[:, 2, 0:1], 1e-8, None, ALU.max))
                seq(dve.reciprocal(qs[:, 1:2], qs[:, 0:1]))
                seq(dve.tensor_scalar(qs[:, 1:2], qs[:, 1:2], 32767.0, None, ALU.mult))
                seq(dve.tensor_scalar(dst, src, qs[:, 1:2], ROUND, ALU.mult, ALU.add))
                dve.reciprocal(qs[:, 2:3], qs[:, 1:2])
                seq(dve.tensor_scalar(dst, dst, ROUND, 32767.0, ALU.subtract, ALU.min))
                dve.tensor_scalar(dst, dst, -32768.0, qs[:, 2:3], ALU.max, ALU.mult).then_inc(sem(name), 1)

            quantise(0, xnT[:], xq, "f_xq")
            seq(dve.tensor_tensor(out_s, x[0:S, :], W("b_out", slice(0, S)), ALU.add))
            dve.wait_ge(sem("f_gelu"), 1)
            quantise(1, hid, hid, "f_hq")
            dve.wait_ge(sem("f_y"), 1)
            dve.tensor_tensor(out_s, out_s, ps[0:S, 4, 0:D], ALU.add).then_inc(sem("result"), 1)


def kernel(**inputs):
    import concourse.bacc as bacc
    from concourse.bass_utils import run_bass_kernel_spmd

    a = {k: np.asarray(v) for k, v in inputs.items()}

    def rows(name, width):
        return np.broadcast_to(a[name].reshape(1, width), (P, width))

    par = {
        "conv_q": a["L1_attn_conv_w_q"], "conv_k": a["L1_attn_conv_w_k"], "conv_v": a["L1_attn_conv_w_v"],
        "fir_s": a["L1_attn_fir_short_w"].reshape(D, FIR_S), "fir_l": a["L1_attn_fir_long_w"].reshape(D, FIR_L),
        "b1": a["L1_attn_mlp_b1"].reshape(D, 1), "b_in": a["L1_ffn_b_in"].reshape(FT, P).T,
        "rms_w": np.tile(rows("L1_attn_rms_w", DD), (1, DH)), "bo": rows("L1_xattn_bo", D),
        "b_out": rows("L1_ffn_b_out", D), "b2": rows("L1_attn_mlp_b2", 4), "temp": rows("L1_attn_logit_temp", 1),
        "res": rows("L1_attn_conv_res_logit", DH), "wb": np.repeat(a["L1_attn_Wb"], DD, axis=1),
        "w2": a["L1_attn_mlp_w2"], "router": a["L0_ffn_router_w"].T,
    }

    def tiles(w):
        return w.reshape(-1, P, w.shape[1]).transpose(1, 0, 2)

    ctx = a["ctx_1024"][0]
    arrays = {
        "x": np.concatenate([a["x"][0], a["x"][0]], 0),
        "cst": constants(),
        "par": np.concatenate([par[k] for k in PARAM], 1),
        "ctxT": ctx.T, "ctxN": tiles(ctx).reshape(P, KT * D), "mask": a["mask_SxS2_ik0"],
        "a_w": np.concatenate([a["L0_attn_qkv"].T, a["L0_attn_wo"].T], 1),
        "gateT": a["L0_ffn_gate_w"].reshape(EXPERTS * FF, D).T, "upT": a["L0_ffn_up_w"].reshape(EXPERTS * FF, D).T,
        "downT": tiles(a["L0_ffn_down_w"].transpose(0, 2, 1).reshape(EXPERTS * FF, D)),
        "d_w": np.concatenate([a["L1_attn_Wq"], a["L1_attn_Wk"], a["L1_attn_Wv"], a["L1_attn_Wo"],
                               a["L1_attn_mlp_w1"][0:D]], 1),
        "w1s": a["L1_attn_mlp_w1"][D:],
        "win": tiles(a["L1_ffn_W_in"].T), "wout": tiles(a["L1_ffn_W_out"]),
    }
    for i, names in enumerate((("L0_xattn_W_q", "L0_xattn_W_k", "L0_xattn_W_v", "L0_xattn_W_o"),
                               ("L1_xattn_Wq", "L1_xattn_Wk", "L1_xattn_Wv", "L1_xattn_Wo"))):
        if i == 0:
            arrays["wq0"] = a[names[0]]
        else:
            arrays["wqT1"] = tiles(a[names[0]].T)
        arrays[f"wkT{i}"] = tiles(a[names[1]].T)
        arrays[f"wv{i}"] = a[names[2]]
        arrays[f"wo{i}"] = tiles(a[names[3]])

    nc = bacc.Bacc("TRN2", target_bir_lowering=False, num_devices=1)
    dram, feed = {}, {}
    for name, v in arrays.items():
        v = np.ascontiguousarray(v)
        feed[f"in_{name}"] = v
        dram[name] = nc.dram_tensor(f"in_{name}", v.shape, mybir.dt.from_np(v.dtype), kind="ExternalInput").ap()
    dram["out"] = nc.dram_tensor("out", (S, D), F32, kind="ExternalOutput").ap()
    build(nc, dram)
    r = run_bass_kernel_spmd(nc, [feed], core_ids=[0])
    return r.results[0]["out"].reshape(1, S, D)
```
